# Optimizing a Trainium2 kernel written in Bass

```python
import numpy as np
import jax
import jax.numpy as jnp

def _softmax(x, axis=-1):
    return jax.nn.softmax(x, axis=axis)

def _gelu(x):
    return jax.nn.gelu(x, approximate=True)

def _silu(x):
    return jax.nn.silu(x)

def _sigmoid(x):
    return jax.nn.sigmoid(x)

def _layernorm(x, axis=-1, eps=1e-05):
    m = jnp.mean(x, axis=axis, keepdims=True)
    v = jnp.var(x, axis=axis, keepdims=True)
    return (x - m) / jnp.sqrt(v + eps)

def _scatter_add(tgt, idx, src, axis=0):
    return tgt.at[idx].add(src)

def _segment_sum(src, seg, n):
    return jax.ops.segment_sum(src, seg, n)
kernel_name = 'mk_gnn_preln_d2_gnn_r8_ce20ba'

def setup_inputs(seed: int=0):
    np.random.seed(seed)
    _w = jnp.asarray

    def _rec_inputs():
        import jax
        import jax.numpy as jnp
        _gk = jax.random.key(seed)
        x = -0.0003713 + 1 * jax.random.normal(jax.random.fold_in(_gk, 1), (6250, 128), jnp.float32)
        src = jax.random.randint(jax.random.fold_in(_gk, 2), (100000,), 0, 6250, jnp.int32)
        dst = jnp.minimum((6250 * jax.random.uniform(jax.random.fold_in(_gk, 3), (100000,)) ** 2.0).astype(jnp.int32), 49999)
        _o = jnp.argsort(dst, stable=True)
        src = src[_o]
        dst = dst[_o]
        edge_attr_128 = 5.93493e-05 + 1.00006 * jax.random.normal(jax.random.fold_in(_gk, 11), (100000, 128), jnp.float32)
        return (x, src, dst, edge_attr_128)
    x, src, dst, edge_attr_128 = _rec_inputs()

    def _L0_gnn_setup():
        import jax, jax.numpy as jnp
        import numpy as np
        N_NODES = 12500
        N_EDGES = 75000
        D_NODE = 128
        D_EDGE = 128
        HIDDEN = 128
        LN_EPS = 1e-05
        key = jax.random.key(seed)
        ks = jax.random.split(key, 12)
        x = jax.random.normal(ks[0], (N_NODES, D_NODE), dtype=jnp.float32)
        edge_index = jax.random.randint(ks[1], (2, N_EDGES), 0, N_NODES, dtype=jnp.int64)
        edge_attr = jax.random.normal(ks[2], (N_EDGES, D_EDGE), dtype=jnp.float32)
        in_dim = D_NODE + D_EDGE
        s1 = 1.0 / np.sqrt(in_dim)
        s2 = 1.0 / np.sqrt(HIDDEN)
        W1 = jax.random.uniform(ks[3], (in_dim, HIDDEN), minval=-s1, maxval=s1, dtype=jnp.float32)
        b1 = jax.random.uniform(ks[4], (HIDDEN,), minval=-s1, maxval=s1, dtype=jnp.float32)
        W2 = jax.random.uniform(ks[5], (HIDDEN, HIDDEN), minval=-s2, maxval=s2, dtype=jnp.float32)
        b2 = jax.random.uniform(ks[6], (HIDDEN,), minval=-s2, maxval=s2, dtype=jnp.float32)
        W3 = jax.random.uniform(ks[7], (HIDDEN, D_NODE), minval=-s2, maxval=s2, dtype=jnp.float32)
        b3 = jax.random.uniform(ks[8], (D_NODE,), minval=-s2, maxval=s2, dtype=jnp.float32)
        ln_w = jnp.ones((D_NODE,), dtype=jnp.float32)
        ln_b = jnp.zeros((D_NODE,), dtype=jnp.float32)
        return {'x': x, 'edge_index': edge_index, 'edge_attr': edge_attr, 'W1': W1, 'b1': b1, 'W2': W2, 'b2': b2, 'W3': W3, 'b3': b3, 'ln_w': ln_w, 'ln_b': ln_b}
    _L0_gnn_all = _L0_gnn_setup()
    _L0_gnn_in = {k: v for k, v in _L0_gnn_all.items() if k in ('W1', 'b1', 'W2', 'b2', 'W3', 'b3', 'ln_w', 'ln_b')}
    del _L0_gnn_all

    def _L1_gnn_setup():
        import jax, jax.numpy as jnp
        import numpy as np
        N, E, D, H, L, FF = (6250, 62500, 128, 8, 2, 512)
        HD = D // H

        def _layernorm(x, g, b):
            mu = jnp.mean(x, axis=-1, keepdims=True)
            var = jnp.mean(jnp.square(x - mu), axis=-1, keepdims=True)
            return (x - mu) * jax.lax.rsqrt(var + 1e-05) * g + b

        def _forward(edge_index, x, Wq, bq, Wk, bk, Wv, bv, Wo, bo, Wpos, bpos, Wdeg, bdeg, ln1_g, ln1_b, ln2_g, ln2_b, W1, b1, W2, b2):
            n = x.shape[0]
            loops = jnp.arange(n, dtype=edge_index.dtype)
            src = jnp.concatenate([edge_index[0], loops])
            dst = jnp.concatenate([edge_index[1], loops])
            scale = np.float32(np.sqrt(HD))
            for l in range(L):
                xn = _layernorm(x, ln1_g[l], ln1_b[l])
                deg = jax.ops.segment_sum(jnp.ones_like(src, dtype=x.dtype), src, num_segments=n)
                deg = (deg - deg.mean()) / (jnp.std(deg, ddof=1) + 1e-06)
                pos = xn @ Wpos[l] + bpos[l] + deg[:, None] * Wdeg[l][0] + bdeg[l]
                xp = xn + pos
                q = (xp @ Wq[l] + bq[l]).reshape(n, H, HD)
                k = (xp @ Wk[l] + bk[l]).reshape(n, H, HD)
                v = (xp @ Wv[l] + bv[l]).reshape(n, H, HD)
                att = jnp.einsum('ehd,ehd->eh', q[dst], k[src]) / scale
                att = jnp.nan_to_num(jnp.clip(att, -50.0, 50.0), nan=0.0, posinf=50.0, neginf=-50.0)
                m = jax.ops.segment_max(att, dst, num_segments=n)
                ex = jnp.exp(att - m[dst])
                s = jax.ops.segment_sum(ex, dst, num_segments=n)
                alpha = ex / (s[dst] + 1e-16)
                msg = (v[src] * alpha[:, :, None]).reshape(-1, D)
                aggr = jax.ops.segment_sum(msg, dst, num_segments=n)
                x = x + (aggr @ Wo[l] + bo[l])
                h = jax.nn.gelu(_layernorm(x, ln2_g[l], ln2_b[l]) @ W1[l] + b1[l], approximate=False)
                x = x + (h @ W2[l] + b2[l])
            return x
        key = jax.random.key(seed)
        ks = jax.random.split(key, 16)
        inp = {'x': jax.random.normal(ks[0], (N, D), jnp.float32), 'edge_index': jax.random.randint(ks[1], (2, E), 0, N, jnp.int32)}

        def w(k, shape, fan_in):
            return jax.random.normal(k, shape, jnp.float32) / np.float32(np.sqrt(fan_in))
        inp['Wq'] = w(ks[2], (L, D, D), D)
        inp['Wk'] = w(ks[3], (L, D, D), D)
        inp['Wv'] = w(ks[4], (L, D, D), D)
        inp['Wo'] = w(ks[5], (L, D, D), D)
        inp['Wpos'] = w(ks[6], (L, D, D), D)
        inp['Wdeg'] = w(ks[7], (L, 1, D), 1)
        inp['W1'] = w(ks[8], (L, D, FF), D)
        inp['W2'] = w(ks[9], (L, FF, D), FF)
        for name, shape in [('bq', (L, D)), ('bk', (L, D)), ('bv', (L, D)), ('bo', (L, D)), ('bpos', (L, D)), ('bdeg', (L, D)), ('ln1_b', (L, D)), ('ln2_b', (L, D)), ('b1', (L, FF)), ('b2', (L, D))]:
            inp[name] = jnp.zeros(shape, jnp.float32)
        inp['ln1_g'] = jnp.ones((L, D), jnp.float32)
        inp['ln2_g'] = jnp.ones((L, D), jnp.float32)
        return inp
    _L1_gnn_all = _L1_gnn_setup()
    _L1_gnn_in = {k: v for k, v in _L1_gnn_all.items() if k in ('Wq', 'bq', 'Wk', 'bk', 'Wv', 'bv', 'Wo', 'bo', 'Wpos', 'bpos', 'Wdeg', 'bdeg', 'ln1_g', 'ln1_b', 'ln2_g', 'ln2_b', 'W1', 'b1', 'W2', 'b2')}
    del _L1_gnn_all
    return {'x': x, 'src': src, 'dst': dst, 'edge_attr_128': edge_attr_128, 'L0_gnn_W1': _L0_gnn_in['W1'], 'L0_gnn_b1': _L0_gnn_in['b1'], 'L0_gnn_W2': _L0_gnn_in['W2'], 'L0_gnn_b2': _L0_gnn_in['b2'], 'L0_gnn_W3': _L0_gnn_in['W3'], 'L0_gnn_b3': _L0_gnn_in['b3'], 'L0_gnn_ln_w': _L0_gnn_in['ln_w'], 'L0_gnn_ln_b': _L0_gnn_in['ln_b'], 'L1_gnn_Wq': _L1_gnn_in['Wq'], 'L1_gnn_bq': _L1_gnn_in['bq'], 'L1_gnn_Wk': _L1_gnn_in['Wk'], 'L1_gnn_bk': _L1_gnn_in['bk'], 'L1_gnn_Wv': _L1_gnn_in['Wv'], 'L1_gnn_bv': _L1_gnn_in['bv'], 'L1_gnn_Wo': _L1_gnn_in['Wo'], 'L1_gnn_bo': _L1_gnn_in['bo'], 'L1_gnn_Wpos': _L1_gnn_in['Wpos'], 'L1_gnn_bpos': _L1_gnn_in['bpos'], 'L1_gnn_Wdeg': _L1_gnn_in['Wdeg'], 'L1_gnn_bdeg': _L1_gnn_in['bdeg'], 'L1_gnn_ln1_g': _L1_gnn_in['ln1_g'], 'L1_gnn_ln1_b': _L1_gnn_in['ln1_b'], 'L1_gnn_ln2_g': _L1_gnn_in['ln2_g'], 'L1_gnn_ln2_b': _L1_gnn_in['ln2_b'], 'L1_gnn_W1': _L1_gnn_in['W1'], 'L1_gnn_b1': _L1_gnn_in['b1'], 'L1_gnn_W2': _L1_gnn_in['W2'], 'L1_gnn_b2': _L1_gnn_in['b2']}

def reference(x, src, dst, edge_attr_128, L0_gnn_W1, L0_gnn_b1, L0_gnn_W2, L0_gnn_b2, L0_gnn_W3, L0_gnn_b3, L0_gnn_ln_w, L0_gnn_ln_b, L1_gnn_Wq, L1_gnn_bq, L1_gnn_Wk, L1_gnn_bk, L1_gnn_Wv, L1_gnn_bv, L1_gnn_Wo, L1_gnn_bo, L1_gnn_Wpos, L1_gnn_bpos, L1_gnn_Wdeg, L1_gnn_bdeg, L1_gnn_ln1_g, L1_gnn_ln1_b, L1_gnn_ln2_g, L1_gnn_ln2_b, L1_gnn_W1, L1_gnn_b1, L1_gnn_W2, L1_gnn_b2):
    import jax
    import jax.numpy as jnp

    def _L0_gnn_ref(x, edge_index, edge_attr, W1, b1, W2, b2, W3, b3, ln_w, ln_b):
        import jax, jax.numpy as jnp
        import numpy as np
        N_NODES = 12500
        N_EDGES = 75000
        D_NODE = 128
        D_EDGE = 128
        HIDDEN = 128
        LN_EPS = 1e-05
        col = edge_index[1]
        agg = jax.ops.segment_sum(edge_attr, col, num_segments=x.shape[0])
        h = jnp.concatenate([x, agg], axis=-1)
        h = jax.nn.relu(h @ W1 + b1)
        h = jax.nn.relu(h @ W2 + b2)
        h = h @ W3 + b3
        mu = jnp.mean(h, axis=-1, keepdims=True)
        var = jnp.mean(jnp.square(h - mu), axis=-1, keepdims=True)
        h = (h - mu) * jax.lax.rsqrt(var + LN_EPS) * ln_w + ln_b
        return h

    def _L1_gnn_ref(x, edge_index, Wq, bq, Wk, bk, Wv, bv, Wo, bo, Wpos, bpos, Wdeg, bdeg, ln1_g, ln1_b, ln2_g, ln2_b, W1, b1, W2, b2):
        import jax, jax.numpy as jnp
        import numpy as np
        N, E, D, H, L, FF = (6250, 62500, 128, 8, 2, 512)
        HD = D // H

        def _layernorm(x, g, b):
            mu = jnp.mean(x, axis=-1, keepdims=True)
            var = jnp.mean(jnp.square(x - mu), axis=-1, keepdims=True)
            return (x - mu) * jax.lax.rsqrt(var + 1e-05) * g + b

        def _forward(edge_index, x, Wq, bq, Wk, bk, Wv, bv, Wo, bo, Wpos, bpos, Wdeg, bdeg, ln1_g, ln1_b, ln2_g, ln2_b, W1, b1, W2, b2):
            n = x.shape[0]
            loops = jnp.arange(n, dtype=edge_index.dtype)
            src = jnp.concatenate([edge_index[0], loops])
            dst = jnp.concatenate([edge_index[1], loops])
            scale = np.float32(np.sqrt(HD))
            for l in range(L):
                xn = _layernorm(x, ln1_g[l], ln1_b[l])
                deg = jax.ops.segment_sum(jnp.ones_like(src, dtype=x.dtype), src, num_segments=n)
                deg = (deg - deg.mean()) / (jnp.std(deg, ddof=1) + 1e-06)
                pos = xn @ Wpos[l] + bpos[l] + deg[:, None] * Wdeg[l][0] + bdeg[l]
                xp = xn + pos
                q = (xp @ Wq[l] + bq[l]).reshape(n, H, HD)
                k = (xp @ Wk[l] + bk[l]).reshape(n, H, HD)
                v = (xp @ Wv[l] + bv[l]).reshape(n, H, HD)
                att = jnp.einsum('ehd,ehd->eh', q[dst], k[src]) / scale
                att = jnp.nan_to_num(jnp.clip(att, -50.0, 50.0), nan=0.0, posinf=50.0, neginf=-50.0)
                m = jax.ops.segment_max(att, dst, num_segments=n)
                ex = jnp.exp(att - m[dst])
                s = jax.ops.segment_sum(ex, dst, num_segments=n)
                alpha = ex / (s[dst] + 1e-16)
                msg = (v[src] * alpha[:, :, None]).reshape(-1, D)
                aggr = jax.ops.segment_sum(msg, dst, num_segments=n)
                x = x + (aggr @ Wo[l] + bo[l])
                h = jax.nn.gelu(_layernorm(x, ln2_g[l], ln2_b[l]) @ W1[l] + b1[l], approximate=False)
                x = x + (h @ W2[l] + b2[l])
            return x
        return _forward(edge_index, x, Wq, bq, Wk, bk, Wv, bv, Wo, bo, Wpos, bpos, Wdeg, bdeg, ln1_g, ln1_b, ln2_g, ln2_b, W1, b1, W2, b2)
    edge_index = jnp.stack([src, dst])
    h = jnp.maximum(_layernorm(x, axis=-1), 0.0)
    x = x + _L0_gnn_ref(h, edge_index, edge_attr_128, L0_gnn_W1, L0_gnn_b1, L0_gnn_W2, L0_gnn_b2, L0_gnn_W3, L0_gnn_b3, L0_gnn_ln_w, L0_gnn_ln_b)
    h = jnp.maximum(_layernorm(x, axis=-1), 0.0)
    x = x + _L1_gnn_ref(h, edge_index, L1_gnn_Wq, L1_gnn_bq, L1_gnn_Wk, L1_gnn_bk, L1_gnn_Wv, L1_gnn_bv, L1_gnn_Wo, L1_gnn_bo, L1_gnn_Wpos, L1_gnn_bpos, L1_gnn_Wdeg, L1_gnn_bdeg, L1_gnn_ln1_g, L1_gnn_ln1_b, L1_gnn_ln2_g, L1_gnn_ln2_b, L1_gnn_W1, L1_gnn_b1, L1_gnn_W2, L1_gnn_b2)
    return x

_drawn_inputs = setup_inputs


def setup_inputs(seed=0):
    import zlib

    import numpy as np

    out = dict(_drawn_inputs(seed))
    spreads = {'L0_gnn_ln_w': (1.0, 0.2),
     'L0_gnn_ln_b': (0.0, 0.1),
     'L1_gnn_bq': (0.0, 0.1),
     'L1_gnn_bk': (0.0, 0.1),
     'L1_gnn_bv': (0.0, 0.1),
     'L1_gnn_bo': (0.0, 0.1),
     'L1_gnn_bpos': (0.0, 0.1),
     'L1_gnn_bdeg': (0.0, 0.1),
     'L1_gnn_ln1_g': (1.0, 0.2),
     'L1_gnn_ln1_b': (0.0, 0.1),
     'L1_gnn_ln2_g': (1.0, 0.2),
     'L1_gnn_ln2_b': (0.0, 0.1),
     'L1_gnn_b1': (0.0, 0.1),
     'L1_gnn_b2': (0.0, 0.1)}
    factors = {}
    for name, (base, spread) in spreads.items():
        noise = np.random.default_rng([zlib.crc32(name.encode()), seed]).standard_normal(out[name].shape)
        drawn = base * np.exp(spread * noise) if base else spread * noise
        out[name] = jnp.asarray(drawn.astype(out[name].dtype))
    for name, factor in factors.items():
        out[name] = (out[name] * factor).astype(out[name].dtype)
    return out
```

```python
from contextlib import ExitStack

import concourse.bass as bass
from concourse import mybir

ALU = mybir.AluOpType
ACT = mybir.ActivationFunctionType
AX_X = mybir.AxisListType.X
F32 = mybir.dt.float32
BF16 = mybir.dt.bfloat16
I32 = mybir.dt.int32
ENGINE = mybir.EngineType

P = 128
N, E, D = 6250, 100000, 128
HEADS, HD, LAYERS, FF = 8, 16, 2, 512
MW = D + HEADS
EPS = 1e-5
CLIP = 50.0
SUM_GUARD = 1e-16 * 1.9287498e-22
NT = -(-N // P)
NPAD = NT * P
LAST_ROWS = N - (NT - 1) * P
CLAMPED = "the step tables are clamped to this range where they are built"
SHIFT = 7

AT_EDGES = 128
AT_TILES = -(-E // AT_EDGES)
QUAD, QUADS = 4, 8
BODY = QUAD * QUADS
AT_BODIES = -(-(AT_TILES + NT - 1) // BODY)
AT_STEPS = AT_BODIES * BODY
AT_QUADS = AT_BODIES * QUADS
KV_SLOTS = BODY // 2
ARENA = 14400
ES_SUB = 4
ES_EDGES = P * ES_SUB
ES_TILES = -(-E // ES_EDGES)
ES_SLOTS = 4
ES_BODIES = -(-(ES_TILES + NT - 1) // ES_SLOTS)
HIST_ROWS = 125
HIST_COLS = E // HIST_ROWS
HIST_BODY = -(-HIST_COLS // ES_BODIES)
HIST_PAD = HIST_BODY * ES_BODIES

GROUP = 7
GROUPS = NT // GROUP
SUBS = ((0, 4), (4, 3))
assert GROUP * GROUPS == NT and P * SUBS[0][1] <= 512


class Table:

    def __init__(self, no, name, edges, tiles, steps, src):
        self.no, self.name, self.edges, self.tiles = no, name, edges, tiles
        self.chunks = -(-tiles // P)
        self.step_chunks = -(-steps // P)
        self.rows, self.steps = self.chunks * P, self.step_chunks * P
        self.last_start = E - edges
        self.repeated = tiles * edges - E
        self.src = src
        self.width = edges * (2 if src else 1) + 1


def gnn_kernel(nc, A, out):
    x, src, dst, edge_attr = A["x"], A["src"], A["dst"], A["edge_attr_128"]
    ES = Table(0, "es", ES_EDGES, ES_TILES, ES_BODIES * ES_SLOTS, False)
    AT = Table(1, "at", AT_EDGES, AT_TILES, AT_STEPS, True)
    TABLES = (ES, AT)

    ctx = ExitStack()
    with ctx:
        ctx.enter_context(nc.allow_non_contiguous_dma(reason="columns of indices and of small parameters"))

        def sb(name, shape, dt=F32):
            return ctx.enter_context(nc.sbuf_tensor(name, shape, dt))

        def sem(name):
            return ctx.enter_context(nc.semaphore(name))

        def sems(name, n):
            return [sem(f"{name}{i}") for i in range(n)]

        def dram(name, shape, dt=F32):
            return nc.dram_tensor(name, shape, dt).ap()

        kv_dram = [dram(f"kv_rows{l}", [NPAD, 2 * D]) for l in range(LAYERS)]
        x1_dram = dram("x1_rows", [NPAD, D])
        for T in TABLES:
            T.rows_dram = dram(f"{T.name}_rows", [T.rows, T.width], I32)
            T.nt_dram = dram(f"{T.name}_node_tile", [T.steps], I32)
        es_start_dram = dram("es_first_edge", [ES.steps], I32)

        xcur = sb("x_stream", [P, NT, D])
        q_all = sb("queries", [P, NT, D])
        agg = sb("aggregate", [P, NT, MW])
        iota_n = sb("iota_n", [P, P])
        ident = sb("ident", [P, P])
        hist_iota = sb("hist_iota", [P, P, HIST_BODY], BF16)
        src_lo = sb("src_lo", [HIST_ROWS, HIST_PAD], BF16)
        src_hi = sb("src_hi", [HIST_ROWS, HIST_PAD], BF16)
        deg = sb("degree", [P, NT])
        half_neg = sb("minus_half", [P, GROUP])
        ones_f = sb("ones_f", [P, P])
        at_negdst = sb("at_negdst", [P, AT.steps])
        at_src = sb("at_src", [P, AT.steps], I32)
        es_dst = sb("es_dst", [P, ES.steps, ES_SUB])
        es_start = sb("es_start", [1, ES.steps], I32)
        es_nt = sb("es_nt", [1, ES.steps], I32)
        at_nt = sb("at_nt", [1, AT.steps], I32)
        idx_stage = sb("idx_stage", [P, 2, KV_SLOTS], I32)
        w1_0 = sb("w1_0", [P, 2, D])
        w2_0 = sb("w2_0", [P, D])
        w3_0 = sb("w3_0", [P, D])
        cols_0 = sb("cols_0", [P, 2])
        rows_0 = sb("rows_0", [P, 3, D])
        w_qkv = [sb(f"w_qkv{l}", [P, 3 * D]) for l in range(LAYERS)]
        wdeg_bc = [sb(f"wdeg_bc{l}", [P, 3 * D]) for l in range(LAYERS)]
        bqkv_bc = [sb(f"bqkv_bc{l}", [P, 3 * D]) for l in range(LAYERS)]
        w_o = [sb(f"w_o{l}", [P, D]) for l in range(LAYERS)]
        w_up = [sb(f"w_up{l}", [P, FF]) for l in range(LAYERS)]
        w_down = [sb(f"w_down{l}", [P, FF // P, D]) for l in range(LAYERS)]
        b_up = [sb(f"b_up{l}", [P, FF // P]) for l in range(LAYERS)]
        rows_l = [sb(f"rows_l{l}", [P, 2, D]) for l in range(LAYERS)]
        bn = sb("bn", [P, GROUP, 6])
        norm_stat = sb("norm_stat", [P, 5, GROUP])
        mean, gap, spread2, var_eps, rstd = (norm_stat[:, i, :] for i in range(5))
        att_s = [sb(f"att_self{u}", [P, 3, 4 * HEADS]) for u in range(2)]
        arena = sb("arena", [P, ARENA])
        bank = ctx.enter_context(nc.psum_tensor("bank", [P, 8, 512], F32))

        class Area:

            def __init__(self, *regions):
                self.regions, self.at = list(regions), 0

            def take(self, words):
                while self.at + words > self.regions[0].shape[1]:
                    self.regions.pop(0)
                    self.at = 0
                v = self.regions[0][:, self.at:self.at + words]
                self.at += words
                return v

        area = Area(arena[:, :], xcur[:, :, :].rearrange("p t d -> p (t d)"), q_all[:, :, :].rearrange("p t d -> p (t d)"))
        for T in TABLES:
            T.first = area.take(T.chunks).bitcast(I32)
            T.last = area.take(T.chunks).bitcast(I32)
            T.ones_steps = area.take(T.chunks).bitcast(BF16).rearrange("p (c w) -> p c w", w=2)
            T.incl = area.take(T.chunks)
            T.done = area.take(T.chunks * T.steps // 2).bitcast(BF16).rearrange("p (c s) -> p c s", c=T.chunks)
            T.tile_i = area.take(T.step_chunks).bitcast(I32)
            T.start_i = area.take(T.step_chunks).bitcast(I32)
            T.off = area.take(T.step_chunks)
            T.step_id = area.take(T.step_chunks)
            T.ftile = area.take(T.step_chunks)
            T.ftile_i = area.take(T.step_chunks).bitcast(I32)
            T.nt_i = area.take(T.step_chunks).bitcast(I32)
            T.nt_nodes = area.take(T.step_chunks)
            T.step_rows = area.take(T.step_chunks * T.width).bitcast(I32).rearrange("p (k w) -> p k w", w=T.width)
            T.rel = area.take(T.step_chunks * T.edges).rearrange("p (k e) -> p k e", e=T.edges)
        src_f = area.take(AT.steps).rearrange("p (k e) -> p k e", e=P)
        iota_s = area.take(AT.steps)
        iota_i = area.take(AT.steps).bitcast(I32)
        step_id_i = area.take(AT.step_chunks).bitcast(I32)
        node_id_i = area.take(NT).bitcast(I32)
        node_mask = area.take(NT)
        deg_tmp = area.take(NT)
        stat = area.take(8)
        neg1 = area.take(P).bitcast(I32)
        zero_i = area.take(2 * P).bitcast(I32)
        tri = area.take(P // 2).bitcast(BF16)
        ones_b = area.take(P // 2).bitcast(BF16)
        src_i = area.take(2 * HIST_PAD)[0:HIST_ROWS, :].bitcast(I32).rearrange("p (a c) -> p a c", a=2)
        raw_qkv = [area.take(3 * D) for _ in range(LAYERS)]
        raw_pos = [area.take(D) for _ in range(LAYERS)]
        pos_t = [area.take(D) for _ in range(LAYERS)]
        raw_a = [area.take(3 * D) for _ in range(LAYERS)]
        bqkv_row = [area.take(3 * D)[0:1, :] for _ in range(LAYERS)]
        cols_l = [area.take(7 + FF // P) for _ in range(LAYERS)]
        bc_l = [area.take(3 * P).rearrange("p (i n) -> p i n", i=3) for _ in range(LAYERS)]

        area = Area(arena[:, :])
        es_attr = area.take(ES_SLOTS * ES_SUB * D).rearrange("p (s j d) -> p s j d", s=ES_SLOTS, j=ES_SUB)
        es_sel = area.take(ES_SLOTS * ES_SUB * P).rearrange("p (s j n) -> p s j n", s=ES_SLOTS, j=ES_SUB)
        oh_lo = area.take(P * HIST_BODY // 2)[0:HIST_ROWS, :].bitcast(BF16).rearrange("p (n c) -> p n c", c=HIST_BODY)
        oh_hi = area.take(NT * HIST_BODY // 2)[0:HIST_ROWS, :].bitcast(BF16).rearrange("p (n c) -> p n c", c=HIST_BODY)

        area = Area(arena[:, :])
        kv = area.take(KV_SLOTS * 2 * D).rearrange("p (s c) -> p s c", s=KV_SLOTS)
        sel = area.take(QUADS * QUAD * P).rearrange("p (k j n) -> p k j n", k=QUADS, j=QUAD)
        dist = area.take(QUAD * P).rearrange("p (j n) -> p j n", j=QUAD)
        sel_t = area.take(2 * QUAD * P).rearrange("p (k j e) -> p k j e", k=2, j=QUAD)
        q_win = area.take(2 * QUAD * D).rearrange("p (k j d) -> p k j d", k=2, j=QUAD)
        prod = area.take(2 * QUAD * D).rearrange("p (k j d) -> p k j d", k=2, j=QUAD)
        msg = area.take(2 * QUAD * MW).rearrange("p (k j c) -> p k j c", k=2, j=QUAD)
        att = area.take(2 * 3 * QUAD * HEADS).rearrange("p (k i c) -> p k i c", k=2, i=3)

        area = Area(arena[:, :])
        z, t_sb, xo, xob, xb, t1, hid = [], [], [], [], [], [], []
        for u in range(2):
            z.append(area.take(4 * D).rearrange("p (t d) -> p t d", t=4))
            t_sb.append(area.take(4 * P))
            xo.append(area.take(4 * D).rearrange("p (t d) -> p t d", t=4))
            xob.append(area.take(4 * D).rearrange("p (t d) -> p t d", t=4))
            xb.append(area.take(4 * D).rearrange("p (t d) -> p t d", t=4))
            t1.append(area.take(4 * D).rearrange("p (t d) -> p t d", t=4))
            hid.append(area.take(FF // P * 4 * P))
        h1_t = [hid[u][:, 0:512] for u in range(2)]
        h2_t = [hid[u][:, 512:1024] for u in range(2)]
        agg_t = [hid[u][:, 1024:1536] for u in range(2)]
        agg_s = [hid[u][:, 1536:2048].rearrange("p (t d) -> p t d", t=4) for u in range(2)]
        qkv = [hid[u][:, 0:4 * 3 * D].rearrange("p (t c) -> p t c", t=4) for u in range(2)]

        s_const = sem("const_ready")
        s_iota = sem("iota_ready")
        s_ends_zero = sem("ends_zeroed")
        s_ends = {T.name: sem(f"{T.name}_ends_loaded") for T in TABLES}
        s_rows = {T.name: sem(f"{T.name}_rows_written") for T in TABLES}
        s_src = sem("src_loaded")
        s_w0 = sem("w0_loaded")
        s_wl = sem("wl_loaded")
        s_dve = sem("dve_chain")
        s_steps = sem("steps_counted")
        s_incl = sem("steps_summed")
        s_done = sem("done_marked")
        s_tile = sem("tile_summed")
        s_tile_i = sem("tile_ready")
        s_got = {T.name: sem(f"{T.name}_rows_gathered") for T in TABLES}
        s_rel = sem("rel_ready")
        s_relt = sem("rel_transposed")
        s_tab = sem("table_ready")
        s_nt_out = {T.name: sem(f"{T.name}_nt_written") for T in TABLES}
        s_nt_in = {T.name: sem(f"{T.name}_nt_loaded") for T in TABLES}
        s_wprep = sem("weights_mixed")
        s_wmm = sem("weight_products")
        s_identity = sem("identity_ready")

        es_in = sems("es_attr_loaded", ES_SLOTS)
        es_sel_ready = sem("es_sel_ready")
        es_summed = sem("es_summed")
        es_added = sem("es_added")
        hist_oh = sem("hist_onehots_ready")
        hist_mm = sem("hist_counted")
        s_degmm = sem("degree_summed")
        s_degdve = sem("degree_parts_ready")
        s_degpow = sem("degree_std_ready")

        block = ctx.enter_context(nc.Block())

        def column(a):
            return a.rearrange("(p o) -> p o", o=1)

        n_ends = {"es": 0, "at": 0}
        n_rows = {"es": 0, "at": 0}
        W0_LOADS = 3 + 2 + 3
        WL_LOADS = LAYERS * (3 + 1 + 1 + 1 + 1 + 3 + 7 + 1 + 2)

        def sp_prepare(sp):
            sp.wait_ge(s_ends_zero, 1)
            for T in TABLES:
                e, full, tail = T.edges, (T.chunks - 1) * P, T.tiles - (T.chunks - 1) * P
                tiled = dst[0:(T.tiles - 1) * e].rearrange("(t e) -> t e", e=e)
                parts = []
                for c in range(T.chunks - 1):
                    parts += [(T.first[:, c:c + 1], tiled[c * P:(c + 1) * P, 0:1]),
                              (T.last[:, c:c + 1], tiled[c * P:(c + 1) * P, e - 1:e])]
                c = T.chunks - 1
                parts += [(T.first[0:tail - 1, c:c + 1], tiled[full:, 0:1]),
                          (T.last[0:tail - 1, c:c + 1], tiled[full:, e - 1:e]),
                          (T.first[tail - 1:tail, c:c + 1], column(dst[(T.tiles - 1) * e:(T.tiles - 1) * e + 1])),
                          (T.last[tail - 1:tail, c:c + 1], column(dst[E - 1:E]))]
                for o, i in parts:
                    sp.dma_start(o, i).then_inc(s_ends[T.name], 16)
                n_ends[T.name] = 16 * len(parts)
            sp.wait_ge(s_const, 1)
            for T in TABLES:
                e, last = T.edges, T.tiles - 1
                r = T.rows_dram
                parts = [(r[0:last, 0:e], dst[0:last * e].rearrange("(t e) -> t e", e=e)),
                         (r[last:last + 1, T.repeated:e], dst[last * e:E].rearrange("(o e) -> o e", o=1)),
                         (r[0:last, T.width - 1:T.width], dst[0:last * e].rearrange("(t e) -> t e", e=e)[:, 0:1]),
                         (r[last:last + 1, T.width - 1:T.width], column(dst[last * e:last * e + 1])),
                         (r[T.tiles:T.rows, T.width - 1:T.width], zero_i[0:T.rows - T.tiles, 0:1])]
                for a in range(0, T.repeated, P):
                    w = min(P, T.repeated - a)
                    parts.append((r[last:last + 1, a:a + w], neg1[0:1, 0:w]))
                for a in range(0, e, P):
                    parts.append((r[T.tiles:T.rows, a:a + P], neg1[0:T.rows - T.tiles, :]))
                if T.src:
                    parts += [(r[0:last, e:2 * e], src[0:last * e].rearrange("(t e) -> t e", e=e)),
                              (r[last:last + 1, e:2 * e], src[T.last_start:E].rearrange("(o e) -> o e", o=1)),
                              (r[T.tiles:T.rows, e:2 * e], zero_i[0:T.rows - T.tiles, 0:e])]
                for o, i in parts:
                    sp.dma_start(o, i).then_inc(s_rows[T.name], 16)
                n_rows[T.name] = 16 * len(parts)

        def sp_tables(sp):
            for T in TABLES:
                sp.wait_ge(s_rel, T.no + 1)
                sp.dma_start(T.nt_dram.rearrange("(k p) -> p k", p=P), T.nt_i).then_inc(s_nt_out[T.name], 16)
                n = 16
                if T is ES:
                    sp.dma_start(es_start_dram.rearrange("(k p) -> p k", p=P), T.start_i).then_inc(s_nt_out[T.name], 16)
                    n = 32
                sp.wait_ge(s_nt_out[T.name], n)
                sp.dma_start((es_nt if T is ES else at_nt)[:, :],
                             T.nt_dram.rearrange("(o s) -> o s", o=1)).then_inc(s_nt_in[T.name], 16)
                if T is ES:
                    sp.dma_start(es_start[:, :], es_start_dram.rearrange("(o s) -> o s", o=1)).then_inc(s_nt_in[T.name], 16)

        def act_load_weights(act):
            act.wait_ge(s_ends_zero, 1)
            act.dma_start(src_i[:, 0, 0:HIST_COLS], src.rearrange("(p c) -> p c", p=HIST_ROWS)).then_inc(s_src, 16)
            for o, i in ((w1_0[:, :, :], A["L0_gnn_W1"].rearrange("(k p) n -> p k n", p=P)),
                         (w2_0[:, :], A["L0_gnn_W2"]), (w3_0[:, :], A["L0_gnn_W3"]),
                         (cols_0[:, 0:1], column(A["L0_gnn_b1"])), (cols_0[:, 1:2], column(A["L0_gnn_b2"])),
                         (rows_0[:, 0, :], A["L0_gnn_b3"].partition_broadcast(P)),
                         (rows_0[:, 1, :], A["L0_gnn_ln_w"].partition_broadcast(P)),
                         (rows_0[:, 2, :], A["L0_gnn_ln_b"].partition_broadcast(P))):
                act.dma_start(o, i).then_inc(s_w0, 16)
            for l in range(LAYERS):
                w = {k[len("L1_gnn_"):]: v[l] for k, v in A.items() if k.startswith("L1_gnn_")}
                loads = [(raw_qkv[l][:, i * D:(i + 1) * D], w[k]) for i, k in enumerate(("Wq", "Wk", "Wv"))]
                loads += [(raw_pos[l], w["Wpos"]), (w_o[l][:, :], w["Wo"]), (w_up[l][:, :], w["W1"]),
                          (w_down[l][:, :, :], w["W2"].rearrange("(k p) n -> p k n", p=P))]
                loads += [(bqkv_row[l][:, i * D:(i + 1) * D], w[k].rearrange("(o d) -> o d", o=1))
                          for i, k in enumerate(("bq", "bk", "bv"))]
                cols = [w["ln1_g"], w["ln1_b"], w["bpos"], w["bdeg"], w["Wdeg"].rearrange("o d -> (o d)"), w["ln2_g"], w["ln2_b"]]
                loads += [(cols_l[l][:, i:i + 1], column(c)) for i, c in enumerate(cols)]
                loads += [(cols_l[l][:, 7:7 + FF // P], w["b1"].rearrange("(k p) -> p k", p=P)),
                          (rows_l[l][:, 0, :], w["bo"].partition_broadcast(P)),
                          (rows_l[l][:, 1, :], w["b2"].partition_broadcast(P))]
                for o, i in loads:
                    act.dma_start(o, i).then_inc(s_wl, 16)

        def pool_prepare(pool):
            pool.memset(neg1, -1)
            pool.memset(zero_i, 0)
            pool.memset(ones_b, 1.0)
            pool.memset(tri, 1.0)
            pool.memset(ones_f[:, :], 1.0)
            pool.memset(ident[:, :], 1.0)
            pool.memset(half_neg[:, :], -0.5).then_inc(s_const, 1)
            pool.iota(iota_i, [[1, AT.steps]], base=0, channel_multiplier=0)
            pool.iota(step_id_i, [[P, AT.step_chunks]], base=0, channel_multiplier=1)
            pool.iota(node_id_i, [[P, NT]], base=0, channel_multiplier=1).then_inc(s_iota, 1)
            pool.wait_ge(s_const, 1)
            pool.affine_select(out=tri, in_=tri, pattern=[[1, P]], compare_op=ALU.is_ge, fill=0.0, base=0, channel_multiplier=-1)
            pool.affine_select(out=ident[:, :], in_=ident[:, :], pattern=[[1, P]], compare_op=ALU.is_equal, fill=0.0, base=0,
                               channel_multiplier=-1).then_inc(s_identity, 1)

        def pool_gather_rows(pool):
            for T in TABLES:
                pool.wait_ge(s_rows[T.name], n_rows[T.name])
                pool.wait_ge(s_tile_i, T.no + 1)
                for k in range(T.step_chunks):
                    pool.indirect_dma_start(T.step_rows[:, k, :], None, T.rows_dram,
                                            bass.IndirectOffsetOnAxis(T.tile_i[:, k:k + 1], 0)).then_inc(s_got[T.name], 16)

        chain = [0]

        def link(dve, ins):
            chain[0] += 1
            ins.then_inc(s_dve, 1)
            dve.wait_ge(s_dve, chain[0])

        def dve_prepare(dve):
            for T in TABLES:
                dve.memset(T.first, 0)
                dve.memset(T.last, 0)
            dve.memset(src_i, -1).then_inc(s_ends_zero, 1)
            for T in TABLES:
                dve.memset(T.ones_steps, 1.0)
            link(dve, dve.memset(agg[:, :, :], 0.0))
            dve.wait_ge(s_iota, 1)
            dve.tensor_copy(iota_s, iota_i)
            dve.tensor_copy(iota_n[:, :], iota_i[:, 0:P])
            for T in TABLES:
                dve.tensor_copy(T.step_id, step_id_i[:, 0:T.step_chunks])
            dve.tensor_scalar(node_mask, node_id_i, float(N), None, ALU.is_lt)
            link(dve, dve.tensor_copy(hist_iota[:, :, :], iota_i[:, 0:P].unsqueeze(2).to_broadcast([P, P, HIST_BODY])))
            for T in TABLES:
                dve.wait_ge(s_ends[T.name], n_ends_total(T))
                dve.tensor_scalar(T.first, T.first, SHIFT, None, ALU.arith_shift_right)
                link(dve, dve.tensor_scalar(T.last, T.last, SHIFT, None, ALU.arith_shift_right))
                dve.scalar_tensor_tensor(out=T.ones_steps[:, :, 1], in0=T.last, scalar=1.0, in1=T.first, op0=ALU.add,
                                         op1=ALU.subtract).then_inc(s_steps, 1)
            dve.wait_ge(s_src, 16)
            dve.tensor_scalar(src_i[:, 1, :], src_i[:, 0, :], SHIFT, None, ALU.arith_shift_right)
            link(dve, dve.tensor_scalar(src_i[:, 0, :], src_i[:, 0, :], P - 1, None, ALU.bitwise_and))
            dve.tensor_copy(src_lo[:, :], src_i[:, 0, :])
            link(dve, dve.tensor_copy(src_hi[:, :], src_i[:, 1, :]))
            for T in TABLES:
                dve.wait_ge(s_incl, T.no + 1)
                link(dve, dve.tensor_copy(T.incl, small(T, 0)))
                for c in range(T.chunks):
                    last = dve.tensor_scalar(T.done[:, c, :], iota_s[:, 0:T.steps], T.incl[:, c:c + 1], None, ALU.is_ge)
                last.then_inc(s_done, 1)
            for T in TABLES:
                dve.wait_ge(s_tile, T.no + 1)
                sums = small(T, 1)
                dve.tensor_copy(T.off, sums[:, :, 1])
                if T is ES:
                    dve.tensor_scalar(T.start_i, sums[:, :, 0], float(T.edges), float(T.last_start), ALU.mult, ALU.min)
                dve.tensor_scalar(T.tile_i, sums[:, :, 0], float(T.rows - 1), None, ALU.min).then_inc(s_tile_i, 1)
            dve_weights(dve)
            for T in TABLES:
                dve.wait_ge(s_got[T.name], 16 * T.step_chunks)
                link(dve, dve.tensor_scalar(T.ftile_i, T.step_rows[:, :, T.width - 1], SHIFT, None, ALU.arith_shift_right))
                link(dve, dve.tensor_tensor(T.ftile, T.ftile_i, T.off, ALU.subtract))
                link(dve, dve.tensor_tensor(T.ftile, T.ftile, T.step_id, ALU.add))
                link(dve, dve.tensor_scalar(T.ftile, T.ftile, 0.0, float(NT - 1), ALU.max, ALU.min))
                dve.tensor_copy(T.nt_i, T.ftile)
                link(dve, dve.tensor_scalar(T.nt_nodes, T.ftile, float(P), None, ALU.mult))
                for k in range(T.step_chunks):
                    rel = T.nt_nodes[:, k:k + 1]
                    if T is ES:
                        last = dve.tensor_scalar(T.rel[:, k, :], T.step_rows[:, k, 0:T.edges], rel, None, ALU.subtract)
                    else:
                        last = dve.tensor_scalar(T.rel[:, k, :], T.step_rows[:, k, 0:T.edges], -1.0, rel, ALU.mult, ALU.add)
                if T.src:
                    last = dve.tensor_copy(src_f, T.step_rows[:, :, T.edges:2 * T.edges])
                last.then_inc(s_rel, 1)
            dve.wait_ge(s_relt, 1)
            dve.tensor_copy(es_dst[:, :, :].rearrange("p (k s) j -> p k s j", s=P),
                            bank[:, 6:8, :].rearrange("p b (j s) -> p b s j", s=P)).then_inc(s_tab, 1)
            dve.wait_ge(s_relt, 2)
            dve.tensor_copy(at_negdst[:, :], bank[:, 2:4, :].rearrange("p b c -> p (b c)")[:, 0:AT.steps])
            dve.tensor_copy(at_src[:, :], bank[:, 4:6, :].rearrange("p b c -> p (b c)")[:, 0:AT.steps]).then_inc(s_tab, 1)

        def n_ends_total(T):
            return 16 * (2 * (T.chunks - 1) + 4)

        def small(T, what):
            if what == 0:
                return bank[:, T.no, 0:T.chunks]
            return bank[:, T.no, 16:16 + 2 * T.step_chunks].rearrange("p (k w) -> p k w", w=2)

        QS = 1.0 / float(HD) ** 0.5

        def dve_weights(dve):
            dve.wait_ge(s_identity, 1)
            dve.wait_ge(s_wl, 16 * WL_LOADS)
            for l in range(LAYERS):
                c = cols_l[l]
                dve.tensor_tensor(raw_pos[l], raw_pos[l], ident[:, :], ALU.add)
                link(dve, dve.tensor_tensor(c[:, 2:3], c[:, 2:3], c[:, 3:4], ALU.add))
                for i, k in enumerate((1, 2, 4)):
                    last = dve.tensor_copy(bc_l[l][:, i, :], c[:, k:k + 1].to_broadcast([P, P]))
                last.then_inc(s_wprep, 1)
            for l in range(LAYERS):
                dve.wait_ge(s_wmm, 1 + l)
                dve.tensor_copy(pos_t[l], bank[:, 2 + 3 * l, 0:P]).then_inc(s_wprep, 1)
                dve.tensor_scalar(wdeg_bc[l][:, 0:D], bank[:, 2 + 3 * l, P:P + D], QS, None, ALU.mult)
                dve.tensor_copy(wdeg_bc[l][:, D:3 * D], bank[:, 2 + 3 * l, P + D:P + 3 * D])
                dve.tensor_tensor(b_up[l][:, :], bank[:, 4 + 3 * l, 384:388], cols_l[l][:, 7:11], ALU.add)
                dve.tensor_scalar(w_up[l][:, :], w_up[l][:, :], cols_l[l][:, 5:6], None, ALU.mult)
            for l in range(LAYERS):
                a = bank[:, 3 + 3 * l, 0:3 * D]
                dve.wait_ge(s_wmm, 3 + l)
                dve.tensor_copy(raw_a[l], a).then_inc(s_wprep, 1)
                dve.tensor_scalar(w_qkv[l][:, 0:D], a[:, 0:D], cols_l[l][:, 0:1], QS, ALU.mult, ALU.mult)
                dve.tensor_scalar(w_qkv[l][:, D:3 * D], a[:, D:3 * D], cols_l[l][:, 0:1], None, ALU.mult)
            for l in range(LAYERS):
                b = bank[:, 4 + 3 * l, 0:3 * D]
                dve.wait_ge(s_wmm, 5 + l)
                dve.tensor_scalar(bqkv_bc[l][:, 0:D], b[:, 0:D], QS, None, ALU.mult)
                dve.tensor_copy(bqkv_bc[l][:, D:3 * D], b[:, D:3 * D]).then_inc(s_wprep, 1)

        def pe_prepare(pe):
            pe.wait_ge(s_identity, 1)
            for T in TABLES:
                pe.wait_ge(s_steps, T.no + 1)
                last = pe.matmul(small(T, 0), tri, T.ones_steps[:, :, 1], start=True, stop=T.chunks == 1, skip_group_check=True)
                for c in range(T.chunks - 1):
                    last = pe.matmul(small(T, 0)[:, c + 1:], ones_b, T.ones_steps[:, c:c + 1, 1].to_broadcast([P, T.chunks - 1 - c]),
                                     start=False, stop=c == T.chunks - 2, skip_group_check=True)
                last.then_inc(s_incl, 1)
            for T in TABLES:
                pe.wait_ge(s_done, T.no + 1)
                for k in range(T.step_chunks):
                    for c in range(T.chunks):
                        last = pe.matmul(small(T, 1)[:, k, :], T.done[:, c, k * P:(k + 1) * P], T.ones_steps[:, c, :],
                                         start=c == 0, stop=c == T.chunks - 1)
                last.then_inc(s_tile, 1)
            for l in range(LAYERS):
                pe.wait_ge(s_wprep, 1 + l)
                pe.transpose(bank[:, 2 + 3 * l, 0:P], raw_pos[l], ident[:, :])
                pe.matmul(bank[:, 2 + 3 * l, P:P + 3 * D], bc_l[l][:, 2, :], raw_qkv[l], start=True, stop=True)
                for k in range(FF // P):
                    last = pe.matmul(bank[:, 4 + 3 * l, 384 + k:385 + k], w_up[l][:, k * P:(k + 1) * P], cols_l[l][:, 6:7],
                                     start=True, stop=True)
                last.then_inc(s_wmm, 1)
            for l in range(LAYERS):
                pe.wait_ge(s_wprep, 3 + l)
                pe.matmul(bank[:, 3 + 3 * l, 0:3 * D], pos_t[l], raw_qkv[l], start=True, stop=True).then_inc(s_wmm, 1)
            for l in range(LAYERS):
                b = bank[:, 4 + 3 * l, 0:3 * D]
                pe.wait_ge(s_wprep, 5 + l)
                pe.matmul(b, bc_l[l][:, 1, :], raw_qkv[l], start=True, stop=False)
                pe.matmul(b, ones_f[0:1, :], bqkv_row[l], start=False, stop=False)
                pe.matmul(b, bc_l[l][:, 0, :], raw_a[l], start=False, stop=True).then_inc(s_wmm, 1)
            pe.wait_ge(s_wprep, 6 + LAYERS)
            pe.wait_ge(s_rel, 1)
            for k in range(ES.step_chunks):
                for j in range(ES_SUB):
                    last = pe.transpose(bank[:, 6 + k, j * P:(j + 1) * P],
                                        ES.rel[:, k, :].rearrange("s (p j) -> s p j", j=ES_SUB)[:, :, j], ident[:, :])
            last.then_inc(s_relt, 1)
            pe.wait_ge(s_rel, 2)
            for k in range(AT.step_chunks):
                pe.transpose(bank[:, 2 + k // 4, k % 4 * P:(k % 4 + 1) * P], AT.rel[:, k, :], ident[:, :])
                last = pe.transpose(bank[:, 4 + k // 4, k % 4 * P:(k % 4 + 1) * P], src_f[:, k, :], ident[:, :])
            last.then_inc(s_relt, 1)

        def sp_edge_sums(sp):
            sp.wait_ge(s_nt_in["es"], 32)
            sp.wait_ge(s_tab, 2)

            def body(i, first):
                _, starts = nc.values_load_multi_w_load_instructions(
                    es_start[0:1, bass.ds(i * ES_SLOTS, ES_SLOTS)], engines=(ENGINE.SP,), min_val=0, max_val=E - ES_EDGES, skip_runtime_bounds_check_because=CLAMPED)
                for s in range(ES_SLOTS):
                    if not first:
                        sp.wait_ge(es_summed, (i - 1) * ES_SLOTS + s + 1)
                    sp.dma_start(es_attr[:, s, :, :],
                                 edge_attr[bass.ds(starts[s], ES_EDGES), :].rearrange("(p j) d -> p j d", j=ES_SUB)
                                 ).then_inc(es_in[s], 16)
            body(0, True)
            with sp.Fori(1, ES_BODIES) as i:
                body(i, False)

        def pe_edge_sums(pe):
            def body(i, first, last_body):
                for s in range(ES_SLOTS):
                    pe.wait_ge(es_in[s], 16 * (i + 1))
                    pe.wait_ge(es_sel_ready, i * ES_SLOTS + s + 1)
                    if not first:
                        pe.wait_ge(es_added, (i - 1) * ES_SLOTS + s + 1)
                    for j in range(ES_SUB):
                        last = pe.matmul(bank[:, 4 + s, 0:D], es_sel[:, s, j, :], es_attr[:, s, j, :],
                                         start=j == 0, stop=j == ES_SUB - 1)
                    last.then_inc(es_summed, 1)
                pe.wait_ge(hist_oh, i + 1)
                for c in range(HIST_BODY):
                    last = pe.matmul(bank[:, 0, 0:NT], oh_lo[:, :, c], oh_hi[:, :, c], start=first and c == 0,
                                     stop=last_body and c == HIST_BODY - 1, skip_group_check=True)
                last.then_inc(hist_mm, 1)
            body(0, True, False)
            with pe.Fori(1, ES_BODIES - 1) as i:
                body(i, False, False)
            body(ES_BODIES - 1, False, True)
            pe.wait_ge(s_degdve, 1)
            pe.matmul(bank[:, 1, 0:NT], ones_f[:, :], deg_tmp, start=True, stop=True).then_inc(s_degmm, 1)
            pe.wait_ge(s_degdve, 2)
            pe.matmul(bank[:, 1, 64:64 + NT], ones_f[:, :], deg_tmp, start=True, stop=True).then_inc(s_degmm, 1)

        def dve_edge_sums(dve):
            dve.wait_ge(s_nt_in["es"], 32)
            dve.wait_ge(s_tab, 2)

            def body(i, first):
                if not first:
                    dve.wait_ge(hist_mm, i)
                cols = bass.ds(i * HIST_BODY, HIST_BODY)
                dve.tensor_tensor(oh_lo, hist_iota[0:HIST_ROWS, :, :],
                                  src_lo[:, cols].unsqueeze(1).to_broadcast([HIST_ROWS, P, HIST_BODY]), ALU.is_equal)
                dve.tensor_tensor(oh_hi, hist_iota[0:HIST_ROWS, 0:NT, :],
                                  src_hi[:, cols].unsqueeze(1).to_broadcast([HIST_ROWS, NT, HIST_BODY]),
                                  ALU.is_equal).then_inc(hist_oh, 1)
                _, tiles = nc.values_load_multi_w_load_instructions(
                    es_nt[0:1, bass.ds(i * ES_SLOTS, ES_SLOTS)], engines=(ENGINE.DVE,), min_val=0, max_val=NT - 1, skip_runtime_bounds_check_because=CLAMPED)
                for s in range(ES_SLOTS):
                    if not first:
                        dve.wait_ge(es_summed, (i - 1) * ES_SLOTS + s + 1)
                    dve.tensor_tensor(es_sel[:, s, :, :], iota_n[:, :].unsqueeze(1).to_broadcast([P, ES_SUB, P]),
                                      es_dst[:, bass.ds(i * ES_SLOTS + s, 1), :].rearrange("p s j -> p (s j)").unsqueeze(2)
                                      .to_broadcast([P, ES_SUB, P]), ALU.is_equal).then_inc(es_sel_ready, 1)
                for s in range(ES_SLOTS):
                    dve.wait_ge(es_summed, i * ES_SLOTS + s + 1)
                    if not (first and s == 0):
                        dve.wait_ge(es_added, i * ES_SLOTS + s)
                    a = agg[:, bass.ds(tiles[s], 1), 0:D].rearrange("p t d -> p (t d)")
                    dve.tensor_tensor(a, bank[:, 4 + s, 0:D], a, ALU.add).then_inc(es_added, 1)
            body(0, True)
            with dve.Fori(1, ES_BODIES) as i:
                body(i, False)
            dve.wait_ge(hist_mm, ES_BODIES)
            link(dve, dve.tensor_scalar(deg[:, :], bank[:, 0, 0:NT], 1.0, None, ALU.add))
            dve.tensor_tensor(deg_tmp, deg[:, :], node_mask, ALU.mult).then_inc(s_degdve, 1)
            dve.wait_ge(s_degmm, 1)
            link(dve, dve.tensor_reduce(stat[:, 0:1], bank[:, 1, 0:NT], AX_X, ALU.add))
            link(dve, dve.tensor_scalar(stat[:, 1:2], stat[:, 0:1], 1.0 / N, None, ALU.mult))
            link(dve, dve.tensor_scalar(deg[:, :], deg[:, :], stat[:, 1:2], None, ALU.subtract))
            link(dve, dve.tensor_tensor(deg[:, :], deg[:, :], node_mask, ALU.mult))
            dve.tensor_tensor(deg_tmp, deg[:, :], deg[:, :], ALU.mult).then_inc(s_degdve, 1)
            dve.wait_ge(s_degmm, 2)
            link(dve, dve.tensor_reduce(stat[:, 2:3], bank[:, 1, 64:64 + NT], AX_X, ALU.add))
            dve.tensor_scalar(stat[:, 3:4], stat[:, 2:3], 1.0 / (N - 1), None, ALU.mult).then_inc(s_degdve, 1)
            dve.wait_ge(s_degpow, 2)
            link(dve, dve.tensor_scalar(stat[:, 5:6], stat[:, 5:6], 1e-6, None, ALU.add))
            link(dve, dve.reciprocal(stat[:, 6:7], stat[:, 5:6]))
            link(dve, dve.tensor_scalar(deg[:, :], deg[:, :], stat[:, 6:7], None, ALU.mult))

        def pool_degree(pool):
            pool.memset(stat[:, 4:5], 0.5).then_inc(s_degpow, 1)
            pool.wait_ge(s_degdve, 3)
            pool.wait_ge(s_degpow, 1)
            pool.tensor_tensor(stat[:, 5:6], stat[:, 3:4], stat[:, 4:5], ALU.pow).then_inc(s_degpow, 1)

        PER_GROUP = {
            "loaded": (16, 0, 16), "var": (4, 2, 1), "rstd": (4, 2, 1), "z": (2, 2, 1), "t": (2, 2, 1), "t_sb": (2, 2, 1),
            "agg_s": (1, 0, 0), "aggt": (1, 1, 1), "aggt_sb": (1, 1, 1), "h1": (1, 0, 0), "h1_sb": (1, 0, 0), "h2": (1, 0, 0),
            "h2_sb": (1, 0, 0), "o": (1, 1, 1), "zw": (1, 0, 1), "x1": (1, 0, 0), "zr": (1, 0, 0), "xh": (1, 0, 0),
            "qkv": ("t", "t", 0), "qkv_out": ("t", "t", 0), "biased": (1, 1, 0), "q_out": (1, 1, 0), "kv_out": (16, 16, 0),
            "kept": (1, 1, 0), "att": (1, 1, 0), "ex": (1, 1, 0), "an": (0, 1, 1), "xb": (0, 1, 1), "xo": (0, 1, 1), "xob": (0, 1, 1),
            "up": (0, FF // P, FF // P), "up_sb": (0, FF // P, FF // P), "down": (0, 1, 1), "y": (0, 1, 1), "saved": (16, 0, 16),
        }
        dense_sem = {(name, u): sem(f"{name}{u}") for name in PER_GROUP for u in range(2)}
        dense_chain = sem("dense_dve_chain")

        def counted_before(name, u, ph):
            per = [SUBS[u][1] if c == "t" else c for c in PER_GROUP[name][:ph]]
            partial = 16 * u if name == "loaded" and ph > 0 else 0
            return GROUPS * sum(per) + partial

        def tiles_at(g, u):
            return g * GROUP + SUBS[u][0], SUBS[u][1]

        def node_view(buf, g, u, lo=0, hi=D):
            base, t = tiles_at(g, u)
            return buf[:, bass.ds(base, t), lo:hi]

        def rows_of(d, g, u, whole):
            base, t = tiles_at(g, u)
            return d[bass.ds(base * P, whole * P), :].rearrange("(t p) c -> p t c", p=P)

        class Phase:

            def __init__(self, ph, kind, layer_post, layer_pre, norms):
                self.ph, self.kind, self.post, self.pre = ph, kind, layer_post, layer_pre
                self.norms = norms
                self.n = 0

            def s(self, name, u):
                return dense_sem[name, u]

            def at(self, name, u, n):
                return counted_before(name, u, self.ph) + n

            def wait_last(self, eng, name, u, n):
                if not (isinstance(n, int) and self.at(name, u, n) == 0):
                    eng.wait_ge(self.s(name, u), self.at(name, u, n))

            def begin(self):
                self.n = 0

            def end(self):
                assert self.n == self.chain_len, (self.ph, self.n)

            def mark(self, ins):
                self.n += 1
                ins.then_inc(dense_chain, 1)

            def see(self, dve, g):
                dve.wait_ge(dense_chain, self.chain_base + g * self.chain_len + self.n)

        MLP, POST, FINAL = range(3)
        phases = [Phase(0, MLP, None, 0, 4), Phase(1, POST, 0, 1, 2), Phase(2, FINAL, 1, None, 1)]
        T_BANK, O_BANK, H_BANK = (0, 1), (2, 3), ((4, 5), (6, 7))

        def run_groups(eng, body):
            body(0, False)
            with eng.Fori(1, GROUPS - 1) as g:
                body(g, False)
            body(GROUPS - 1, True)

        def sp_dense(sp, F):
            s = F.s

            def transfer(d, buf, g, u, last, store, done):
                base, t = tiles_at(g, u)
                whole = t - 1 if last and u == 1 and d.shape[0] == N else t
                pairs = [(rows_of(d, g, u, whole), buf[:, 0:whole, :])]
                if whole < t:
                    pairs.append((d[(NT - 1) * P:N, :], buf[0:LAST_ROWS, t - 1, :]))
                else:
                    pairs = [(rows_of(d, g, u, t), buf[:, 0:t, :])]
                for dr, sbv in pairs:
                    sp.dma_start(*((dr, sbv) if store else (sbv, dr))).then_inc(done, 16)

            def body(g, last):
                for u in range(2):
                    if F.kind == MLP:
                        F.wait_last(sp, "x1", u, g)
                        transfer(x, xb[u], g, u, last, False, s("loaded", u))
                    if F.kind == FINAL:
                        F.wait_last(sp, "xob", u, g)
                        transfer(x1_dram, t1[u], g, u, last, False, s("loaded", u))
                for u in range(2):
                    if F.kind == MLP:
                        sp.wait_ge(s("x1", u), F.at("x1", u, g + 1))
                        transfer(x1_dram, xo[u], g, u, last, True, s("saved", u))
                    if F.pre is not None:
                        sp.wait_ge(s("biased", u), F.at("biased", u, g + 1))
                        base, t = tiles_at(g, u)
                        sp.dma_start(kv_dram[F.pre][bass.ds(base * P, t * P), :].rearrange("(t p) c -> p t c", p=P),
                                     qkv[u][:, 0:t, D:3 * D]).then_inc(s("kv_out", u), 16)
                    if F.kind == FINAL:
                        sp.wait_ge(s("y", u), F.at("y", u, g + 1))
                        transfer(out, xo[u], g, u, last, True, s("saved", u))
            return body

        def pool_rstd(pool, F, count):
            pool.wait_ge(F.s("var", 0), F.at("var", 0, count))
            pool.tensor_tensor(rstd, var_eps, half_neg[:, :], ALU.pow).then_inc(F.s("rstd", 0), 1)

        def pool_dense(pool, F):
            s, l = F.s, F.pre

            def body(g, last):
                if F.kind == MLP:
                    pool_rstd(pool, F, F.norms * g + 1)
                    for u in range(2):
                        t = SUBS[u][1]
                        F.wait_last(pool, "aggt", u, g)
                        F.wait_last(pool, "kv_out", u, 16 * g)
                        pool.tensor_copy(agg_s[u][:, 0:t, :], node_view(agg, g, u, 0, D)).then_inc(s("agg_s", u), 1)
                    for i in range(1, F.norms):
                        pool_rstd(pool, F, F.norms * g + i + 1)
                else:
                    lp = F.post
                    for u in range(2):
                        t = SUBS[u][1]
                        F.wait_last(pool, "xo", u, g)
                        pool.tensor_tensor(xb[u][:, 0:t, :], node_view(xcur, g, u),
                                           rows_l[lp][:, 0:1, :].to_broadcast([P, t, D]), ALU.add).then_inc(s("xb", u), 1)
                    pool_rstd(pool, F, F.norms * g + 1)
                    for u in range(2):
                        t = SUBS[u][1]
                        if F.kind == FINAL:
                            pool.wait_ge(s("loaded", u), F.at("loaded", u, 16 * (g + 1)))
                            pool.tensor_tensor(xob[u][:, 0:t, :], xo[u][:, 0:t, :], t1[u][:, 0:t, :], ALU.add).then_inc(s("zw", u), 1)
                            pool.wait_ge(s("zw", u), F.at("zw", u, g + 1))
                            pool.tensor_tensor(xob[u][:, 0:t, :], xob[u][:, 0:t, :],
                                               rows_l[lp][:, 1:2, :].to_broadcast([P, t, D]), ALU.add).then_inc(s("xob", u), 1)
                        else:
                            pool.tensor_tensor(xob[u][:, 0:t, :], xo[u][:, 0:t, :],
                                               rows_l[lp][:, 1:2, :].to_broadcast([P, t, D]), ALU.add).then_inc(s("xob", u), 1)
                    if F.pre is not None:
                        pool_rstd(pool, F, F.norms * g + 2)
                if F.pre is not None:
                    for u in range(2):
                        t = SUBS[u][1]
                        name, rows = ("xh", xob) if F.kind == MLP else ("y", xo)
                        pool.wait_ge(s(name, u), F.at(name, u, g + 1))
                        pool.sem_inc(Z.turn, 1)
                        pool.tensor_copy(node_view(xcur, g, u), rows[u][:, 0:t, :]).then_inc(s("kept", u), 1)
                    for u in range(2):
                        t = SUBS[u][1]
                        pool.wait_ge(s("qkv_out", u), F.at("qkv_out", u, SUBS[u][1] * (g + 1)))
                        pool.tensor_tensor(qkv[u][:, 0:t, :], qkv[u][:, 0:t, :],
                                           bqkv_bc[l][:, :].unsqueeze(1).to_broadcast([P, t, 3 * D]), ALU.add).then_inc(s("biased", u), 1)
                        pool.wait_ge(s("biased", u), F.at("biased", u, g + 1))
                        pool.sem_inc(Z.turn, 1)
                        pool.tensor_copy(node_view(q_all, g, u), qkv[u][:, 0:t, 0:D]).then_inc(s("q_out", u), 1)
            return body

        def pe_transposes(pe, F, u, src_rows, ready, n, done):
            pe.wait_ge(F.s(ready, u), F.at(ready, u, n))
            for t in range(SUBS[u][1]):
                last = pe.transpose(bank[:, T_BANK[u], t * P:(t + 1) * P], src_rows[:, t, :], ident[:, :])
            last.then_inc(F.s(done, u), 1)

        def pe_dense(pe, F):
            s = F.s

            def body(g, last):
                if F.kind == MLP:
                    for u in range(2):
                        pe_transposes(pe, F, u, z[u], "z", F.norms_t * g + 1, "t")
                    for u in range(2):
                        pe.wait_ge(s("t_sb", u), F.at("t_sb", u, 2 * g + 1))
                        pe_transposes(pe, F, u, agg_s[u], "agg_s", g + 1, "aggt")
                    for u in range(2):
                        c = SUBS[u][1] * P
                        pe.wait_ge(s("aggt_sb", u), F.at("aggt_sb", u, g + 1))
                        pe.matmul(bank[:, H_BANK[u][0], 0:c], w1_0[:, 0, :], t_sb[u][:, 0:c], start=True, stop=False)
                        pe.matmul(bank[:, H_BANK[u][0], 0:c], w1_0[:, 1, :], agg_t[u][:, 0:c], start=False, stop=True).then_inc(s("h1", u), 1)
                    for u in range(2):
                        c = SUBS[u][1] * P
                        pe.wait_ge(s("h1_sb", u), F.at("h1_sb", u, g + 1))
                        pe.matmul(bank[:, H_BANK[u][1], 0:c], w2_0[:, :], h1_t[u][:, 0:c], start=True, stop=True).then_inc(s("h2", u), 1)
                    for u in range(2):
                        pe.wait_ge(s("h2_sb", u), F.at("h2_sb", u, g + 1))
                        for t in range(SUBS[u][1]):
                            m = pe.matmul(bank[:, O_BANK[u], t * P:(t + 1) * P], h2_t[u][:, t * P:(t + 1) * P], w3_0[:, :],
                                          start=True, stop=True)
                        m.then_inc(s("o", u), 1)
                else:
                    l = F.post
                    for u in range(2):
                        pe_transposes(pe, F, u, z[u], "an", g + 1, "aggt")
                    for u in range(2):
                        pe.wait_ge(s("aggt_sb", u), F.at("aggt_sb", u, g + 1))
                        for t in range(SUBS[u][1]):
                            m = pe.matmul(bank[:, O_BANK[u], t * P:(t + 1) * P], t_sb[u][:, t * P:(t + 1) * P], w_o[l][:, :],
                                          start=True, stop=True)
                        m.then_inc(s("o", u), 1)
                    for u in range(2):
                        pe_transposes(pe, F, u, z[u], "z", F.norms_t * g + 1, "t")
                    nt = F.norms_t
                    for k in range(FF // P):
                        for u in range(2):
                            c = SUBS[u][1] * P
                            if k == 0:
                                pe.wait_ge(s("t_sb", u), F.at("t_sb", u, nt * g + 1))
                            if k >= 2:
                                pe.wait_ge(s("up_sb", u), F.at("up_sb", u, (FF // P) * g + k - 1))
                            pe.matmul(bank[:, H_BANK[u][k % 2], 0:c], w_up[l][:, k * P:(k + 1) * P], t_sb[u][:, 0:c],
                                      start=True, stop=True).then_inc(s("up", u), 1)
                    for u in range(2):
                        pe.wait_ge(s("up_sb", u), F.at("up_sb", u, (FF // P) * (g + 1)))
                        pe.wait_ge(s("xo", u), F.at("xo", u, g + 1))
                        for t in range(SUBS[u][1]):
                            for k in range(FF // P):
                                m = pe.matmul(bank[:, O_BANK[u], t * P:(t + 1) * P],
                                              hid[u][:, k * 512 + t * P:k * 512 + (t + 1) * P], w_down[l][:, k, :],
                                              start=k == 0, stop=k == FF // P - 1)
                        m.then_inc(s("down", u), 1)
                if F.pre is not None:
                    for u in range(2):
                        pe_transposes(pe, F, u, z[u], "z", F.norms_t * (g + 1), "t")
                    for t in range(4):
                        for u in range(2):
                            if t == 0:
                                pe.wait_ge(s("t_sb", u), F.at("t_sb", u, F.norms_t * (g + 1)))
                            if t >= SUBS[u][1]:
                                continue
                            if t >= 2:
                                pe.wait_ge(s("qkv_out", u), F.at("qkv_out", u, SUBS[u][1] * g + t - 1))
                            pe.matmul(bank[:, H_BANK[u][t % 2], 0:3 * D], t_sb[u][:, t * P:(t + 1) * P], w_qkv[F.pre][:, :],
                                      start=True, stop=True).then_inc(s("qkv", u), 1)
            return body

        def act_dense(act, F):
            s = F.s

            def move(u, wait, n, dest, done, func=ACT.Copy, bias=None, from_bank=None):
                c = SUBS[u][1] * P
                act.wait_ge(s(wait, u), F.at(wait, u, n))
                kw = {} if bias is None else {"bias": bias}
                act.activation(dest[:, 0:c], bank[:, T_BANK[u] if from_bank is None else from_bank, 0:c], func, **kw).then_inc(s(done, u), 1)

            def body(g, last):
                if F.kind == MLP:
                    for u in range(2):
                        move(u, "t", 2 * g + 1, t_sb[u], "t_sb", ACT.Relu)
                    for u in range(2):
                        move(u, "aggt", g + 1, agg_t[u], "aggt_sb")
                    for u in range(2):
                        move(u, "h1", g + 1, h1_t[u], "h1_sb", ACT.Relu, cols_0[:, 0:1], H_BANK[u][0])
                    for u in range(2):
                        move(u, "h2", g + 1, h2_t[u], "h2_sb", ACT.Relu, cols_0[:, 1:2], H_BANK[u][1])
                    for u in range(2):
                        t = SUBS[u][1]
                        act.wait_ge(s("zr", u), F.at("zr", u, g + 1))
                        act.activation(xob[u][:, 0:t, :], z[u][:, 0:t, :], ACT.Relu).then_inc(s("xh", u), 1)
                else:
                    for u in range(2):
                        move(u, "aggt", g + 1, t_sb[u], "aggt_sb")
                    for u in range(2):
                        move(u, "t", F.norms_t * g + 1, t_sb[u], "t_sb")
                    for k in range(FF // P):
                        for u in range(2):
                            if k == 0 and F.pre is not None:
                                F.wait_last(act, "kv_out", u, 16 * g)
                            move(u, "up", (FF // P) * g + k + 1, hid[u][:, k * 512:(k + 1) * 512], "up_sb", ACT.Gelu,
                                 b_up[F.post][:, k:k + 1], H_BANK[u][k % 2])
                if F.pre is not None:
                    for u in range(2):
                        move(u, "t", F.norms_t * (g + 1), t_sb[u], "t_sb")
                    for u in range(2):
                        t = SUBS[u][1]
                        act.wait_ge(s("att", u), F.at("att", u, g + 1))
                        act.activation(node_view(agg, g, u, D, MW), att_s[u][:, 2, 0:t * HEADS].rearrange("p (t h) -> p t h", h=HEADS),
                                       ACT.Exp).then_inc(s("ex", u), 1)
            return body

        def dve_dense(dve, F):
            s, see, mark = F.s, F.see, F.mark

            def norm_pair(g, n, rows, dest, done=None, pre_wait=None):
                for u in range(2):
                    if pre_wait is not None:
                        pre_wait(u)
                    for t in range(SUBS[u][1]):
                        last = dve.bn_stats(bn[:, SUBS[u][0] + t, :], rows(u, t))
                    mark(last)
                see(dve, g)
                dve.tensor_tensor(mean, bn[:, :, 1], bn[:, :, 4], ALU.add)
                dve.tensor_tensor(gap, bn[:, :, 1], bn[:, :, 4], ALU.subtract)
                mark(dve.tensor_tensor(spread2, bn[:, :, 2], bn[:, :, 5], ALU.add))
                see(dve, g)
                dve.tensor_scalar(mean, mean, 0.5, None, ALU.mult)
                dve.tensor_tensor(gap, gap, gap, ALU.mult)
                mark(dve.tensor_scalar(spread2, spread2, 1.0 / D, EPS, ALU.mult, ALU.add))
                see(dve, g)
                dve.scalar_tensor_tensor(out=var_eps, in0=gap, scalar=0.25, in1=spread2, op0=ALU.mult, op1=ALU.add).then_inc(s("var", 0), 1)
                for u in range(2):
                    if u == 0:
                        dve.wait_ge(s("rstd", 0), F.at("rstd", 0, F.norms * g + n + 1))
                    for t in range(SUBS[u][1]):
                        last = dve.tensor_scalar(dest(u, t), rows(u, t), mean[:, SUBS[u][0] + t:SUBS[u][0] + t + 1],
                                                 rstd[:, SUBS[u][0] + t:SUBS[u][0] + t + 1], ALU.subtract, ALU.mult)
                    last.then_inc(s(done, u), 1)

            def body(g, last):
                F.begin()
                if F.kind == MLP:
                    loads = lambda u: 16 * (g + 1) + (16 if last and u == 1 else 0)
                    norm_pair(g, 0, lambda u, t: xb[u][:, t, :], lambda u, t: z[u][:, t, :], "z",
                              lambda u: dve.wait_ge(s("loaded", u), F.at("loaded", u, loads(u))))
                    for u in range(2):
                        t = SUBS[u][1]
                        dve.wait_ge(s("o", u), F.at("o", u, g + 1))
                        mark(dve.tensor_tensor(xob[u][:, 0:t, :], bank[:, O_BANK[u], 0:t * P].rearrange("p (t d) -> p t d", d=D),
                                               rows_0[:, 0:1, :].to_broadcast([P, t, D]), ALU.add))
                    see(dve, g)
                    norm_pair(g, 1, lambda u, t: xob[u][:, t, :], lambda u, t: z[u][:, t, :], "zw")
                    for u in range(2):
                        t = SUBS[u][1]
                        dve.wait_ge(s("zw", u), F.at("zw", u, g + 1))
                        mark(dve.tensor_tensor(z[u][:, 0:t, :], z[u][:, 0:t, :], rows_0[:, 1:2, :].to_broadcast([P, t, D]), ALU.mult))
                        mark(dve.tensor_tensor(xob[u][:, 0:t, :], xb[u][:, 0:t, :], rows_0[:, 2:3, :].to_broadcast([P, t, D]), ALU.add))
                    see(dve, g)
                    for u in range(2):
                        t = SUBS[u][1]
                        F.wait_last(dve, "saved", u, 16 * g)
                        dve.tensor_tensor(xo[u][:, 0:t, :], z[u][:, 0:t, :], xob[u][:, 0:t, :], ALU.add).then_inc(s("x1", u), 1)
                    norm_pair(g, 2, lambda u, t: xo[u][:, t, :], lambda u, t: z[u][:, t, :], "zr",
                              lambda u: dve.wait_ge(s("x1", u), F.at("x1", u, g + 1)))
                    for u in range(2):
                        dve.wait_ge(s("xh", u), F.at("xh", u, g + 1))
                    norm_pair(g, 3, lambda u, t: xob[u][:, t, :], lambda u, t: z[u][:, t, :], "z")
                else:
                    lp = F.post
                    for u in range(2):
                        t = SUBS[u][1]
                        mark(dve.tensor_scalar(att_s[u][:, 0, 0:t * HEADS].rearrange("p (t h) -> p t h", h=HEADS),
                                               node_view(agg, g, u, D, MW), SUM_GUARD, None, ALU.add))
                    see(dve, g)
                    for u in range(2):
                        t = SUBS[u][1]
                        mark(dve.reciprocal(att_s[u][:, 1, 0:t * HEADS], att_s[u][:, 0, 0:t * HEADS]))
                    see(dve, g)
                    for u in range(2):
                        t = SUBS[u][1]
                        dve.tensor_tensor(z[u][:, 0:t, :].rearrange("p t (h c) -> p t h c", h=HEADS),
                                          node_view(agg, g, u).rearrange("p t (h c) -> p t h c", h=HEADS),
                                          att_s[u][:, 1, 0:t * HEADS].rearrange("p (t h o) -> p t h o", h=HEADS, o=1)
                                          .to_broadcast([P, t, HEADS, HD]), ALU.mult).then_inc(s("an", u), 1)
                    for u in range(2):
                        t = SUBS[u][1]
                        dve.wait_ge(s("o", u), F.at("o", u, g + 1))
                        dve.wait_ge(s("xb", u), F.at("xb", u, g + 1))
                        if F.kind == FINAL:
                            F.wait_last(dve, "saved", u, 16 * g)
                        dve.tensor_tensor(xo[u][:, 0:t, :], bank[:, O_BANK[u], 0:t * P].rearrange("p (t d) -> p t d", d=D),
                                          xb[u][:, 0:t, :], ALU.add).then_inc(s("xo", u), 1)
                    norm_pair(g, 0, lambda u, t: xo[u][:, t, :], lambda u, t: z[u][:, t, :], "z",
                              lambda u: dve.wait_ge(s("xo", u), F.at("xo", u, g + 1)))
                    for u in range(2):
                        t = SUBS[u][1]
                        dve.wait_ge(s("down", u), F.at("down", u, g + 1))
                        dve.wait_ge(s("xob", u), F.at("xob", u, g + 1))
                        dve.tensor_tensor(xo[u][:, 0:t, :], bank[:, O_BANK[u], 0:t * P].rearrange("p (t d) -> p t d", d=D),
                                          xob[u][:, 0:t, :], ALU.add).then_inc(s("y", u), 1)
                    if F.pre is not None:
                        norm_pair(g, 1, lambda u, t: xo[u][:, t, :], lambda u, t: z[u][:, t, :], "z",
                                  lambda u: dve.wait_ge(s("y", u), F.at("y", u, g + 1)))
                if F.pre is not None:
                    l = F.pre
                    for t in range(4):
                        for u in range(2):
                            if t >= SUBS[u][1]:
                                continue
                            dve.wait_ge(s("qkv", u), F.at("qkv", u, SUBS[u][1] * g + t + 1))
                            if t == 0:
                                F.wait_last(dve, "kv_out", u, 16 * g)
                            node = g * GROUP + SUBS[u][0] + t
                            dve.scalar_tensor_tensor(out=qkv[u][:, t, :], in0=wdeg_bc[l][:, :], scalar=deg[:, bass.ds(node, 1)],
                                                     in1=bank[:, H_BANK[u][t % 2], 0:3 * D], op0=ALU.mult, op1=ALU.add
                                                     ).then_inc(s("qkv_out", u), 1)
                    for u in range(2):
                        t = SUBS[u][1]
                        dve.wait_ge(s("biased", u), F.at("biased", u, g + 1))
                        dve.wait_ge(s("t", u), F.at("t", u, F.norms_t * (g + 1)))
                        mark(dve.tensor_tensor(z[u][:, 0:t, :], qkv[u][:, 0:t, 0:D], qkv[u][:, 0:t, D:2 * D], ALU.mult))
                    see(dve, g)
                    for u in range(2):
                        t = SUBS[u][1]
                        mark(dve.tensor_reduce(att_s[u][:, 0, 0:t * HEADS],
                                               z[u][:, 0:t, :].rearrange("p t (h c) -> p (t h) c", h=HEADS), AX_X, ALU.add))
                    see(dve, g)
                    for u in range(2):
                        clip_logits(dve, F, g, u, SUBS[u][1] * HEADS)
                    for u in range(2):
                        t = SUBS[u][1]
                        dve.wait_ge(s("ex", u), F.at("ex", u, g + 1))
                        mark(dve.tensor_tensor(node_view(agg, g, u).rearrange("p t (h c) -> p t h c", h=HEADS),
                                               qkv[u][:, 0:t, 2 * D:3 * D].rearrange("p t (h c) -> p t h c", h=HEADS),
                                               node_view(agg, g, u, D, MW).unsqueeze(3).to_broadcast([P, t, HEADS, HD]), ALU.mult))
                F.end()
            return body

        def clip_logits(dve, F, g, u, n):
            a = att_s[u]
            mark, see = F.mark, F.see
            mark(dve.tensor_tensor(a[:, 1, 0:n], a[:, 0, 0:n], a[:, 0, 0:n], ALU.is_equal))
            mark(dve.tensor_scalar(a[:, 2, 0:n], a[:, 0, 0:n], -CLIP, CLIP, ALU.max, ALU.min))
            see(dve, g)
            dve.tensor_tensor(a[:, 2, 0:n], a[:, 2, 0:n], a[:, 1, 0:n], ALU.mult).then_inc(F.s("att", u), 1)

        chain_base = 0
        for F in phases:
            F.norms_t = {MLP: 2, POST: 2, FINAL: 1}[F.kind]
            F.chain_len = 4 * F.norms + (6 if F.kind == MLP else 4) + (10 if F.pre is not None else 0)
            F.chain_base = chain_base
            chain_base += GROUPS * F.chain_len

        class Attention:

            def __init__(self):
                self.kv_in = sems("kv_loaded", KV_SLOTS // QUAD)
                self.qw_in = sems("q_loaded", 2)
                self.idx = sem("idx_staged")
                self.turn = sem("gather_turn")
                self.sel = sem("sel_ready")
                self.dist = sem("dist_ready")
                self.selt = sem("selt_ready")
                self.selt_sb = sem("selt_copied")
                self.qe = sem("q_spread")
                self.prod = sem("prod_ready")
                self.att = sem("att_chain")
                self.logit = sem("logits_ready")
                self.ex = sem("exp_ready")
                self.msg = sem("msg_ready")
                self.sum = sem("summed")
                self.added = sem("added")

        Z = Attention()
        ATT_BANK = ((0, 1), (2, 3), 4)

        def run_bodies(eng, body):
            body(0, True, False)
            with eng.Fori(1, AT_BODIES - 1) as i:
                body(i, False, False)
            body(AT_BODIES - 1, False, True)

        def pool_attention(pool, l):
            k0 = l * AT_QUADS

            def body(i, first, last):
                for r in range(QUADS):
                    slot = r % (KV_SLOTS // QUAD)
                    k = i * QUADS + r
                    if not (first and r < KV_SLOTS // QUAD):
                        pool.wait_ge(Z.msg, k0 + k - KV_SLOTS // QUAD + 1)
                    if slot == 0:
                        half = r * QUAD // KV_SLOTS
                        pool.tensor_copy(idx_stage[:, half, :], at_src[:, bass.ds(i * BODY + r * QUAD, KV_SLOTS)]).then_inc(Z.idx, 1)
                        pool.wait_ge(Z.idx, (k0 // QUADS + i) * 2 + half + 1)
                    pool.sem_inc(Z.turn, 1)
                    for j in range(QUAD):
                        n = slot * QUAD + j
                        pool.indirect_dma_start(kv[:, n, :], None, kv_dram[l], bass.IndirectOffsetOnAxis(idx_stage[:, half, n:n + 1], 0)
                                                ).then_inc(Z.kv_in[slot], 16)
            run_bodies(pool, body)

        def sp_attention(sp, l):
            k0 = l * AT_QUADS
            def body(i, first, last):
                for r in range(QUADS):
                    k = i * QUADS + r
                    _, tiles = nc.values_load_multi_w_load_instructions(
                        at_nt[0:1, bass.ds(i * BODY + r * QUAD, QUAD)], engines=(ENGINE.SP,), min_val=0, max_val=NT - 1, skip_runtime_bounds_check_because=CLAMPED)
                    if not (first and r < 2):
                        sp.wait_ge(Z.qe, k0 + k - 1)
                    for j in range(QUAD):
                        sp.dma_start(q_win[:, r % 2, j, :], q_all[:, bass.ds(tiles[j], 1), :].rearrange("p t d -> p (t d)")
                                     ).then_inc(Z.qw_in[r % 2], 16)
            run_bodies(sp, body)

        def act_attention(act, l):
            k0 = l * AT_QUADS
            def select(k, r, step, first):
                if not first:
                    act.wait_ge(Z.sel, (k0 + k))
                for j in range(QUAD):
                    m = act.activation(dist[:, j, :], iota_n[:, :], ACT.Abs, bias=at_negdst[:, bass.ds(step + j, 1)])
                m.then_inc(Z.dist, 1)
                act.wait_ge(Z.dist, k0 + k + 1)
                if not (isinstance(k, int) and k < QUADS):
                    act.wait_ge(Z.sum, (k0 + k - QUADS + 1) * QUAD)
                act.activation(sel[:, r % QUADS, :, :], dist, ACT.Relu, scale=-1.0, bias=1.0).then_inc(Z.sel, 1)

            def copy_t(k, r):
                act.wait_ge(Z.selt, k0 + k + 1)
                if not (isinstance(k, int) and k < 2):
                    act.wait_ge(Z.qe, k0 + k - 1)
                act.activation(sel_t[:, r % 2, :, :], bank[:, ATT_BANK[0][r % 2], :].rearrange("p (j e) -> p j e", j=QUAD),
                               ACT.Copy).then_inc(Z.selt_sb, 1)

            def body(i, first, last):
                for r in range(QUADS):
                    k = i * QUADS + r
                    if not (last and r + 2 >= QUADS):
                        copy_t(k + 2, r + 2)
                    if not (last and r + 3 >= QUADS):
                        select(k + 3, r + 3, (i * QUADS + r + 3) * QUAD, False)
                    act.wait_ge(Z.logit, k0 + k + 1)
                    act.activation(msg[:, r % 2, :, D:MW], att[:, r % 2, 2, :].rearrange("p (j h) -> p j h", j=QUAD),
                                   ACT.Exp).then_inc(Z.ex, 1)
            select(0, 0, 0, True)
            copy_t(0, 0)
            select(1, 1, QUAD, False)
            copy_t(1, 1)
            select(2, 2, 2 * QUAD, False)
            run_bodies(act, body)

        def pe_attention(pe, l):
            k0 = l * AT_QUADS
            def transposes(k, r):
                pe.wait_ge(Z.sel, k0 + k + 1)
                if not (isinstance(k, int) and k < 2):
                    pe.wait_ge(Z.selt_sb, k0 + k - 1)
                for j in range(QUAD):
                    m = pe.transpose(bank[:, ATT_BANK[0][r % 2], j * P:(j + 1) * P], sel[:, r % QUADS, j, :], ident[:, :])
                m.then_inc(Z.selt, 1)

            def spread(k, r, i):
                pe.wait_ge(Z.selt_sb, k0 + k + 1)
                pe.wait_ge(Z.qw_in[r % 2], 16 * QUAD * (k0 // 2 + i * (QUADS // 2) + r // 2 + 1))
                if not (isinstance(k, int) and k < 2):
                    pe.wait_ge(Z.prod, k0 + k - 1)
                for j in range(QUAD):
                    m = pe.matmul(bank[:, ATT_BANK[1][r % 2], j * D:(j + 1) * D], sel_t[:, r % 2, j, :], q_win[:, r % 2, j, :],
                                  start=True, stop=True)
                m.then_inc(Z.qe, 1)

            def sums(k, r):
                pe.wait_ge(Z.msg, k0 + k + 1)
                for j in range(QUAD):
                    if not (isinstance(k, int) and k < 1):
                        pe.wait_ge(Z.added, (k0 + k - 1) * QUAD + j + 1)
                    pe.matmul(bank[:, ATT_BANK[2] + j, 0:MW], sel[:, r % QUADS, j, :], msg[:, r % 2, j, :],
                              start=True, stop=True).then_inc(Z.sum, 1)

            def body(i, first, last):
                for r in range(QUADS):
                    k = i * QUADS + r
                    if not (last and r + 2 >= QUADS):
                        spread(k + 2, r + 2, i)
                    if not (first and r == 0):
                        sums(k - 1, (r - 1) % QUADS)
                    if not (last and r + 3 >= QUADS):
                        transposes(k + 3, r + 3)
            transposes(0, 0)
            spread(0, 0, 0)
            transposes(1, 1)
            spread(1, 1, 0)
            transposes(2, 2)
            run_bodies(pe, body)
            sums(AT_QUADS - 1, QUADS - 1)

        def dve_attention(dve, l):
            k0 = l * AT_QUADS
            HALF = QUADS // 2

            def load_tiles(step, n):
                _, tiles = nc.values_load_multi_w_load_instructions(
                    at_nt[0:1, bass.ds(step, n)], engines=(ENGINE.DVE,), min_val=0, max_val=NT - 1, skip_runtime_bounds_check_because=CLAMPED)
                return tiles

            def add(k, j, tile):
                dve.wait_ge(Z.sum, (k0 + k) * QUAD + j + 1)
                if not (isinstance(k, int) and k * QUAD + j == 0):
                    dve.wait_ge(Z.added, (k0 + k) * QUAD + j)
                a = agg[:, bass.ds(tile, 1), :].rearrange("p t c -> p (t c)")
                dve.tensor_tensor(a, bank[:, ATT_BANK[2] + j, 0:MW], a, ALU.add).then_inc(Z.added, 1)

            def weigh(k, r):
                dve.wait_ge(Z.ex, k0 + k + 1)
                if not (isinstance(k, int) and k < 2):
                    dve.wait_ge(Z.sum, (k0 + k - 1) * QUAD)
                s = r * QUAD % KV_SLOTS
                dve.tensor_tensor(msg[:, r % 2, :, 0:D].rearrange("p j (h c) -> p j h c", h=HEADS),
                                  kv[:, s:s + QUAD, D:2 * D].rearrange("p j (h c) -> p j h c", h=HEADS),
                                  msg[:, r % 2, :, D:MW].unsqueeze(3).to_broadcast([P, QUAD, HEADS, HD]), ALU.mult).then_inc(Z.msg, 1)

            def body(i, first, last):
                for r in range(QUADS):
                    k = i * QUADS + r
                    a = att[:, r % 2, :, :]
                    s = r * QUAD % KV_SLOTS
                    dve.wait_ge(Z.qe, k0 + k + 1)
                    dve.wait_ge(Z.kv_in[s // QUAD], 16 * QUAD * (k0 * QUAD // KV_SLOTS + i * (QUADS * QUAD // KV_SLOTS) + r * QUAD // KV_SLOTS + 1))
                    dve.tensor_tensor(prod[:, r % 2, :, :], bank[:, ATT_BANK[1][r % 2], :].rearrange("p (j d) -> p j d", j=QUAD),
                                      kv[:, s:s + QUAD, 0:D], ALU.mult).then_inc(Z.prod, 1)
                    behind = 0 if first and r < HALF else 2
                    if r % HALF == 0:
                        tiles = load_tiles((k - behind) * QUAD, (HALF - 2 + behind) * QUAD)

                    def join(j):
                        if not (first and r < 2):
                            add(k - 2, j, tiles[(r % HALF - 2 + behind) * QUAD + j])
                    join(0)
                    dve.wait_ge(Z.prod, k0 + k + 1)
                    dve.tensor_reduce(a[:, 0, :], prod[:, r % 2, :, :].rearrange("p j (h c) -> p (j h) c", h=HEADS), AX_X,
                                      ALU.add).then_inc(Z.att, 1)
                    join(1)
                    if not (first and r == 0):
                        weigh(k - 1, (r - 1) % QUADS)
                    dve.wait_ge(Z.att, 3 * (k0 + k) + 1)
                    dve.tensor_tensor(a[:, 1, :], a[:, 0, :], a[:, 0, :], ALU.is_equal).then_inc(Z.att, 1)
                    join(2)
                    dve.tensor_scalar(a[:, 2, :], a[:, 0, :], -CLIP, CLIP, ALU.max, ALU.min).then_inc(Z.att, 1)
                    join(3)
                    dve.wait_ge(Z.att, 3 * (k0 + k) + 3)
                    dve.tensor_tensor(a[:, 2, :], a[:, 2, :], a[:, 1, :], ALU.mult).then_inc(Z.logit, 1)
            run_bodies(dve, body)
            weigh(AT_QUADS - 1, QUADS - 1)
            tiles = load_tiles(AT_STEPS - 2 * QUAD, 2 * QUAD)
            for n, tile in enumerate(tiles):
                add(AT_QUADS - 2 + n // QUAD, n % QUAD, tile)

        def dense_done(eng, F):
            for u in range(2):
                eng.wait_ge(F.s("q_out", u), F.at("q_out", u, GROUPS))
                eng.wait_ge(F.s("kv_out", u), F.at("kv_out", u, 16 * GROUPS))
            eng.wait_ge(dense_chain, F.chain_base + GROUPS * F.chain_len)

        def attention_done(eng, l):
            eng.wait_ge(Z.added, (l + 1) * AT_STEPS)

        @block.vector
        def _(dve):
            dve_prepare(dve)
            dve_edge_sums(dve)
            dve.wait_ge(s_w0, 16 * W0_LOADS)
            for l in range(LAYERS):
                run_groups(dve, dve_dense(dve, phases[l]))
                if l == 0:
                    dve.wait_ge(s_nt_in["at"], 16)
                dense_done(dve, phases[l])
                dve_attention(dve, l)
                attention_done(dve, l)
            run_groups(dve, dve_dense(dve, phases[LAYERS]))

        @block.sync
        def _(sp):
            sp_prepare(sp)
            sp_tables(sp)
            sp_edge_sums(sp)
            sp.wait_ge(es_added, ES_BODIES * ES_SLOTS)
            for l in range(LAYERS):
                run_groups(sp, sp_dense(sp, phases[l]))
                if l == 0:
                    sp.wait_ge(s_nt_in["at"], 16)
                    for u in range(2):
                        sp.wait_ge(phases[0].s("saved", u), 16 * GROUPS)
                dense_done(sp, phases[l])
                sp_attention(sp, l)
                attention_done(sp, l)
            run_groups(sp, sp_dense(sp, phases[LAYERS]))
            for u in range(2):
                sp.wait_ge(phases[LAYERS].s("saved", u), phases[LAYERS].at("saved", u, 16 * (GROUPS + u)))

        @block.scalar
        def _(act):
            act_load_weights(act)
            act.wait_ge(s_w0, 16 * W0_LOADS)
            act.wait_ge(es_added, ES_BODIES * ES_SLOTS)
            for l in range(LAYERS):
                run_groups(act, act_dense(act, phases[l]))
                dense_done(act, phases[l])
                act_attention(act, l)
                attention_done(act, l)
            run_groups(act, act_dense(act, phases[LAYERS]))

        @block.gpsimd
        def _(pool):
            pool_prepare(pool)
            pool_gather_rows(pool)
            pool_degree(pool)
            pool.wait_ge(es_added, ES_BODIES * ES_SLOTS)
            for l in range(LAYERS):
                run_groups(pool, pool_dense(pool, phases[l]))
                dense_done(pool, phases[l])
                pool_attention(pool, l)
                attention_done(pool, l)
            run_groups(pool, pool_dense(pool, phases[LAYERS]))

        @block.tensor
        def _(pe):
            pe_prepare(pe)
            pe_edge_sums(pe)
            pe.wait_ge(s_w0, 16 * W0_LOADS)
            for l in range(LAYERS):
                run_groups(pe, pe_dense(pe, phases[l]))
                dense_done(pe, phases[l])
                pe_attention(pe, l)
                attention_done(pe, l)
            run_groups(pe, pe_dense(pe, phases[LAYERS]))


_INS = ["x", "src", "dst", "edge_attr_128"] + [f"L0_gnn_{k}" for k in ("W1", "b1", "W2", "b2", "W3", "b3", "ln_w", "ln_b")] + [
    f"L1_gnn_{k}" for k in ("Wq", "bq", "Wk", "bk", "Wv", "bv", "Wo", "bo", "Wpos", "bpos", "Wdeg", "bdeg", "ln1_g", "ln1_b",
                            "ln2_g", "ln2_b", "W1", "b1", "W2", "b2")]


def kernel(**inputs):
    import numpy as _np
    import concourse.bacc as _bacc
    from concourse.bass_utils import run_bass_kernel_spmd as _run

    nc = _bacc.Bacc("TRN2", target_bir_lowering=False, num_devices=1)
    arrays, args = {}, {}
    for name in _INS:
        a = _np.ascontiguousarray(inputs[name])
        arrays[f"in_{name}_dram"] = a
        args[name] = nc.dram_tensor(f"in_{name}_dram", a.shape, mybir.dt.from_np(a.dtype), kind="ExternalInput").ap()
    out = nc.dram_tensor("out_0_dram", (N, D), F32, kind="ExternalOutput").ap()
    gnn_kernel(nc, args, out)
    r = _run(nc, [arrays], core_ids=[0])
    return r.results[0]["out_0_dram"]
```

```python
from contextlib import ExitStack

import concourse.bass as bass
from concourse import mybir

ALU = mybir.AluOpType
ACT = mybir.ActivationFunctionType
AX_X = mybir.AxisListType.X
F32 = mybir.dt.float32
BF16 = mybir.dt.bfloat16
I32 = mybir.dt.int32
ENGINE = mybir.EngineType

P = 128
N, E, D = 6250, 100000, 128
HEADS, HD, LAYERS, FF = 8, 16, 2, 512
MW = D + HEADS
EPS = 1e-5
CLIP = 50.0
SUM_GUARD = 1e-16 * 1.9287498e-22
NT = -(-N // P)
NPAD = NT * P
LAST_ROWS = N - (NT - 1) * P
CLAMPED = "the step tables are clamped to this range where they are built"
SHIFT = 7

AT_EDGES = 128
AT_TILES = -(-E // AT_EDGES)
QUAD, QUADS = 4, 8
BODY = QUAD * QUADS
AT_BODIES = -(-(AT_TILES + NT - 1) // BODY)
AT_STEPS = AT_BODIES * BODY
AT_QUADS = AT_BODIES * QUADS
KV_SLOTS = BODY // 2
ARENA = 18432
ES_SUB = 4
ES_EDGES = P * ES_SUB
ES_TILES = -(-E // ES_EDGES)
ES_SLOTS = 4
ES_BODIES = -(-(ES_TILES + NT - 1) // (2 * ES_SLOTS))
ES_ROUNDS = 2 * ES_BODIES
ES_STEPS = ES_ROUNDS * ES_SLOTS
DVE_SLOTS = 2
ACT_SLOTS = ES_SLOTS - DVE_SLOTS
HIST_ROWS = 125
HIST_COLS = E // HIST_ROWS
HIST_ROUND = -(-HIST_COLS // ES_ROUNDS)
HIST_PAD = HIST_ROUND * ES_ROUNDS

UNIT, BUFS = 4, 4
UNITS = -(-NT // UNIT)
assert UNIT * P <= 512 and NT == (UNITS - 1) * UNIT + 1


class Table:

    def __init__(self, no, name, edges, tiles, steps, src):
        self.no, self.name, self.edges, self.tiles = no, name, edges, tiles
        self.chunks = -(-tiles // P)
        self.step_chunks = -(-steps // P)
        self.rows, self.steps = self.chunks * P, self.step_chunks * P
        self.last_start = E - edges
        self.repeated = tiles * edges - E
        self.src = src
        self.width = edges * (2 if src else 1) + 1


def gnn_kernel(nc, A, out):
    x, src, dst, edge_attr = A["x"], A["src"], A["dst"], A["edge_attr_128"]
    ES = Table(0, "es", ES_EDGES, ES_TILES, ES_STEPS, False)
    AT = Table(1, "at", AT_EDGES, AT_TILES, AT_STEPS, True)
    TABLES = (ES, AT)

    ctx = ExitStack()
    with ctx:
        ctx.enter_context(nc.allow_non_contiguous_dma(reason="columns of indices and of small parameters"))

        def sb(name, shape, dt=F32):
            return ctx.enter_context(nc.sbuf_tensor(name, shape, dt))

        def sem(name):
            return ctx.enter_context(nc.semaphore(name))

        def sems(name, n):
            return [sem(f"{name}{i}") for i in range(n)]

        def dram(name, shape, dt=F32):
            return nc.dram_tensor(name, shape, dt).ap()

        kv_dram = [dram(f"kv_rows{l}", [NPAD, 2 * D]) for l in range(LAYERS)]
        x1_dram = dram("x1_rows", [NPAD, D])
        for T in TABLES:
            T.rows_dram = dram(f"{T.name}_rows", [T.rows, T.width], I32)
            T.nt_dram = dram(f"{T.name}_node_tile", [T.steps], I32)
        es_start_dram = dram("es_first_edge", [ES.steps], I32)

        xcur = sb("x_stream", [P, NT, D])
        q_all = sb("queries", [P, NT, D])
        agg = sb("aggregate", [P, NT, MW])
        iota_n = sb("iota_n", [P, P])
        ident = sb("ident", [P, P])
        hist_iota = sb("hist_iota", [P, P, HIST_ROUND], BF16)
        src_lo = sb("src_lo", [HIST_ROWS, HIST_PAD], BF16)
        src_hi = sb("src_hi", [HIST_ROWS, HIST_PAD], BF16)
        deg = sb("degree", [P, NT])
        node_mask = sb("node_mask", [P, NT])
        deg_tmp = sb("degree_parts", [P, NT])
        stat = sb("degree_stats", [P, 8])
        half_neg = sb("minus_half", [P, UNIT])
        ones_f = sb("ones_f", [P, P])
        at_negdst = sb("at_negdst", [P, AT.steps])
        at_src = sb("at_src", [P, AT.steps], I32)
        es_dst = sb("es_dst", [P, ES.steps, ES_SUB])
        es_start = sb("es_start", [1, ES.steps], I32)
        es_nt = sb("es_nt", [1, ES.steps], I32)
        at_nt = sb("at_nt", [1, AT.steps], I32)
        idx_stage = sb("idx_stage", [P, 2, KV_SLOTS], I32)
        w1_0 = sb("w1_0", [P, 2, D])
        w2_0 = sb("w2_0", [P, D])
        w3_0 = sb("w3_0", [P, D])
        cols_0 = sb("cols_0", [P, 2])
        rows_0 = sb("rows_0", [P, 3, D])
        w_qkv = [sb(f"w_qkv{l}", [P, 3 * D]) for l in range(LAYERS)]
        wdeg_bc = [sb(f"wdeg_bc{l}", [P, 3 * D]) for l in range(LAYERS)]
        bias_rows = [sb(f"bias_rows{l}", [3, 3 * D], BF16) for l in range(LAYERS)]
        ones_3 = sb("ones_3", [3, P], BF16)
        w_o = [sb(f"w_o{l}", [P, D]) for l in range(LAYERS)]
        w_up = [sb(f"w_up{l}", [P, FF]) for l in range(LAYERS)]
        w_down = [sb(f"w_down{l}", [P, FF // P, D]) for l in range(LAYERS)]
        b_up = [sb(f"b_up{l}", [P, FF // P]) for l in range(LAYERS)]
        rows_l = [sb(f"rows_l{l}", [P, 2, D]) for l in range(LAYERS)]
        bn = [sb(f"bn{b}", [P, UNIT, 6]) for b in range(BUFS)]
        norm_stat = [sb(f"norm_stat{b}", [P, 6, UNIT]) for b in range(BUFS)]
        att_s = [sb(f"att_self{b}", [P, 3, UNIT * HEADS]) for b in range(BUFS)]
        arena = sb("arena", [P, ARENA])
        bank = ctx.enter_context(nc.psum_tensor("bank", [P, 8, 512], F32))

        class Area:

            def __init__(self, *regions):
                self.regions, self.at = list(regions), 0

            def take(self, words):
                while self.at + words > self.regions[0].shape[1]:
                    self.regions.pop(0)
                    self.at = 0
                v = self.regions[0][:, self.at:self.at + words]
                self.at += words
                return v

        area = Area(arena[:, :], xcur[:, :, :].rearrange("p t d -> p (t d)"), q_all[:, :, :].rearrange("p t d -> p (t d)"))
        for T in TABLES:
            T.first = area.take(T.chunks).bitcast(I32)
            T.last = area.take(T.chunks).bitcast(I32)
            T.ones_steps = area.take(T.chunks).bitcast(BF16).rearrange("p (c w) -> p c w", w=2)
            T.incl = area.take(T.chunks)
            T.done = area.take(T.chunks * T.steps // 2).bitcast(BF16).rearrange("p (c s) -> p c s", c=T.chunks)
            T.tile_i = area.take(T.step_chunks).bitcast(I32)
            T.start_i = area.take(T.step_chunks).bitcast(I32)
            T.off = area.take(T.step_chunks)
            T.step_id = area.take(T.step_chunks)
            T.ftile = area.take(T.step_chunks)
            T.ftile_i = area.take(T.step_chunks).bitcast(I32)
            T.nt_i = area.take(T.step_chunks).bitcast(I32)
            T.nt_nodes = area.take(T.step_chunks)
            T.step_rows = area.take(T.step_chunks * T.width).bitcast(I32).rearrange("p (k w) -> p k w", w=T.width)
            T.rel = area.take(T.step_chunks * T.edges).rearrange("p (k e) -> p k e", e=T.edges)
        src_f = area.take(AT.steps).rearrange("p (k e) -> p k e", e=P)
        iota_s = area.take(AT.steps)
        iota_i = area.take(AT.steps).bitcast(I32)
        step_id_i = area.take(AT.step_chunks).bitcast(I32)
        node_id_i = area.take(NT).bitcast(I32)
        neg1 = area.take(P).bitcast(I32)
        zero_i = area.take(2 * P).bitcast(I32)
        tri = area.take(P // 2).bitcast(BF16)
        ones_b = area.take(P // 2).bitcast(BF16)
        src_i = area.take(2 * HIST_PAD)[0:HIST_ROWS, :].bitcast(I32).rearrange("p (a c) -> p a c", a=2)
        raw_qkv = [area.take(3 * D) for _ in range(LAYERS)]
        raw_pos = [area.take(D) for _ in range(LAYERS)]
        pos_t = [area.take(D) for _ in range(LAYERS)]
        raw_a = [area.take(3 * D) for _ in range(LAYERS)]
        bqkv_row = [area.take(3 * D)[0:1, :] for _ in range(LAYERS)]
        bias_rest = [area.take(3 * D)[0:3, :] for _ in range(LAYERS)]
        bias_parts = [area.take(9 * D // 2).bitcast(BF16)[0:3, :].rearrange("p (i c) -> p i c", i=3) for _ in range(LAYERS)]
        cols_l = [area.take(7 + FF // P) for _ in range(LAYERS)]
        bc_l = [area.take(3 * P).rearrange("p (i n) -> p i n", i=3) for _ in range(LAYERS)]

        area = Area(arena[:, :])
        es_attr = area.take(2 * ES_SLOTS * ES_SUB * D).rearrange("p (h s j d) -> p h s j d", h=2, s=ES_SLOTS, j=ES_SUB)
        es_sel = area.take(2 * ES_SLOTS * ES_SUB * P).rearrange("p (h s j n) -> p h s j n", h=2, s=ES_SLOTS, j=ES_SUB)
        es_dist = area.take(ACT_SLOTS * ES_SUB * P).rearrange("p (s j n) -> p s j n", s=ACT_SLOTS, j=ES_SUB)
        oh_lo, oh_hi = [[area.take(-(-n * HIST_ROUND // 2))[0:HIST_ROWS, :].bitcast(BF16)[:, 0:n * HIST_ROUND]
                         .rearrange("p (n c) -> p n c", c=HIST_ROUND) for h in range(2)] for n in (P, NT)]

        area = Area(arena[:, :])
        kv = area.take(KV_SLOTS * 2 * D).rearrange("p (s c) -> p s c", s=KV_SLOTS)
        sel = area.take(QUADS * QUAD * P).rearrange("p (k j n) -> p k j n", k=QUADS, j=QUAD)
        dist = area.take(QUAD * P).rearrange("p (j n) -> p j n", j=QUAD)
        sel_t = area.take(2 * QUAD * P).rearrange("p (k j e) -> p k j e", k=2, j=QUAD)
        q_win = area.take(2 * QUAD * D).rearrange("p (k j d) -> p k j d", k=2, j=QUAD)
        prod = area.take(2 * QUAD * D).rearrange("p (k j d) -> p k j d", k=2, j=QUAD)
        msg = area.take(2 * QUAD * MW).rearrange("p (k j c) -> p k j c", k=2, j=QUAD)
        att = area.take(2 * 3 * QUAD * HEADS).rearrange("p (k i c) -> p k i c", k=2, i=3)

        area = Area(arena[:, :])
        z, t_sb, xo, xob, xb, hid = [], [], [], [], [], []
        for b in range(BUFS):
            z.append(area.take(4 * D).rearrange("p (t d) -> p t d", t=4))
            t_sb.append(area.take(4 * P))
            xo.append(area.take(4 * D).rearrange("p (t d) -> p t d", t=4))
            xob.append(area.take(4 * D).rearrange("p (t d) -> p t d", t=4))
            xb.append(area.take(4 * D).rearrange("p (t d) -> p t d", t=4))
            hid.append(area.take(FF // P * 4 * P))
        h1_t = [hid[b][:, 0:512] for b in range(BUFS)]
        h2_t = [hid[b][:, 512:1024] for b in range(BUFS)]
        agg_t = [hid[b][:, 1024:1536] for b in range(BUFS)]
        agg_s = [hid[b][:, 1536:2048].rearrange("p (t d) -> p t d", t=UNIT) for b in range(BUFS)]
        qkv = [hid[b][:, 0:UNIT * 3 * D].rearrange("p (t c) -> p t c", t=UNIT) for b in range(BUFS)]

        def stat_rows(u):
            return [norm_stat[u.b][:, i, 0:u.t] for i in range(6)]

        s_const = sem("const_ready")
        s_iota = sem("iota_ready")
        s_ends_zero = sem("ends_zeroed")
        s_ends = {T.name: sem(f"{T.name}_ends_loaded") for T in TABLES}
        s_rows = {T.name: sem(f"{T.name}_rows_written") for T in TABLES}
        s_src = sem("src_loaded")
        s_w0 = sem("w0_loaded")
        s_wl = sem("wl_loaded")
        s_dve = sem("dve_chain")
        s_steps = sem("steps_counted")
        s_incl = sem("steps_summed")
        s_done = sem("done_marked")
        s_tile = sem("tile_summed")
        s_tile_i = sem("tile_ready")
        s_got = {T.name: sem(f"{T.name}_rows_gathered") for T in TABLES}
        s_rel = sem("rel_ready")
        s_relt = sem("rel_transposed")
        s_tab = sem("table_ready")
        s_nt_out = {T.name: sem(f"{T.name}_nt_written") for T in TABLES}
        s_nt_in = {T.name: sem(f"{T.name}_nt_loaded") for T in TABLES}
        s_wprep = sem("weights_mixed")
        s_wmm = sem("weight_products")
        s_identity = sem("identity_ready")

        es_in = sems("es_attr_loaded", 2 * ES_SLOTS)
        es_sel_dve = sem("es_sel_ready_dve")
        es_sel_act = sem("es_sel_ready_act")
        es_dist_ready = sem("es_dist_ready")
        es_summed = sem("es_summed")
        es_added = sem("es_added")
        hist_oh = sem("hist_onehots_ready")
        hist_mm = sem("hist_counted")
        s_degmm = sem("degree_summed")
        s_degdve = sem("degree_parts_ready")
        s_degpow = sem("degree_std_ready")

        block = ctx.enter_context(nc.Block())

        def column(a):
            return a.rearrange("(p o) -> p o", o=1)

        n_ends = {"es": 0, "at": 0}
        n_rows = {"es": 0, "at": 0}
        W0_LOADS = 3 + 2 + 3
        WL_LOADS = LAYERS * (3 + 1 + 1 + 1 + 1 + 3 + 7 + 1 + 2)

        def sp_prepare(sp):
            sp.wait_ge(s_ends_zero, 1)
            for T in TABLES:
                e, full, tail = T.edges, (T.chunks - 1) * P, T.tiles - (T.chunks - 1) * P
                tiled = dst[0:(T.tiles - 1) * e].rearrange("(t e) -> t e", e=e)
                parts = []
                for c in range(T.chunks - 1):
                    parts += [(T.first[:, c:c + 1], tiled[c * P:(c + 1) * P, 0:1]),
                              (T.last[:, c:c + 1], tiled[c * P:(c + 1) * P, e - 1:e])]
                c = T.chunks - 1
                parts += [(T.first[0:tail - 1, c:c + 1], tiled[full:, 0:1]),
                          (T.last[0:tail - 1, c:c + 1], tiled[full:, e - 1:e]),
                          (T.first[tail - 1:tail, c:c + 1], column(dst[(T.tiles - 1) * e:(T.tiles - 1) * e + 1])),
                          (T.last[tail - 1:tail, c:c + 1], column(dst[E - 1:E]))]
                for o, i in parts:
                    sp.dma_start(o, i).then_inc(s_ends[T.name], 16)
                n_ends[T.name] = 16 * len(parts)
            sp.wait_ge(s_const, 1)
            for T in TABLES:
                e, last = T.edges, T.tiles - 1
                r = T.rows_dram
                parts = [(r[0:last, 0:e], dst[0:last * e].rearrange("(t e) -> t e", e=e)),
                         (r[last:last + 1, T.repeated:e], dst[last * e:E].rearrange("(o e) -> o e", o=1)),
                         (r[0:last, T.width - 1:T.width], dst[0:last * e].rearrange("(t e) -> t e", e=e)[:, 0:1]),
                         (r[last:last + 1, T.width - 1:T.width], column(dst[last * e:last * e + 1])),
                         (r[T.tiles:T.rows, T.width - 1:T.width], zero_i[0:T.rows - T.tiles, 0:1])]
                for a in range(0, T.repeated, P):
                    w = min(P, T.repeated - a)
                    parts.append((r[last:last + 1, a:a + w], neg1[0:1, 0:w]))
                for a in range(0, e, P):
                    parts.append((r[T.tiles:T.rows, a:a + P], neg1[0:T.rows - T.tiles, :]))
                if T.src:
                    parts += [(r[0:last, e:2 * e], src[0:last * e].rearrange("(t e) -> t e", e=e)),
                              (r[last:last + 1, e:2 * e], src[T.last_start:E].rearrange("(o e) -> o e", o=1)),
                              (r[T.tiles:T.rows, e:2 * e], zero_i[0:T.rows - T.tiles, 0:e])]
                for o, i in parts:
                    sp.dma_start(o, i).then_inc(s_rows[T.name], 16)
                n_rows[T.name] = 16 * len(parts)

        def sp_tables(sp):
            for T in TABLES:
                sp.wait_ge(s_rel, T.no + 1)
                sp.dma_start(T.nt_dram.rearrange("(k p) -> p k", p=P), T.nt_i).then_inc(s_nt_out[T.name], 16)
                n = 16
                if T is ES:
                    sp.dma_start(es_start_dram.rearrange("(k p) -> p k", p=P), T.start_i).then_inc(s_nt_out[T.name], 16)
                    n = 32
                sp.wait_ge(s_nt_out[T.name], n)
                sp.dma_start((es_nt if T is ES else at_nt)[:, :],
                             T.nt_dram.rearrange("(o s) -> o s", o=1)).then_inc(s_nt_in[T.name], 16)
                if T is ES:
                    sp.dma_start(es_start[:, :], es_start_dram.rearrange("(o s) -> o s", o=1)).then_inc(s_nt_in[T.name], 16)

        def act_load_weights(act):
            act.wait_ge(s_ends_zero, 1)
            act.dma_start(src_i[:, 0, 0:HIST_COLS], src.rearrange("(p c) -> p c", p=HIST_ROWS)).then_inc(s_src, 16)
            for o, i in ((w1_0[:, :, :], A["L0_gnn_W1"].rearrange("(k p) n -> p k n", p=P)),
                         (w2_0[:, :], A["L0_gnn_W2"]), (w3_0[:, :], A["L0_gnn_W3"]),
                         (cols_0[:, 0:1], column(A["L0_gnn_b1"])), (cols_0[:, 1:2], column(A["L0_gnn_b2"])),
                         (rows_0[:, 0, :], A["L0_gnn_b3"].partition_broadcast(P)),
                         (rows_0[:, 1, :], A["L0_gnn_ln_w"].partition_broadcast(P)),
                         (rows_0[:, 2, :], A["L0_gnn_ln_b"].partition_broadcast(P))):
                act.dma_start(o, i).then_inc(s_w0, 16)
            for l in range(LAYERS):
                w = {k[len("L1_gnn_"):]: v[l] for k, v in A.items() if k.startswith("L1_gnn_")}
                loads = [(raw_qkv[l][:, i * D:(i + 1) * D], w[k]) for i, k in enumerate(("Wq", "Wk", "Wv"))]
                loads += [(raw_pos[l], w["Wpos"]), (w_o[l][:, :], w["Wo"]), (w_up[l][:, :], w["W1"]),
                          (w_down[l][:, :, :], w["W2"].rearrange("(k p) n -> p k n", p=P))]
                loads += [(bqkv_row[l][:, i * D:(i + 1) * D], w[k].rearrange("(o d) -> o d", o=1))
                          for i, k in enumerate(("bq", "bk", "bv"))]
                cols = [w["ln1_g"], w["ln1_b"], w["bpos"], w["bdeg"], w["Wdeg"].rearrange("o d -> (o d)"), w["ln2_g"], w["ln2_b"]]
                loads += [(cols_l[l][:, i:i + 1], column(c)) for i, c in enumerate(cols)]
                loads += [(cols_l[l][:, 7:7 + FF // P], w["b1"].rearrange("(k p) -> p k", p=P)),
                          (rows_l[l][:, 0, :], w["bo"].partition_broadcast(P)),
                          (rows_l[l][:, 1, :], w["b2"].partition_broadcast(P))]
                for o, i in loads:
                    act.dma_start(o, i).then_inc(s_wl, 16)

        def pool_prepare(pool):
            pool.memset(neg1, -1)
            pool.memset(zero_i, 0)
            pool.memset(ones_b, 1.0)
            pool.memset(ones_3[:, :], 1.0)
            pool.memset(tri, 1.0)
            pool.memset(ones_f[:, :], 1.0)
            pool.memset(ident[:, :], 1.0)
            pool.memset(half_neg[:, :], -0.5).then_inc(s_const, 1)
            pool.iota(iota_i, [[1, AT.steps]], base=0, channel_multiplier=0)
            pool.iota(step_id_i, [[P, AT.step_chunks]], base=0, channel_multiplier=1)
            pool.iota(node_id_i, [[P, NT]], base=0, channel_multiplier=1).then_inc(s_iota, 1)
            pool.wait_ge(s_const, 1)
            pool.affine_select(out=tri, in_=tri, pattern=[[1, P]], compare_op=ALU.is_ge, fill=0.0, base=0, channel_multiplier=-1)
            pool.affine_select(out=ident[:, :], in_=ident[:, :], pattern=[[1, P]], compare_op=ALU.is_equal, fill=0.0, base=0,
                               channel_multiplier=-1).then_inc(s_identity, 1)

        def pool_gather_rows(pool):
            for T in TABLES:
                pool.wait_ge(s_rows[T.name], n_rows[T.name])
                pool.wait_ge(s_tile_i, T.no + 1)
                for k in range(T.step_chunks):
                    pool.indirect_dma_start(T.step_rows[:, k, :], None, T.rows_dram,
                                            bass.IndirectOffsetOnAxis(T.tile_i[:, k:k + 1], 0)).then_inc(s_got[T.name], 16)

        chain = [0]

        def link(dve, ins):
            chain[0] += 1
            ins.then_inc(s_dve, 1)
            dve.wait_ge(s_dve, chain[0])

        def dve_prepare(dve):
            for T in TABLES:
                dve.memset(T.first, 0)
                dve.memset(T.last, 0)
            dve.memset(src_i, -1).then_inc(s_ends_zero, 1)
            for T in TABLES:
                dve.memset(T.ones_steps, 1.0)
            link(dve, dve.memset(agg[:, :, :], 0.0))
            dve.wait_ge(s_iota, 1)
            dve.tensor_copy(iota_s, iota_i)
            dve.tensor_copy(iota_n[:, :], iota_i[:, 0:P])
            for T in TABLES:
                dve.tensor_copy(T.step_id, step_id_i[:, 0:T.step_chunks])
            dve.tensor_scalar(node_mask[:, :], node_id_i, float(N), None, ALU.is_lt)
            link(dve, dve.tensor_copy(hist_iota[:, :, :], iota_i[:, 0:P].unsqueeze(2).to_broadcast([P, P, HIST_ROUND])))
            for T in TABLES:
                dve.wait_ge(s_ends[T.name], n_ends_total(T))
                dve.tensor_scalar(T.first, T.first, SHIFT, None, ALU.arith_shift_right)
                link(dve, dve.tensor_scalar(T.last, T.last, SHIFT, None, ALU.arith_shift_right))
                dve.scalar_tensor_tensor(out=T.ones_steps[:, :, 1], in0=T.last, scalar=1.0, in1=T.first, op0=ALU.add,
                                         op1=ALU.subtract).then_inc(s_steps, 1)
            dve.wait_ge(s_src, 16)
            dve.tensor_scalar(src_i[:, 1, :], src_i[:, 0, :], SHIFT, None, ALU.arith_shift_right)
            link(dve, dve.tensor_scalar(src_i[:, 0, :], src_i[:, 0, :], P - 1, None, ALU.bitwise_and))
            dve.tensor_copy(src_lo[:, :], src_i[:, 0, :])
            link(dve, dve.tensor_copy(src_hi[:, :], src_i[:, 1, :]))
            for T in TABLES:
                dve.wait_ge(s_incl, T.no + 1)
                link(dve, dve.tensor_copy(T.incl, small(T, 0)))
                for c in range(T.chunks):
                    last = dve.tensor_scalar(T.done[:, c, :], iota_s[:, 0:T.steps], T.incl[:, c:c + 1], None, ALU.is_ge)
                last.then_inc(s_done, 1)
            for T in TABLES:
                dve.wait_ge(s_tile, T.no + 1)
                sums = small(T, 1)
                dve.tensor_copy(T.off, sums[:, :, 1])
                if T is ES:
                    dve.tensor_scalar(T.start_i, sums[:, :, 0], float(T.edges), float(T.last_start), ALU.mult, ALU.min)
                dve.tensor_scalar(T.tile_i, sums[:, :, 0], float(T.rows - 1), None, ALU.min).then_inc(s_tile_i, 1)
            dve_weights(dve)
            for T in TABLES:
                dve.wait_ge(s_got[T.name], 16 * T.step_chunks)
                link(dve, dve.tensor_scalar(T.ftile_i, T.step_rows[:, :, T.width - 1], SHIFT, None, ALU.arith_shift_right))
                link(dve, dve.tensor_tensor(T.ftile, T.ftile_i, T.off, ALU.subtract))
                link(dve, dve.tensor_tensor(T.ftile, T.ftile, T.step_id, ALU.add))
                link(dve, dve.tensor_scalar(T.ftile, T.ftile, 0.0, float(NT - 1), ALU.max, ALU.min))
                dve.tensor_copy(T.nt_i, T.ftile)
                link(dve, dve.tensor_scalar(T.nt_nodes, T.ftile, float(P), None, ALU.mult))
                for k in range(T.step_chunks):
                    rel = T.nt_nodes[:, k:k + 1]
                    if T is ES:
                        last = dve.tensor_scalar(T.rel[:, k, :], T.step_rows[:, k, 0:T.edges], rel, None, ALU.subtract)
                    else:
                        last = dve.tensor_scalar(T.rel[:, k, :], T.step_rows[:, k, 0:T.edges], -1.0, rel, ALU.mult, ALU.add)
                if T.src:
                    last = dve.tensor_copy(src_f, T.step_rows[:, :, T.edges:2 * T.edges])
                last.then_inc(s_rel, 1)
            dve.wait_ge(s_relt, 1)
            dve.tensor_copy(es_dst[:, :, :].rearrange("p (k s) j -> p k s j", s=P),
                            bank[:, 6:8, :].rearrange("p b (j s) -> p b s j", s=P)).then_inc(s_tab, 1)
            dve.wait_ge(s_relt, 2)
            dve.tensor_copy(at_negdst[:, :], bank[:, 2:4, :].rearrange("p b c -> p (b c)")[:, 0:AT.steps])
            dve.tensor_copy(at_src[:, :], bank[:, 4:6, :].rearrange("p b c -> p (b c)")[:, 0:AT.steps]).then_inc(s_tab, 1)

        def n_ends_total(T):
            return 16 * (2 * (T.chunks - 1) + 4)

        def small(T, what):
            if what == 0:
                return bank[:, T.no, 0:T.chunks]
            return bank[:, T.no, 16:16 + 2 * T.step_chunks].rearrange("p (k w) -> p k w", w=2)

        QS = 1.0 / float(HD) ** 0.5

        def dve_weights(dve):
            dve.wait_ge(s_identity, 1)
            dve.wait_ge(s_wl, 16 * WL_LOADS)
            for l in range(LAYERS):
                c = cols_l[l]
                dve.tensor_tensor(raw_pos[l], raw_pos[l], ident[:, :], ALU.add)
                link(dve, dve.tensor_tensor(c[:, 2:3], c[:, 2:3], c[:, 3:4], ALU.add))
                for i, k in enumerate((1, 2, 4)):
                    last = dve.tensor_copy(bc_l[l][:, i, :], c[:, k:k + 1].to_broadcast([P, P]))
                last.then_inc(s_wprep, 1)
            for l in range(LAYERS):
                dve.wait_ge(s_wmm, 1 + l)
                dve.tensor_copy(pos_t[l], bank[:, 2 + 3 * l, 0:P]).then_inc(s_wprep, 1)
                dve.tensor_scalar(wdeg_bc[l][:, 0:D], bank[:, 2 + 3 * l, P:P + D], QS, None, ALU.mult)
                dve.tensor_copy(wdeg_bc[l][:, D:3 * D], bank[:, 2 + 3 * l, P + D:P + 3 * D])
                dve.tensor_tensor(b_up[l][:, :], bank[:, 4 + 3 * l, 384:388], cols_l[l][:, 7:11], ALU.add)
                dve.tensor_scalar(w_up[l][:, :], w_up[l][:, :], cols_l[l][:, 5:6], None, ALU.mult)
            for l in range(LAYERS):
                a = bank[:, 3 + 3 * l, 0:3 * D]
                dve.wait_ge(s_wmm, 3 + l)
                dve.tensor_copy(raw_a[l], a).then_inc(s_wprep, 1)
                dve.tensor_scalar(w_qkv[l][:, 0:D], a[:, 0:D], cols_l[l][:, 0:1], QS, ALU.mult, ALU.mult)
                dve.tensor_scalar(w_qkv[l][:, D:3 * D], a[:, D:3 * D], cols_l[l][:, 0:1], None, ALU.mult)
            for l in range(LAYERS):
                b = bank[:, 4 + 3 * l, 0:3 * D]
                dve.wait_ge(s_wmm, 5 + l)
                rest, parts = bias_rest[l], bias_parts[l]
                dve.tensor_scalar(rest[:, 0:D], b[0:3, 0:D], QS, None, ALU.mult)
                link(dve, dve.tensor_copy(rest[:, D:3 * D], b[0:3, D:3 * D]))
                for i in range(3):
                    link(dve, dve.tensor_copy(parts[:, i, :], rest))
                    link(dve, dve.tensor_tensor(rest, rest, parts[:, i, :], ALU.subtract))
                link(dve, dve.tensor_scalar(bias_rows[l][:, :], parts[:, 0, :], ident[0:3, 0:1], None, ALU.mult))
                for i in range(1, 3):
                    last = dve.scalar_tensor_tensor(out=bias_rows[l][:, :], in0=parts[:, i, :], scalar=ident[0:3, i:i + 1],
                                                    in1=bias_rows[l][:, :], op0=ALU.mult, op1=ALU.add)
                    if i == 1:
                        link(dve, last)
                last.then_inc(s_wprep, 1)

        def pe_prepare(pe):
            pe.wait_ge(s_identity, 1)
            for T in TABLES:
                pe.wait_ge(s_steps, T.no + 1)
                last = pe.matmul(small(T, 0), tri, T.ones_steps[:, :, 1], start=True, stop=T.chunks == 1, skip_group_check=True)
                for c in range(T.chunks - 1):
                    last = pe.matmul(small(T, 0)[:, c + 1:], ones_b, T.ones_steps[:, c:c + 1, 1].to_broadcast([P, T.chunks - 1 - c]),
                                     start=False, stop=c == T.chunks - 2, skip_group_check=True)
                last.then_inc(s_incl, 1)
            for T in TABLES:
                pe.wait_ge(s_done, T.no + 1)
                for k in range(T.step_chunks):
                    for c in range(T.chunks):
                        last = pe.matmul(small(T, 1)[:, k, :], T.done[:, c, k * P:(k + 1) * P], T.ones_steps[:, c, :],
                                         start=c == 0, stop=c == T.chunks - 1)
                last.then_inc(s_tile, 1)
            for l in range(LAYERS):
                pe.wait_ge(s_wprep, 1 + l)
                pe.transpose(bank[:, 2 + 3 * l, 0:P], raw_pos[l], ident[:, :])
                pe.matmul(bank[:, 2 + 3 * l, P:P + 3 * D], bc_l[l][:, 2, :], raw_qkv[l], start=True, stop=True)
                for k in range(FF // P):
                    last = pe.matmul(bank[:, 4 + 3 * l, 384 + k:385 + k], w_up[l][:, k * P:(k + 1) * P], cols_l[l][:, 6:7],
                                     start=True, stop=True)
                last.then_inc(s_wmm, 1)
            for l in range(LAYERS):
                pe.wait_ge(s_wprep, 3 + l)
                pe.matmul(bank[:, 3 + 3 * l, 0:3 * D], pos_t[l], raw_qkv[l], start=True, stop=True).then_inc(s_wmm, 1)
            for l in range(LAYERS):
                b = bank[:, 4 + 3 * l, 0:3 * D]
                pe.wait_ge(s_wprep, 5 + l)
                pe.matmul(b, bc_l[l][:, 1, :], raw_qkv[l], start=True, stop=False)
                pe.matmul(b, ones_f[0:1, :], bqkv_row[l], start=False, stop=False)
                pe.matmul(b, bc_l[l][:, 0, :], raw_a[l], start=False, stop=True).then_inc(s_wmm, 1)
            pe.wait_ge(s_wprep, 6 + LAYERS)
            pe.wait_ge(s_rel, 1)
            for k in range(ES.step_chunks):
                for j in range(ES_SUB):
                    last = pe.transpose(bank[:, 6 + k, j * P:(j + 1) * P],
                                        ES.rel[:, k, :].rearrange("s (p j) -> s p j", j=ES_SUB)[:, :, j], ident[:, :])
            last.then_inc(s_relt, 1)
            pe.wait_ge(s_rel, 2)
            for k in range(AT.step_chunks):
                pe.transpose(bank[:, 2 + k // 4, k % 4 * P:(k % 4 + 1) * P], AT.rel[:, k, :], ident[:, :])
                last = pe.transpose(bank[:, 4 + k // 4, k % 4 * P:(k % 4 + 1) * P], src_f[:, k, :], ident[:, :])
            last.then_inc(s_relt, 1)

        def sp_edge_sums(sp):
            sp.wait_ge(s_nt_in["es"], 32)
            sp.wait_ge(s_tab, 2)

            def body(i, first):
                _, starts = nc.values_load_multi_w_load_instructions(
                    es_start[0:1, bass.ds(i * 2 * ES_SLOTS, 2 * ES_SLOTS)], engines=(ENGINE.SP,), min_val=0, max_val=E - ES_EDGES,
                    skip_runtime_bounds_check_because=CLAMPED)
                for n in range(2 * ES_SLOTS):
                    if not first:
                        sp.wait_ge(es_summed, (i - 1) * 2 * ES_SLOTS + n + 1)
                    sp.dma_start(es_attr[:, n // ES_SLOTS, n % ES_SLOTS, :, :],
                                 edge_attr[bass.ds(starts[n], ES_EDGES), :].rearrange("(p j) d -> p j d", j=ES_SUB)
                                 ).then_inc(es_in[n], 16)
            body(0, True)
            with sp.Fori(1, ES_BODIES) as i:
                body(i, False)

        def run_rounds(eng, body):
            body(0, True, False)
            with eng.Fori(1, ES_BODIES - 1) as i:
                body(i, False, False)
            body(ES_BODIES - 1, False, True)

        def act_edge_sums(act):
            act.wait_ge(s_tab, 2)
            act.wait_ge(s_nt_out["at"], 16)

            def build(m, h, first):
                before = m * ACT_SLOTS
                for n in range(ACT_SLOTS):
                    if not first:
                        act.wait_ge(es_sel_act, before + n + 1 - ACT_SLOTS)
                    for j in range(ES_SUB):
                        last = act.activation(es_dist[:, n, j, :], iota_n[:, :], ACT.Abs, scale=-1.0,
                                              bias=es_dst[:, bass.ds(m * ES_SLOTS + DVE_SLOTS + n, 1), j])
                    last.then_inc(es_dist_ready, 1)
                for n in range(ACT_SLOTS):
                    s = DVE_SLOTS + n
                    act.wait_ge(es_dist_ready, before + n + 1)
                    if not (isinstance(m, int) and m < 2):
                        act.wait_ge(es_summed, (m - 2) * ES_SLOTS + s + 1)
                    act.activation(es_sel[:, h, s, :, :], es_dist[:, n, :, :], ACT.Relu, scale=-1.0, bias=1.0).then_inc(es_sel_act, 1)

            def body(i, first, last):
                for h in range(2):
                    build(i * 2 + h, h, first and h == 0)
            run_rounds(act, body)

        def pe_edge_sums(pe):
            def body(i, first, last_body):
                for h in range(2):
                    m = i * 2 + h
                    for s in range(ES_SLOTS):
                        pe.wait_ge(es_in[h * ES_SLOTS + s], 16 * (i + 1))
                        if s < DVE_SLOTS:
                            pe.wait_ge(es_sel_dve, m * DVE_SLOTS + s + 1)
                        else:
                            pe.wait_ge(es_sel_act, m * ACT_SLOTS + s - DVE_SLOTS + 1)
                        if not (first and h == 0):
                            pe.wait_ge(es_added, (m - 1) * ES_SLOTS + s + 1)
                        for j in range(ES_SUB):
                            last = pe.matmul(bank[:, 4 + s, 0:D], es_sel[:, h, s, j, :], es_attr[:, h, s, j, :],
                                             start=j == 0, stop=j == ES_SUB - 1)
                        last.then_inc(es_summed, 1)
                    pe.wait_ge(hist_oh, m + 1)
                    for c in range(HIST_ROUND):
                        last = pe.matmul(bank[:, 0, 0:NT], oh_lo[h][:, :, c], oh_hi[h][:, :, c], start=first and h == 0 and c == 0,
                                         stop=last_body and h == 1 and c == HIST_ROUND - 1, skip_group_check=True)
                    last.then_inc(hist_mm, 1)
            run_rounds(pe, body)
            pe.wait_ge(s_degdve, 1)
            pe.matmul(bank[:, 6, 0:NT], ones_f[:, :], deg_tmp[:, :], start=True, stop=True).then_inc(s_degmm, 1)
            pe.wait_ge(s_degdve, 2)
            pe.matmul(bank[:, 6, 64:64 + NT], ones_f[:, :], deg_tmp[:, :], start=True, stop=True).then_inc(s_degmm, 1)

        def dve_edge_sums(dve):
            dve.wait_ge(s_nt_in["es"], 32)
            dve.wait_ge(s_tab, 2)
            dve.wait_ge(s_nt_out["at"], 16)

            def one_hots(m, h, buf, parts, codes):
                return dve.tensor_tensor(buf[h], hist_iota[0:HIST_ROWS, 0:parts, :],
                                         codes[:, bass.ds(m * HIST_ROUND, HIST_ROUND)].unsqueeze(1)
                                         .to_broadcast([HIST_ROWS, parts, HIST_ROUND]), ALU.is_equal)

            def select(m, h, s):
                if not (isinstance(m, int) and m < 2):
                    dve.wait_ge(es_summed, (m - 2) * ES_SLOTS + s + 1)
                dve.tensor_tensor(es_sel[:, h, s, :, :], iota_n[:, :].unsqueeze(1).to_broadcast([P, ES_SUB, P]),
                                  es_dst[:, bass.ds(m * ES_SLOTS + s, 1), :].rearrange("p s j -> p (s j)").unsqueeze(2)
                                  .to_broadcast([P, ES_SUB, P]), ALU.is_equal).then_inc(es_sel_dve, 1)

            def body(i, first, last):
                _, tiles = nc.values_load_multi_w_load_instructions(
                    es_nt[0:1, bass.ds(i * 2 * ES_SLOTS, 2 * ES_SLOTS)], engines=(ENGINE.DVE,), min_val=0, max_val=NT - 1,
                    skip_runtime_bounds_check_because=CLAMPED)

                def add(m, h, s):
                    dve.wait_ge(es_summed, m * ES_SLOTS + s + 1)
                    if not (first and h == 0 and s == 0):
                        dve.wait_ge(es_added, m * ES_SLOTS + s)
                    a = agg[:, bass.ds(tiles[h * ES_SLOTS + s], 1), 0:D].rearrange("p t d -> p (t d)")
                    dve.tensor_tensor(a, bank[:, 4 + s, 0:D], a, ALU.add).then_inc(es_added, 1)

                for h in range(2):
                    m, ahead = i * 2 + h, not (last and h == 1)
                    if ahead:
                        if not (first and h == 0):
                            dve.wait_ge(hist_mm, m)
                        one_hots(m + 1, 1 - h, oh_lo, P, src_lo)
                    add(m, h, 0)
                    if ahead:
                        one_hots(m + 1, 1 - h, oh_hi, NT, src_hi).then_inc(hist_oh, 1)
                    add(m, h, 1)
                    for s in range(2):
                        if ahead and s < DVE_SLOTS:
                            select(m + 1, 1 - h, s)
                        add(m, h, 2 + s)
            one_hots(0, 0, oh_lo, P, src_lo)
            one_hots(0, 0, oh_hi, NT, src_hi).then_inc(hist_oh, 1)
            for s in range(DVE_SLOTS):
                select(0, 0, s)
            run_rounds(dve, body)
            dve.wait_ge(hist_mm, ES_ROUNDS)
            link(dve, dve.tensor_scalar(deg[:, :], bank[:, 0, 0:NT], 1.0, None, ALU.add))
            dve.tensor_tensor(deg_tmp[:, :], deg[:, :], node_mask[:, :], ALU.mult).then_inc(s_degdve, 1)
            dve.wait_ge(s_degmm, 1)
            link(dve, dve.tensor_reduce(stat[:, 0:1], bank[:, 6, 0:NT], AX_X, ALU.add))
            link(dve, dve.tensor_scalar(stat[:, 1:2], stat[:, 0:1], 1.0 / N, None, ALU.mult))
            link(dve, dve.tensor_scalar(deg[:, :], deg[:, :], stat[:, 1:2], None, ALU.subtract))
            link(dve, dve.tensor_tensor(deg[:, :], deg[:, :], node_mask[:, :], ALU.mult))
            dve.tensor_tensor(deg_tmp[:, :], deg[:, :], deg[:, :], ALU.mult).then_inc(s_degdve, 1)
            dve.wait_ge(s_degmm, 2)
            link(dve, dve.tensor_reduce(stat[:, 2:3], bank[:, 6, 64:64 + NT], AX_X, ALU.add))
            dve.tensor_scalar(stat[:, 3:4], stat[:, 2:3], 1.0 / (N - 1), None, ALU.mult).then_inc(s_degdve, 1)
            dve.wait_ge(s_degpow, 2)
            link(dve, dve.tensor_scalar(stat[:, 5:6], stat[:, 5:6], 1e-6, None, ALU.add))
            link(dve, dve.reciprocal(stat[:, 6:7], stat[:, 5:6]))
            link(dve, dve.tensor_scalar(deg[:, :], deg[:, :], stat[:, 6:7], None, ALU.mult))

        def pool_degree(pool):
            pool.memset(stat[:, 4:5], 0.5).then_inc(s_degpow, 1)
            pool.wait_ge(s_degdve, 3)
            pool.wait_ge(s_degpow, 1)
            pool.tensor_tensor(stat[:, 5:6], stat[:, 3:4], stat[:, 4:5], ALU.pow).then_inc(s_degpow, 1)

        MLP, POST, FINAL = range(3)

        def norm_steps(k):
            return (f"bn{k}", f"sums{k}", f"halves{k}", f"var{k}")

        def rstd_steps(k):
            return (f"rstd{k}", f"shift{k}")

        def each(name, n):
            return tuple(f"{name}{k}" for k in range(n))

        UPS = FF // P
        SELF = ("prod", "logit", "number", "clip", "att", "self")

        def steps_of(kind, who, t):
            pre = kind != FINAL
            if kind == MLP:
                return {
                    "pe": ("aggt", "zt", "h1", "h2", "o", "xt") + each("qkv", t),
                    "act": ("z0", "aggt_sb", "zt_sb", "h1_sb", "h2_sb", "z1", "z2", "z3", "xt_sb", "exp"),
                    "dve": norm_steps(0) + ("o",) + norm_steps(1) + norm_steps(2) + norm_steps(3) + each("qkv", t) + SELF,
                    "pool": rstd_steps(0) + ("xs",) + rstd_steps(1) + ("zw", "x1") + rstd_steps(2) + rstd_steps(3),
                }[who]
            return {
                "pe": ("aggt", "o", "zt") + each("up", UPS) + ("down",) + ((("xt",) + each("qkv", t)) if pre else ()),
                "act": ("aggt_sb", "z0", "zt_sb") + each("up_sb", UPS) + (("z1", "xt_sb", "exp") if pre else ()),
                "dve": ("guard", "inverse", "an", "x") + norm_steps(0) + ("y",) + ((norm_steps(1) + each("qkv", t) + SELF) if pre else ()),
                "pool": ("xb",) + rstd_steps(0) + (("xsum",) if kind == FINAL else ()) + ("xob",) + (rstd_steps(1) if pre else ()),
            }[who]

        TRANSFERS = {"loaded": (2, 1, 2), "saved": (1, 0, 0), "kept": (1, 1, 1), "out": (2, 2, 0)}
        step_sem = {(who, b): sem(f"{who}_unit{b}") for who in ("pe", "act", "dve", "pool") for b in range(BUFS)}
        move_sem = {(name, b): sem(f"rows_{name}{b}") for name in TRANSFERS for b in range(BUFS)}

        def unit_tiles(n):
            return min(UNIT, NT - n * UNIT)

        class Unit:

            def __init__(self, n, i=0):
                self.b, self.t = n % BUFS, unit_tiles(n) if isinstance(i, int) else UNIT
                self.before = n // BUFS + i
                self.base = (n + i * BUFS) * UNIT
                self.again = n >= BUFS
                self.cols = self.t * P

            def nodes(self, buf, lo=0, hi=D):
                return buf[:, bass.ds(self.base, self.t), lo:hi]

            def rows(self, d):
                if d.shape[0] == N and isinstance(self.base, int) and self.base == NT - 1:
                    return d[(NT - 1) * P:N, :].rearrange("(t p) c -> p t c", t=1), LAST_ROWS
                return d[bass.ds(self.base * P, self.t * P), :].rearrange("(t p) c -> p t c", p=P), P

        class Phase:

            def __init__(self, ph, kind, layer_post, layer_pre):
                self.ph, self.kind, self.post, self.pre = ph, kind, layer_post, layer_pre

            def count(self, who, b, units=UNITS):
                return sum(len(steps_of(self.kind, who, unit_tiles(n))) for n in range(b, units, BUFS))

            def earlier(self, who, b):
                return sum(F.count(who, b) for F in phases[:self.ph])

            def sem(self, who, u):
                return step_sem[who, u.b]

            def done(self, who, step, u, back=0):
                t = UNIT if back else u.t
                n = len(steps_of(self.kind, who, UNIT)) * (u.before - back) + steps_of(self.kind, who, t).index(step) + 1
                return step_sem[who, u.b], n + self.earlier(who, u.b)

            def earlier_moves(self, name, b):
                return 16 * sum(TRANSFERS[name][ph] for ph in range(self.ph)) * len(range(b, UNITS, BUFS))

            def moved(self, name, u, back=0):
                return move_sem[name, u.b], 16 * TRANSFERS[name][self.ph] * (u.before - back + 1) + self.earlier_moves(name, u.b)

        phases = [Phase(0, MLP, None, 0), Phase(1, POST, 0, 1), Phase(2, FINAL, 1, None)]

        def run_units(eng, F, step):
            wide = 4 + (eng is nc.sync)
            parts = wide - (F.kind == FINAL)

            def at(n, i=0):
                return [Unit(n - k, i) if k < parts and (not isinstance(i, int) or 0 <= n - k < UNITS) else None for k in range(wide)]
            rounds = (UNITS - 1 - BUFS) // BUFS
            for n in range(BUFS):
                step(*at(n))
            with eng.Fori(0, rounds) as i:
                for n in range(BUFS, 2 * BUFS):
                    step(*at(n, i))
            for n in range(BUFS * (1 + rounds), UNITS + parts - 1):
                step(*at(n))

        def dense_done(eng, F):
            for b in range(BUFS):
                for who in ("pe", "act", "dve", "pool"):
                    eng.wait_ge(step_sem[who, b], F.earlier(who, b) + F.count(who, b))
                for name in TRANSFERS:
                    if TRANSFERS[name][F.ph]:
                        units = len(range(b, UNITS, BUFS))
                        eng.wait_ge(move_sem[name, b], F.earlier_moves(name, b) + 16 * TRANSFERS[name][F.ph] * units)

        def sp_dense(sp, F):
            def load(u):
                b, t = u.b, u.t
                if F.kind == MLP:
                    if u.again:
                        sp.wait_ge(*F.done("pool", "x1", u, 1))
                    rows, p = u.rows(x)
                    sp.dma_start(xb[b][0:p, 0:t, :], rows).then_inc(move_sem["loaded", b], 16)
                    if u.again:
                        sp.wait_ge(*F.done("pe", "aggt", u, 1))
                    sp.dma_start(agg_s[b][:, 0:t, :], u.nodes(agg)).then_inc(move_sem["loaded", b], 16)
                else:
                    if u.again:
                        sp.wait_ge(*F.done("dve", "x", u, 1))
                    sp.dma_start(xb[b][:, 0:t, :], u.nodes(xcur)).then_inc(move_sem["loaded", b], 16)
                    if F.kind == FINAL:
                        if u.again:
                            sp.wait_ge(*F.done("dve", "y", u, 1))
                        sp.dma_start(xob[b][:, 0:t, :], u.rows(x1_dram)[0]).then_inc(move_sem["loaded", b], 16)

            def project(u):
                sp.wait_ge(*F.done("dve", f"qkv{u.t - 1}", u))
                sp.sem_inc(Z.turn, 1)
                sp.dma_start(u.nodes(q_all), qkv[u.b][:, 0:u.t, 0:D]).then_inc(move_sem["out", u.b], 16)
                sp.dma_start(u.rows(kv_dram[F.pre])[0], qkv[u.b][:, 0:u.t, D:3 * D]).then_inc(move_sem["out", u.b], 16)

            def step(a, _, __, d, e):
                if a:
                    load(a)
                if F.kind == MLP and d:
                    sp.wait_ge(*F.done("pool", "x1", d))
                    sp.dma_start(d.rows(x1_dram)[0], xo[d.b][:, 0:d.t, :]).then_inc(move_sem["saved", d.b], 16)
                    sp.wait_ge(*F.done("act", "z2", d))
                    sp.dma_start(d.nodes(xcur), xob[d.b][:, 0:d.t, :]).then_inc(move_sem["kept", d.b], 16)
                elif d:
                    sp.wait_ge(*F.done("dve", "y", d))
                    rows, p = d.rows(out) if F.kind == FINAL else (d.nodes(xcur), P)
                    sp.dma_start(rows, xo[d.b][0:p, 0:d.t, :]).then_inc(move_sem["kept", d.b], 16)
                if e:
                    project(e)
            return step

        def pool_dense(pool, F):
            def rstd(u, k):
                neg_mean, _, _, var_eps, factor, shift = stat_rows(u)
                pool.wait_ge(*F.done("dve", f"var{k}", u))
                pool.tensor_tensor(factor, var_eps, half_neg[:, 0:u.t], ALU.pow).then_inc(F.sem("pool", u), 1)
                pool.wait_ge(*F.done("pool", f"rstd{k}", u))
                pool.tensor_tensor(shift, factor, neg_mean, ALU.mult).then_inc(F.sem("pool", u), 1)

            def add_row(u, o, a, row):
                pool.tensor_tensor(o[u.b][:, 0:u.t, :], a[u.b][:, 0:u.t, :], row.to_broadcast([P, u.t, D]), ALU.add
                                   ).then_inc(F.sem("pool", u), 1)

            def mlp_step(a, c, d, e):
                if d:
                    pool.wait_ge(*F.done("act", "z1", d))
                    pool.tensor_tensor(z[d.b][:, 0:d.t, :], z[d.b][:, 0:d.t, :], rows_0[:, 1:2, :].to_broadcast([P, d.t, D]), ALU.mult
                                       ).then_inc(F.sem("pool", d), 1)
                    pool.wait_ge(*F.done("pool", "zw", d))
                    pool.tensor_tensor(xo[d.b][:, 0:d.t, :], z[d.b][:, 0:d.t, :], xb[d.b][:, 0:d.t, :], ALU.add
                                       ).then_inc(F.sem("pool", d), 1)
                if a:
                    rstd(a, 0)
                if d:
                    rstd(d, 2)
                if c:
                    rstd(c, 1)
                if a:
                    pool.wait_ge(*F.done("act", "z0", a))
                    add_row(a, xb, xb, rows_0[:, 2:3, :])
                if d:
                    rstd(d, 3)

            def post_step(a, c, d, e):
                bo, b2 = (rows_l[F.post][:, i:i + 1, :] for i in range(2))
                if a:
                    pool.wait_ge(*F.moved("loaded", a))
                    add_row(a, xb, xb, bo)
                if d and F.pre is not None:
                    rstd(d, 1)
                if c:
                    if F.kind == FINAL:
                        pool.tensor_tensor(xob[c.b][:, 0:c.t, :], xo[c.b][:, 0:c.t, :], xob[c.b][:, 0:c.t, :], ALU.add
                                           ).then_inc(F.sem("pool", c), 1)
                        pool.wait_ge(*F.done("pool", "xsum", c))
                        add_row(c, xob, xob, b2)
                    else:
                        add_row(c, xob, xo, b2)
                if a:
                    rstd(a, 0)
            return mlp_step if F.kind == MLP else post_step

        def pe_dense(pe, F):
            def transposes(u, rows, side):
                for t in range(u.t):
                    last = pe.transpose(bank[:, 2 * u.b + side, t * P:(t + 1) * P], rows[u.b][:, t, :], ident[:, :])
                last.then_inc(F.sem("pe", u), 1)

            def product(u, side, w, act_rows, start=True, stop=True):
                return pe.matmul(bank[:, 2 * u.b + side, 0:u.cols], w, act_rows[u.b][:, 0:u.cols], start=start, stop=stop)

            def node_product(u, side, act_rows, w):
                for t in range(u.t):
                    last = pe.matmul(bank[:, 2 * u.b + side, t * P:(t + 1) * P], act_rows[u.b][:, t * P:(t + 1) * P], w,
                                     start=True, stop=True)
                last.then_inc(F.sem("pe", u), 1)

            def project(u, tiles):
                for t in tiles:
                    if t >= u.t:
                        continue
                    if t >= 2:
                        pe.wait_ge(*F.done("dve", f"qkv{t - 2}", u))
                    o = bank[:, 2 * u.b + t % 2, 0:3 * D]
                    pe.matmul(o, t_sb[u.b][:, t * P:(t + 1) * P], w_qkv[F.pre][:, :], start=True, stop=False)
                    pe.matmul(o, ones_3[:, :], bias_rows[F.pre][:, :], start=False, stop=True).then_inc(F.sem("pe", u), 1)

            def free(u):
                if u.again:
                    pe.wait_ge(*F.done("dve", "y" if F.kind == FINAL else "self", u, 1))

            def mlp_step(a, c, d, e):
                if c:
                    pe.wait_ge(*F.done("act", "zt_sb", c))
                    product(c, 0, w1_0[:, 0, :], t_sb, stop=False)
                    product(c, 0, w1_0[:, 1, :], agg_t, start=False).then_inc(F.sem("pe", c), 1)
                if a:
                    free(a)
                    pe.wait_ge(*F.moved("loaded", a))
                    transposes(a, agg_s, 1)
                if c:
                    pe.wait_ge(*F.done("act", "h1_sb", c))
                    product(c, 1, w2_0[:, :], h1_t).then_inc(F.sem("pe", c), 1)
                if e:
                    pe.wait_ge(*F.done("act", "z3", e))
                    transposes(e, z, 1)
                if c:
                    pe.wait_ge(*F.done("act", "h2_sb", c))
                    node_product(c, 0, h2_t, w3_0[:, :])
                if e:
                    pe.wait_ge(*F.done("act", "xt_sb", e))
                    project(e, (0, 1))
                if a:
                    pe.wait_ge(*F.done("act", "z0", a))
                    transposes(a, z, 0)
                if e:
                    project(e, (2, 3))

            def post_step(a, c, d, e):
                l = F.post

                def up(k):
                    if k >= 2:
                        pe.wait_ge(*F.done("act", f"up_sb{k - 2}", c))
                    product(c, k % 2, w_up[l][:, k * P:(k + 1) * P], t_sb).then_inc(F.sem("pe", c), 1)
                if c:
                    pe.wait_ge(*F.done("act", "z0", c))
                    transposes(c, z, 1)
                if e:
                    pe.wait_ge(*F.done("act", "z1", e))
                    transposes(e, z, 1)
                if d:
                    pe.wait_ge(*F.done("act", f"up_sb{UPS - 1}", d))
                    for t in range(d.t):
                        for k in range(UPS):
                            last = pe.matmul(bank[:, 2 * d.b, t * P:(t + 1) * P], hid[d.b][:, k * 512 + t * P:k * 512 + (t + 1) * P],
                                             w_down[l][:, k, :], start=k == 0, stop=k == UPS - 1)
                    last.then_inc(F.sem("pe", d), 1)
                if a:
                    free(a)
                    pe.wait_ge(*F.done("dve", "an", a))
                    transposes(a, z, 1)
                if c:
                    pe.wait_ge(*F.done("act", "zt_sb", c))
                    up(0)
                    up(1)
                if a:
                    pe.wait_ge(*F.done("act", "aggt_sb", a))
                    node_product(a, 0, t_sb, w_o[l][:, :])
                if e:
                    pe.wait_ge(*F.done("act", "xt_sb", e))
                    project(e, (0, 1))
                if c:
                    for k in range(2, UPS):
                        up(k)
                if e:
                    project(e, (2, 3))
            return mlp_step if F.kind == MLP else post_step

        def act_dense(act, F):
            def move(u, side, dest, func=ACT.Copy, **kw):
                act.activation(dest[:, 0:u.cols], bank[:, 2 * u.b + side, 0:u.cols], func, **kw).then_inc(F.sem("act", u), 1)

            def normalise(u, k, rows, dest, func=ACT.Identity):
                _, _, _, _, factor, shift = stat_rows(u)
                act.wait_ge(*F.done("pool", f"shift{k}", u))
                for t in range(u.t):
                    last = act.activation(dest[u.b][:, t, :], rows[u.b][:, t, :], func, bias=shift[:, t:t + 1], scale=factor[:, t:t + 1])
                last.then_inc(F.sem("act", u), 1)

            def exp(u):
                act.wait_ge(*F.done("dve", "att", u))
                act.activation(u.nodes(agg, D, MW), att_s[u.b][:, 2, 0:u.t * HEADS].rearrange("p (t h) -> p t h", h=HEADS),
                               ACT.Exp).then_inc(F.sem("act", u), 1)

            def free(u):
                if u.again:
                    for name in TRANSFERS:
                        if name != "loaded" and TRANSFERS[name][F.ph]:
                            act.wait_ge(*F.moved(name, u, 1))

            def mlp_step(a, c, d, e):
                if c:
                    act.wait_ge(*F.done("pe", "h1", c))
                    move(c, 0, h1_t[c.b], ACT.Relu, bias=cols_0[:, 0:1])
                if e:
                    normalise(e, 3, xob, z)
                if c:
                    act.wait_ge(*F.done("pe", "h2", c))
                    move(c, 1, h2_t[c.b], ACT.Relu, bias=cols_0[:, 1:2])
                if e:
                    act.wait_ge(*F.done("pe", "xt", e))
                    move(e, 1, t_sb[e.b])
                if a:
                    normalise(a, 0, xb, z, ACT.Relu)
                    free(a)
                    act.wait_ge(*F.done("pe", "aggt", a))
                    move(a, 1, agg_t[a.b])
                    act.wait_ge(*F.done("pe", "zt", a))
                    move(a, 0, t_sb[a.b])
                if d:
                    normalise(d, 2, xo, xob, ACT.Relu)
                if c:
                    normalise(c, 1, xob, z)
                if e:
                    exp(e)

            def post_step(a, c, d, e):
                def up(k):
                    act.wait_ge(*F.done("pe", f"up{k}", c))
                    move(c, k % 2, hid[c.b][:, k * 512:(k + 1) * 512], ACT.Gelu, bias=b_up[F.post][:, k:k + 1])
                if c:
                    act.wait_ge(*F.done("pe", "zt", c))
                    move(c, 1, t_sb[c.b])
                if e:
                    act.wait_ge(*F.done("pe", "xt", e))
                    move(e, 1, t_sb[e.b])
                if a:
                    free(a)
                    act.wait_ge(*F.done("pe", "aggt", a))
                    move(a, 1, t_sb[a.b])
                if c:
                    for k in range(UPS):
                        up(k)
                if d and F.pre is not None:
                    normalise(d, 1, xo, z)
                if a:
                    normalise(a, 0, xo, z)
                if e:
                    exp(e)
            return mlp_step if F.kind == MLP else post_step

        def dve_dense(dve, F):
            def count(u, ins):
                ins.then_inc(F.sem("dve", u), 1)

            def stats(u, k, rows):
                neg_mean, gap, spread2, var_eps, _, _ = stat_rows(u)
                halves = bn[u.b][:, 0:u.t, :]
                for t in range(u.t):
                    last = dve.bn_stats(bn[u.b][:, t, :], rows[u.b][:, t, :])
                count(u, last)
                dve.wait_ge(*F.done("dve", f"bn{k}", u))
                dve.tensor_tensor(neg_mean, halves[:, :, 1], halves[:, :, 4], ALU.add)
                dve.tensor_tensor(gap, halves[:, :, 1], halves[:, :, 4], ALU.subtract)
                count(u, dve.tensor_tensor(spread2, halves[:, :, 2], halves[:, :, 5], ALU.add))
                dve.wait_ge(*F.done("dve", f"sums{k}", u))
                dve.tensor_scalar(neg_mean, neg_mean, -0.5, None, ALU.mult)
                dve.tensor_tensor(gap, gap, gap, ALU.mult)
                count(u, dve.tensor_scalar(spread2, spread2, 1.0 / D, EPS, ALU.mult, ALU.add))
                dve.wait_ge(*F.done("dve", f"halves{k}", u))
                count(u, dve.scalar_tensor_tensor(out=var_eps, in0=gap, scalar=0.25, in1=spread2, op0=ALU.mult, op1=ALU.add))

            def from_bank(u):
                return bank[:, 2 * u.b, 0:u.cols].rearrange("p (t d) -> p t d", d=D)

            def project(u):
                for t in range(u.t):
                    dve.wait_ge(*F.done("pe", f"qkv{t}", u))
                    count(u, dve.scalar_tensor_tensor(out=qkv[u.b][:, t, :], in0=wdeg_bc[F.pre][:, :], scalar=deg[:, bass.ds(u.base + t, 1)],
                                                      in1=bank[:, 2 * u.b + t % 2, 0:3 * D], op0=ALU.mult, op1=ALU.add))

            def loop_logits(u):
                rows, n = qkv[u.b][:, 0:u.t, :], u.t * HEADS
                raw, number, logit = (att_s[u.b][:, i, 0:n] for i in range(3))
                dve.wait_ge(*F.done("dve", f"qkv{u.t - 1}", u))
                count(u, dve.tensor_tensor(z[u.b][:, 0:u.t, :], rows[:, :, 0:D], rows[:, :, D:2 * D], ALU.mult))
                dve.wait_ge(*F.done("dve", "prod", u))
                count(u, dve.tensor_reduce(raw, z[u.b][:, 0:u.t, :].rearrange("p t (h c) -> p (t h) c", h=HEADS), AX_X, ALU.add))
                dve.wait_ge(*F.done("dve", "logit", u))
                count(u, dve.tensor_tensor(number, raw, raw, ALU.is_equal))
                count(u, dve.tensor_scalar(logit, raw, -CLIP, CLIP, ALU.max, ALU.min))
                dve.wait_ge(*F.done("dve", "clip", u))
                count(u, dve.tensor_tensor(logit, logit, number, ALU.mult))

            def loop_messages(u):
                rows = qkv[u.b][:, 0:u.t, :]
                dve.wait_ge(*F.done("act", "exp", u))
                count(u, dve.tensor_tensor(u.nodes(agg).rearrange("p t (h c) -> p t h c", h=HEADS),
                                           rows[:, :, 2 * D:3 * D].rearrange("p t (h c) -> p t h c", h=HEADS),
                                           u.nodes(agg, D, MW).unsqueeze(3).to_broadcast([P, u.t, HEADS, HD]), ALU.mult))

            def mlp_step(a, c, d, e):
                if a:
                    dve.wait_ge(*F.moved("loaded", a))
                    stats(a, 0, xb)
                if d:
                    dve.wait_ge(*F.done("pool", "x1", d))
                    stats(d, 2, xo)
                if c:
                    dve.wait_ge(*F.done("pe", "o", c))
                    count(c, dve.tensor_tensor(xob[c.b][:, 0:c.t, :], from_bank(c), rows_0[:, 0:1, :].to_broadcast([P, c.t, D]), ALU.add))
                    dve.wait_ge(*F.done("dve", "o", c))
                    stats(c, 1, xob)
                if e:
                    project(e)
                    loop_logits(e)
                if d:
                    dve.wait_ge(*F.done("act", "z2", d))
                    stats(d, 3, xob)
                if e:
                    loop_messages(e)

            def post_step(a, c, d, e):
                if a:
                    n = a.t * HEADS
                    guarded, inverse = (att_s[a.b][:, i, 0:n].rearrange("p (t h) -> p t h", h=HEADS) for i in range(2))
                    count(a, dve.tensor_scalar(guarded, a.nodes(agg, D, MW), SUM_GUARD, None, ALU.add))
                    dve.wait_ge(*F.done("dve", "guard", a))
                    count(a, dve.reciprocal(inverse, guarded))
                    dve.wait_ge(*F.done("dve", "inverse", a))
                    count(a, dve.tensor_tensor(z[a.b][:, 0:a.t, :].rearrange("p t (h c) -> p t h c", h=HEADS),
                                               a.nodes(agg).rearrange("p t (h c) -> p t h c", h=HEADS),
                                               inverse.unsqueeze(3).to_broadcast([P, a.t, HEADS, HD]), ALU.mult))
                if d:
                    dve.wait_ge(*F.done("pe", "down", d))
                    dve.wait_ge(*F.done("pool", "xob", d))
                    count(d, dve.tensor_tensor(xo[d.b][:, 0:d.t, :], from_bank(d), xob[d.b][:, 0:d.t, :], ALU.add))
                    if F.pre is not None:
                        dve.wait_ge(*F.done("dve", "y", d))
                        stats(d, 1, xo)
                if a:
                    dve.wait_ge(*F.done("pe", "o", a))
                    dve.wait_ge(*F.done("pool", "xb", a))
                    count(a, dve.tensor_tensor(xo[a.b][:, 0:a.t, :], from_bank(a), xb[a.b][:, 0:a.t, :], ALU.add))
                    dve.wait_ge(*F.done("dve", "x", a))
                    stats(a, 0, xo)
                if e:
                    project(e)
                    loop_logits(e)
                    loop_messages(e)
            return mlp_step if F.kind == MLP else post_step

        class Attention:

            def __init__(self):
                self.kv_in = sems("kv_loaded", KV_SLOTS // QUAD)
                self.qw_in = sems("q_loaded", 2)
                self.idx = sem("idx_staged")
                self.turn = sem("gather_turn")
                self.sel = sem("sel_ready")
                self.dist = sem("dist_ready")
                self.selt = sem("selt_ready")
                self.selt_sb = sem("selt_copied")
                self.qe = sem("q_spread")
                self.prod = sem("prod_ready")
                self.att = sem("att_chain")
                self.logit = sem("logits_ready")
                self.ex = sem("exp_ready")
                self.msg = sem("msg_ready")
                self.sum = sem("summed")
                self.added = sem("added")

        Z = Attention()
        ATT_BANK = ((0, 1), (2, 3), 4)

        def run_bodies(eng, body):
            body(0, True, False)
            with eng.Fori(1, AT_BODIES - 1) as i:
                body(i, False, False)
            body(AT_BODIES - 1, False, True)

        def pool_attention(pool, l):
            k0 = l * AT_QUADS

            def body(i, first, last):
                for r in range(QUADS):
                    slot = r % (KV_SLOTS // QUAD)
                    k = i * QUADS + r
                    if not (first and r < KV_SLOTS // QUAD):
                        pool.wait_ge(Z.msg, k0 + k - KV_SLOTS // QUAD + 1)
                    if slot == 0:
                        half = r * QUAD // KV_SLOTS
                        pool.tensor_copy(idx_stage[:, half, :], at_src[:, bass.ds(i * BODY + r * QUAD, KV_SLOTS)]).then_inc(Z.idx, 1)
                        pool.wait_ge(Z.idx, (k0 // QUADS + i) * 2 + half + 1)
                    pool.sem_inc(Z.turn, 1)
                    for j in range(QUAD):
                        n = slot * QUAD + j
                        pool.indirect_dma_start(kv[:, n, :], None, kv_dram[l], bass.IndirectOffsetOnAxis(idx_stage[:, half, n:n + 1], 0)
                                                ).then_inc(Z.kv_in[slot], 16)
            run_bodies(pool, body)

        def sp_attention(sp, l):
            k0 = l * AT_QUADS
            def body(i, first, last):
                for r in range(QUADS):
                    k = i * QUADS + r
                    _, tiles = nc.values_load_multi_w_load_instructions(
                        at_nt[0:1, bass.ds(i * BODY + r * QUAD, QUAD)], engines=(ENGINE.SP,), min_val=0, max_val=NT - 1, skip_runtime_bounds_check_because=CLAMPED)
                    if not (first and r < 2):
                        sp.wait_ge(Z.qe, k0 + k - 1)
                    for j in range(QUAD):
                        sp.dma_start(q_win[:, r % 2, j, :], q_all[:, bass.ds(tiles[j], 1), :].rearrange("p t d -> p (t d)")
                                     ).then_inc(Z.qw_in[r % 2], 16)
            run_bodies(sp, body)

        def act_attention(act, l):
            k0 = l * AT_QUADS
            def select(k, r, step, first):
                if not first:
                    act.wait_ge(Z.sel, (k0 + k))
                for j in range(QUAD):
                    m = act.activation(dist[:, j, :], iota_n[:, :], ACT.Abs, bias=at_negdst[:, bass.ds(step + j, 1)])
                m.then_inc(Z.dist, 1)
                act.wait_ge(Z.dist, k0 + k + 1)
                if not (isinstance(k, int) and k < QUADS):
                    act.wait_ge(Z.sum, (k0 + k - QUADS + 1) * QUAD)
                act.activation(sel[:, r % QUADS, :, :], dist, ACT.Relu, scale=-1.0, bias=1.0).then_inc(Z.sel, 1)

            def copy_t(k, r):
                act.wait_ge(Z.selt, k0 + k + 1)
                if not (isinstance(k, int) and k < 2):
                    act.wait_ge(Z.qe, k0 + k - 1)
                act.activation(sel_t[:, r % 2, :, :], bank[:, ATT_BANK[0][r % 2], :].rearrange("p (j e) -> p j e", j=QUAD),
                               ACT.Copy).then_inc(Z.selt_sb, 1)

            def body(i, first, last):
                for r in range(QUADS):
                    k = i * QUADS + r
                    if not (last and r + 2 >= QUADS):
                        copy_t(k + 2, r + 2)
                    if not (last and r + 3 >= QUADS):
                        select(k + 3, r + 3, (i * QUADS + r + 3) * QUAD, False)
                    act.wait_ge(Z.logit, k0 + k + 1)
                    act.activation(msg[:, r % 2, :, D:MW], att[:, r % 2, 2, :].rearrange("p (j h) -> p j h", j=QUAD),
                                   ACT.Exp).then_inc(Z.ex, 1)
            select(0, 0, 0, True)
            copy_t(0, 0)
            select(1, 1, QUAD, False)
            copy_t(1, 1)
            select(2, 2, 2 * QUAD, False)
            run_bodies(act, body)

        def pe_attention(pe, l):
            k0 = l * AT_QUADS
            def transposes(k, r):
                pe.wait_ge(Z.sel, k0 + k + 1)
                if not (isinstance(k, int) and k < 2):
                    pe.wait_ge(Z.selt_sb, k0 + k - 1)
                for j in range(QUAD):
                    m = pe.transpose(bank[:, ATT_BANK[0][r % 2], j * P:(j + 1) * P], sel[:, r % QUADS, j, :], ident[:, :])
                m.then_inc(Z.selt, 1)

            def spread(k, r, i):
                pe.wait_ge(Z.selt_sb, k0 + k + 1)
                pe.wait_ge(Z.qw_in[r % 2], 16 * QUAD * (k0 // 2 + i * (QUADS // 2) + r // 2 + 1))
                if not (isinstance(k, int) and k < 2):
                    pe.wait_ge(Z.prod, k0 + k - 1)
                for j in range(QUAD):
                    m = pe.matmul(bank[:, ATT_BANK[1][r % 2], j * D:(j + 1) * D], sel_t[:, r % 2, j, :], q_win[:, r % 2, j, :],
                                  start=True, stop=True)
                m.then_inc(Z.qe, 1)

            def sums(k, r):
                pe.wait_ge(Z.msg, k0 + k + 1)
                for j in range(QUAD):
                    if not (isinstance(k, int) and k < 1):
                        pe.wait_ge(Z.added, (k0 + k - 1) * QUAD + j + 1)
                    pe.matmul(bank[:, ATT_BANK[2] + j, 0:MW], sel[:, r % QUADS, j, :], msg[:, r % 2, j, :],
                              start=True, stop=True).then_inc(Z.sum, 1)

            def body(i, first, last):
                for r in range(QUADS):
                    k = i * QUADS + r
                    if not (last and r + 2 >= QUADS):
                        spread(k + 2, r + 2, i)
                    if not (first and r == 0):
                        sums(k - 1, (r - 1) % QUADS)
                    if not (last and r + 3 >= QUADS):
                        transposes(k + 3, r + 3)
            transposes(0, 0)
            spread(0, 0, 0)
            transposes(1, 1)
            spread(1, 1, 0)
            transposes(2, 2)
            run_bodies(pe, body)
            sums(AT_QUADS - 1, QUADS - 1)

        def dve_attention(dve, l):
            k0 = l * AT_QUADS
            HALF = QUADS // 2

            def load_tiles(step, n):
                _, tiles = nc.values_load_multi_w_load_instructions(
                    at_nt[0:1, bass.ds(step, n)], engines=(ENGINE.DVE,), min_val=0, max_val=NT - 1, skip_runtime_bounds_check_because=CLAMPED)
                return tiles

            def add(k, j, tile):
                dve.wait_ge(Z.sum, (k0 + k) * QUAD + j + 1)
                if not (isinstance(k, int) and k * QUAD + j == 0):
                    dve.wait_ge(Z.added, (k0 + k) * QUAD + j)
                a = agg[:, bass.ds(tile, 1), :].rearrange("p t c -> p (t c)")
                dve.tensor_tensor(a, bank[:, ATT_BANK[2] + j, 0:MW], a, ALU.add).then_inc(Z.added, 1)

            def weigh(k, r):
                dve.wait_ge(Z.ex, k0 + k + 1)
                if not (isinstance(k, int) and k < 2):
                    dve.wait_ge(Z.sum, (k0 + k - 1) * QUAD)
                s = r * QUAD % KV_SLOTS
                dve.tensor_tensor(msg[:, r % 2, :, 0:D].rearrange("p j (h c) -> p j h c", h=HEADS),
                                  kv[:, s:s + QUAD, D:2 * D].rearrange("p j (h c) -> p j h c", h=HEADS),
                                  msg[:, r % 2, :, D:MW].unsqueeze(3).to_broadcast([P, QUAD, HEADS, HD]), ALU.mult).then_inc(Z.msg, 1)

            def body(i, first, last):
                for r in range(QUADS):
                    k = i * QUADS + r
                    a = att[:, r % 2, :, :]
                    s = r * QUAD % KV_SLOTS
                    dve.wait_ge(Z.qe, k0 + k + 1)
                    dve.wait_ge(Z.kv_in[s // QUAD], 16 * QUAD * (k0 * QUAD // KV_SLOTS + i * (QUADS * QUAD // KV_SLOTS) + r * QUAD // KV_SLOTS + 1))
                    dve.tensor_tensor(prod[:, r % 2, :, :], bank[:, ATT_BANK[1][r % 2], :].rearrange("p (j d) -> p j d", j=QUAD),
                                      kv[:, s:s + QUAD, 0:D], ALU.mult).then_inc(Z.prod, 1)
                    behind = 0 if first and r < HALF else 2
                    if r % HALF == 0:
                        tiles = load_tiles((k - behind) * QUAD, (HALF - 2 + behind) * QUAD)

                    def join(j):
                        if not (first and r < 2):
                            add(k - 2, j, tiles[(r % HALF - 2 + behind) * QUAD + j])
                    join(0)
                    dve.wait_ge(Z.prod, k0 + k + 1)
                    dve.tensor_reduce(a[:, 0, :], prod[:, r % 2, :, :].rearrange("p j (h c) -> p (j h) c", h=HEADS), AX_X,
                                      ALU.add).then_inc(Z.att, 1)
                    join(1)
                    if not (first and r == 0):
                        weigh(k - 1, (r - 1) % QUADS)
                    dve.wait_ge(Z.att, 3 * (k0 + k) + 1)
                    dve.tensor_tensor(a[:, 1, :], a[:, 0, :], a[:, 0, :], ALU.is_equal).then_inc(Z.att, 1)
                    join(2)
                    dve.tensor_scalar(a[:, 2, :], a[:, 0, :], -CLIP, CLIP, ALU.max, ALU.min).then_inc(Z.att, 1)
                    join(3)
                    dve.wait_ge(Z.att, 3 * (k0 + k) + 3)
                    dve.tensor_tensor(a[:, 2, :], a[:, 2, :], a[:, 1, :], ALU.mult).then_inc(Z.logit, 1)
            run_bodies(dve, body)
            weigh(AT_QUADS - 1, QUADS - 1)
            tiles = load_tiles(AT_STEPS - 2 * QUAD, 2 * QUAD)
            for n, tile in enumerate(tiles):
                add(AT_QUADS - 2 + n // QUAD, n % QUAD, tile)

        def attention_done(eng, l):
            eng.wait_ge(Z.added, (l + 1) * AT_STEPS)

        @block.vector
        def _(dve):
            dve_prepare(dve)
            dve_edge_sums(dve)
            dve.wait_ge(s_w0, 16 * W0_LOADS)
            for l in range(LAYERS):
                run_units(dve, phases[l], dve_dense(dve, phases[l]))
                if l == 0:
                    dve.wait_ge(s_nt_in["at"], 16)
                dense_done(dve, phases[l])
                dve_attention(dve, l)
                attention_done(dve, l)
            run_units(dve, phases[LAYERS], dve_dense(dve, phases[LAYERS]))

        @block.sync
        def _(sp):
            sp_prepare(sp)
            sp_tables(sp)
            sp_edge_sums(sp)
            sp.wait_ge(es_added, ES_STEPS)
            sp.wait_ge(hist_mm, ES_ROUNDS)
            for l in range(LAYERS):
                run_units(sp, phases[l], sp_dense(sp, phases[l]))
                if l == 0:
                    sp.wait_ge(s_nt_in["at"], 16)
                dense_done(sp, phases[l])
                sp_attention(sp, l)
                attention_done(sp, l)
            run_units(sp, phases[LAYERS], sp_dense(sp, phases[LAYERS]))
            dense_done(sp, phases[LAYERS])

        @block.scalar
        def _(act):
            act_load_weights(act)
            act_edge_sums(act)
            act.wait_ge(s_w0, 16 * W0_LOADS)
            act.wait_ge(es_added, ES_STEPS)
            act.wait_ge(hist_mm, ES_ROUNDS)
            for l in range(LAYERS):
                run_units(act, phases[l], act_dense(act, phases[l]))
                dense_done(act, phases[l])
                act_attention(act, l)
                attention_done(act, l)
            run_units(act, phases[LAYERS], act_dense(act, phases[LAYERS]))

        @block.gpsimd
        def _(pool):
            pool_prepare(pool)
            pool_gather_rows(pool)
            pool_degree(pool)
            pool.wait_ge(es_added, ES_STEPS)
            pool.wait_ge(hist_mm, ES_ROUNDS)
            for l in range(LAYERS):
                run_units(pool, phases[l], pool_dense(pool, phases[l]))
                dense_done(pool, phases[l])
                pool_attention(pool, l)
                attention_done(pool, l)
            run_units(pool, phases[LAYERS], pool_dense(pool, phases[LAYERS]))

        @block.tensor
        def _(pe):
            pe_prepare(pe)
            pe_edge_sums(pe)
            pe.wait_ge(s_w0, 16 * W0_LOADS)
            for l in range(LAYERS):
                run_units(pe, phases[l], pe_dense(pe, phases[l]))
                dense_done(pe, phases[l])
                pe_attention(pe, l)
                attention_done(pe, l)
            run_units(pe, phases[LAYERS], pe_dense(pe, phases[LAYERS]))


_INS = ["x", "src", "dst", "edge_attr_128"] + [f"L0_gnn_{k}" for k in ("W1", "b1", "W2", "b2", "W3", "b3", "ln_w", "ln_b")] + [
    f"L1_gnn_{k}" for k in ("Wq", "bq", "Wk", "bk", "Wv", "bv", "Wo", "bo", "Wpos", "bpos", "Wdeg", "bdeg", "ln1_g", "ln1_b",
                            "ln2_g", "ln2_b", "W1", "b1", "W2", "b2")]


def kernel(**inputs):
    import numpy as _np
    import concourse.bacc as _bacc
    from concourse.bass_utils import run_bass_kernel_spmd as _run

    nc = _bacc.Bacc("TRN2", target_bir_lowering=False, num_devices=1)
    arrays, args = {}, {}
    for name in _INS:
        a = _np.ascontiguousarray(inputs[name])
        arrays[f"in_{name}_dram"] = a
        args[name] = nc.dram_tensor(f"in_{name}_dram", a.shape, mybir.dt.from_np(a.dtype), kind="ExternalInput").ap()
    out = nc.dram_tensor("out_0_dram", (N, D), F32, kind="ExternalOutput").ap()
    gnn_kernel(nc, args, out)
    r = _run(nc, [arrays], core_ids=[0])
    return r.results[0]["out_0_dram"]
```

```python
from contextlib import ExitStack

import concourse.bass as bass
from concourse import mybir

ALU = mybir.AluOpType
ACT = mybir.ActivationFunctionType
AX_X = mybir.AxisListType.X
F32 = mybir.dt.float32
BF16 = mybir.dt.bfloat16
I32 = mybir.dt.int32
ENGINE = mybir.EngineType

P = 128
N, E, D = 6250, 100000, 128
HEADS, HD, LAYERS, FF = 8, 16, 2, 512
MW = D + HEADS
EPS = 1e-5
CLIP = 50.0
SUM_GUARD = 1e-16 * 1.9287498e-22
NT = -(-N // P)
NPAD = NT * P
LAST_ROWS = N - (NT - 1) * P
CLAMPED = "the step tables are clamped to this range where they are built"
SHIFT = 7

AT_EDGES = 128
AT_TILES = -(-E // AT_EDGES)
QUAD, QUADS = 4, 16
BODY = QUAD * QUADS
AT_MOST = AT_TILES + NT - 1
AT_BODIES = -(-AT_MOST // BODY)
AT_STEPS = AT_BODIES * BODY
AT_QUADS = AT_BODIES * QUADS
KV_SLOTS = 32
KV_QUADS = KV_SLOTS // QUAD
HALVES = BODY // KV_SLOTS
SEL_SLOTS = 8
GROUP = 4
ES_SUB = 4
ES_EDGES = P * ES_SUB
ES_TILES = -(-E // ES_EDGES)
ES_SLOTS = 4
ES_BODIES = -(-(ES_TILES + NT - 1) // (2 * ES_SLOTS))
ES_ROUNDS = 2 * ES_BODIES
ES_STEPS = ES_ROUNDS * ES_SLOTS
DVE_SLOTS = 2
ACT_SLOTS = ES_SLOTS - DVE_SLOTS
HIST_ROWS = 125
HIST_COLS = E // HIST_ROWS
HIST_ROUND = -(-HIST_COLS // ES_ROUNDS)
HIST_PAD = HIST_ROUND * ES_ROUNDS

UNIT, BUFS = 4, 4
UNITS = -(-NT // UNIT)
UPS = FF // P
UNIT_WORDS = 5 * UNIT * D + UNIT * FF
assert UNIT * P <= 512 and NT == (UNITS - 1) * UNIT + 1

FULL = UNITS - 1
ARENA = (2 * KV_SLOTS * D + (SEL_SLOTS * QUAD + QUAD + 2 * QUAD) * P + 4 * QUAD * D + 2 * QUAD * (MW + 3 * HEADS)
         + UNIT * (4 * D + 2 * P + FF + 3 * D))
LAG = 2
UPDATE_SLOT = 4
for _i in range(LAG, AT_BODIES):
    assert (_i - LAG + 1) * AT_MOST <= FULL * (_i * BODY + (UPDATE_SLOT - 2) * QUAD)


class Table:

    def __init__(self, no, name, edges, tiles, steps, src):
        self.no, self.name, self.edges, self.tiles = no, name, edges, tiles
        self.chunks = -(-tiles // P)
        self.step_chunks = -(-steps // P)
        self.rows, self.steps = self.chunks * P, self.step_chunks * P
        self.last_start = E - edges
        self.repeated = tiles * edges - E
        self.src = src
        self.width = edges * (2 if src else 1) + 1


def gnn_kernel(nc, A, out):
    x, src, dst, edge_attr = A["x"], A["src"], A["dst"], A["edge_attr_128"]
    ES = Table(0, "es", ES_EDGES, ES_TILES, ES_STEPS, False)
    AT = Table(1, "at", AT_EDGES, AT_TILES, AT_STEPS, True)
    TABLES = (ES, AT)

    ctx = ExitStack()
    with ctx:
        ctx.enter_context(nc.allow_non_contiguous_dma(reason="columns of indices and of small parameters"))

        def sb(name, shape, dt=F32):
            return ctx.enter_context(nc.sbuf_tensor(name, shape, dt))

        def sem(name):
            return ctx.enter_context(nc.semaphore(name))

        def sems(name, n):
            return [sem(f"{name}{i}") for i in range(n)]

        def dram(name, shape, dt=F32):
            return nc.dram_tensor(name, shape, dt).ap()

        kv_dram = [dram(f"kv_rows{l}", [NPAD, 2 * D]) for l in range(LAYERS)]
        x1_dram = dram("x1_rows", [NPAD, D])
        for T in TABLES:
            T.rows_dram = dram(f"{T.name}_rows", [T.rows, T.width], I32)
            T.nt_dram = dram(f"{T.name}_node_tile", [T.steps], I32)
        pairs_dram = dram("step_pairs", [AT.steps, 2], I32)
        es_start_dram = dram("es_first_edge", [ES.steps], I32)

        xcur = sb("x_stream", [P, NT, D])
        q_all = sb("queries", [P, NT, D])
        agg = sb("aggregate", [P, NT, MW])
        iota_n = sb("iota_n", [P, P])
        ident = sb("ident", [P, P])
        deg = sb("degree", [P, NT])
        node_mask = sb("node_mask", [P, NT])
        deg_tmp = sb("degree_parts", [P, NT])
        stat = sb("degree_stats", [P, 8])
        minus_past = sb("minus_past", [P, 2])
        half_neg = sb("minus_half", [P, UNIT])
        ones_f = sb("ones_f", [P, P])
        at_negdst = sb("at_negdst", [P, AT.steps])
        at_src = sb("at_src", [P, AT.steps], I32)
        es_start = sb("es_start", [1, ES.steps], I32)
        es_nt = sb("es_nt", [1, ES.steps], I32)
        at_nt = sb("at_nt", [1, AT.steps], I32)
        unit_base = sb("unit_base", [1, UNITS], I32)
        idx_stage = sb("idx_stage", [P, 2, KV_SLOTS], I32)
        w_qkv = [sb(f"w_qkv{l}", [P, 3 * D]) for l in range(LAYERS)]
        wdeg_bc = [sb(f"wdeg_bc{l}", [P, 3 * D]) for l in range(LAYERS)]
        bias_rows = [sb(f"bias_rows{l}", [3, 3 * D], BF16) for l in range(LAYERS)]
        ones_3 = sb("ones_3", [3, P], BF16)
        w_o = [sb(f"w_o{l}", [P, D]) for l in range(LAYERS)]
        w_up = [sb(f"w_up{l}", [P, FF]) for l in range(LAYERS)]
        w_down = [sb(f"w_down{l}", [P, FF // P, D]) for l in range(LAYERS)]
        b_up = [sb(f"b_up{l}", [P, FF // P]) for l in range(LAYERS)]
        rows_l = [sb(f"rows_l{l}", [P, 2, D]) for l in range(LAYERS)]
        bn = [sb(f"bn{b}", [P, UNIT, 6]) for b in range(BUFS)]
        norm_stat = [sb(f"norm_stat{b}", [P, 6, UNIT]) for b in range(BUFS)]
        att_s = [sb(f"att_self{b}", [P, 6, UNIT * HEADS]) for b in range(BUFS)]
        arena = sb("arena", [P, ARENA])
        bank = ctx.enter_context(nc.psum_tensor("bank", [P, 8, 512], F32))

        class Area:

            def __init__(self, *regions):
                self.regions, self.used = regions, [0] * len(regions)

            def take(self, words, skip=0):
                i = [n >= skip and u + words <= r.shape[1] for n, (r, u) in enumerate(zip(self.regions, self.used))].index(True)
                self.used[i] += words
                return self.regions[i][:, self.used[i] - words:self.used[i]]

        W0_WORDS = 7 * D + 2

        area = Area(arena[:, :])
        es_attr = area.take(2 * ES_SLOTS * ES_SUB * D).rearrange("p (h s j d) -> p h s j d", h=2, s=ES_SLOTS, j=ES_SUB)
        es_sel = area.take(2 * ES_SLOTS * ES_SUB * P).rearrange("p (h s j n) -> p h s j n", h=2, s=ES_SLOTS, j=ES_SUB)
        es_dist = area.take(ACT_SLOTS * ES_SUB * P).rearrange("p (s j n) -> p s j n", s=ACT_SLOTS, j=ES_SUB)
        oh_lo, oh_hi = [[area.take(-(-n * HIST_ROUND // 2))[0:HIST_ROWS, :].bitcast(BF16)[:, 0:n * HIST_ROUND]
                         .rearrange("p (n c) -> p n c", c=HIST_ROUND) for h in range(2)] for n in (P, NT)]
        hist_iota = area.take(P * HIST_ROUND // 2).bitcast(BF16).rearrange("p (n c) -> p n c", c=HIST_ROUND)
        src_lo, src_hi = [area.take(HIST_PAD // 2)[0:HIST_ROWS, :].bitcast(BF16) for _ in range(2)]
        es_dst = area.take(ES.steps * ES_SUB).rearrange("p (s j) -> p s j", j=ES_SUB)
        edge_words = area.used[0]

        area = Area(arena[:, edge_words:4 * UNIT_WORDS], q_all[:, :, :].rearrange("p t d -> p (t d)"),
                    xcur[:, 3 * UNIT:, :].rearrange("p t d -> p (t d)"), arena[:, 4 * UNIT_WORDS:ARENA - W0_WORDS])
        for T in TABLES:
            late = T is AT
            T.first = area.take(T.chunks).bitcast(I32)
            T.last = area.take(T.chunks).bitcast(I32)
            T.ones_steps = area.take(T.chunks).bitcast(BF16).rearrange("p (c w) -> p c w", w=2)
            T.incl = area.take(T.chunks)
            T.done = area.take(T.chunks * T.steps // 2).bitcast(BF16).rearrange("p (c s) -> p c s", c=T.chunks)
            T.tile_i = area.take(T.step_chunks).bitcast(I32)
            T.start_i = area.take(T.step_chunks).bitcast(I32)
            T.off = area.take(T.step_chunks, late)
            T.step_id = area.take(T.step_chunks, late)
            T.ftile = area.take(T.step_chunks, late)
            T.ftile_i = area.take(T.step_chunks, late).bitcast(I32)
            T.nt_i = area.take(T.step_chunks, late).bitcast(I32)
            T.nt_nodes = area.take(T.step_chunks, late)
            T.step_rows = area.take(T.step_chunks * T.width, late).bitcast(I32).rearrange("p (k w) -> p k w", w=T.width)
            T.rel = area.take(T.step_chunks * T.edges, late).rearrange("p (k e) -> p k e", e=T.edges)
        pairs = area.take(2 * AT.step_chunks, 1).bitcast(I32).rearrange("p (k w) -> p k w", w=2)
        pairs_in_order = area.take(2 * AT.step_chunks, 1).bitcast(I32).rearrange("p (k w) -> p k w", w=2)
        order_i = area.take(AT.step_chunks, 1).bitcast(I32)
        order_f = area.take(AT.step_chunks, 1)
        quarter = area.take(AT.step_chunks, 1)
        per_unit = [area.take(UNITS, 1) for _ in range(8)]
        grid = [area.take(max(FULL, AT.step_chunks) * FULL, 1) for _ in range(2)]
        past_i = area.take(P).bitcast(I32)
        src_f = area.take(AT.steps, 1).rearrange("p (k e) -> p k e", e=P)
        iota_s = area.take(AT.steps)
        iota_i = area.take(AT.steps).bitcast(I32)
        step_id_i = area.take(AT.step_chunks).bitcast(I32)
        node_id_i = area.take(NT).bitcast(I32)
        neg1 = area.take(P).bitcast(I32)
        zero_i = area.take(2 * P).bitcast(I32)
        tri = area.take(P // 2).bitcast(BF16)
        ones_b = area.take(P // 2).bitcast(BF16)
        src_i = area.take(2 * HIST_PAD)[0:HIST_ROWS, :].bitcast(I32).rearrange("p (a c) -> p a c", a=2)
        raw_qkv = [area.take(3 * D, 1) for _ in range(LAYERS)]
        raw_pos = [area.take(D, 1) for _ in range(LAYERS)]
        pos_t = [area.take(D, 1) for _ in range(LAYERS)]
        raw_a = [area.take(3 * D, 1) for _ in range(LAYERS)]
        bqkv_row = [area.take(3 * D, 1)[0:1, :] for _ in range(LAYERS)]
        cols_l = [area.take(7 + FF // P, 1) for _ in range(LAYERS)]
        bc_l = [area.take(3 * P, 1).rearrange("p (i n) -> p i n", i=3) for _ in range(LAYERS)]
        bias_rest = [raw_a[l][0:3, :] for l in range(LAYERS)]
        bias_part = [raw_qkv[l].bitcast(BF16)[0:3, 0:3 * D] for l in range(LAYERS)]

        area = Area(arena[:, :])
        kv = area.take(KV_SLOTS * 2 * D).rearrange("p (s c) -> p s c", s=KV_SLOTS)
        sel = area.take(SEL_SLOTS * QUAD * P).rearrange("p (k j n) -> p k j n", k=SEL_SLOTS, j=QUAD)
        dist = area.take(QUAD * P).rearrange("p (j n) -> p j n", j=QUAD)
        sel_t = area.take(2 * QUAD * P).rearrange("p (k j e) -> p k j e", k=2, j=QUAD)
        q_win = area.take(2 * QUAD * D).rearrange("p (k j d) -> p k j d", k=2, j=QUAD)
        prod = area.take(2 * QUAD * D).rearrange("p (k j d) -> p k j d", k=2, j=QUAD)
        msg = area.take(2 * QUAD * MW).rearrange("p (k j c) -> p k j c", k=2, j=QUAD)
        att = area.take(2 * 3 * QUAD * HEADS).rearrange("p (k i c) -> p k i c", k=2, i=3)

        upd = []
        attention_words = area.used[0]
        for b, t in enumerate((UNIT, UNIT, 1)):
            if b == 1:
                area = Area(arena[:, KV_SLOTS * 2 * D:attention_words])
            take = lambda: area.take(t * D).rearrange("p (t d) -> p t d", t=t)
            upd.append({"z": take(), "t": area.take(t * P), "x": take(), "y": take(), "zn": take(), "tn": area.take(t * P),
                        "hid": area.take(UPS * t * P), "qkv": area.take(t * 3 * D).rearrange("p (t c) -> p t c", t=t)})
            upd[b]["x1"] = upd[b]["qkv"].rearrange("p t c -> p (t c)")[:, 0:t * D].rearrange("p (t d) -> p t d", t=t)

        area = Area(arena[:, ARENA - W0_WORDS:])
        w1_0 = area.take(2 * D).rearrange("p (k d) -> p k d", k=2)
        w2_0, w3_0 = area.take(D), area.take(D)
        cols_0 = area.take(2)
        rows_0 = area.take(3 * D).rearrange("p (i d) -> p i d", i=3)

        area = Area(arena[:, :])
        z, t_sb, xo, xob, xb, hid = [], [], [], [], [], []
        for b in range(BUFS):
            z.append(area.take(4 * D).rearrange("p (t d) -> p t d", t=4))
            t_sb.append(area.take(4 * P))
            xo.append(area.take(4 * D).rearrange("p (t d) -> p t d", t=4))
            xob.append(area.take(4 * D).rearrange("p (t d) -> p t d", t=4))
            xb.append(area.take(4 * D).rearrange("p (t d) -> p t d", t=4))
            hid.append(area.take(FF // P * 4 * P))
        h1_t = [hid[b][:, 0:512] for b in range(BUFS)]
        h2_t = [hid[b][:, 512:1024] for b in range(BUFS)]
        agg_t = [hid[b][:, 1024:1536] for b in range(BUFS)]
        agg_s = [hid[b][:, 1536:2048].rearrange("p (t d) -> p t d", t=UNIT) for b in range(BUFS)]
        qkv = [hid[b][:, 0:UNIT * 3 * D].rearrange("p (t c) -> p t c", t=UNIT) for b in range(BUFS)]

        def stat_rows(u):
            return [norm_stat[u.b][:, i, 0:u.t] for i in range(6)]

        s_const = sem("const_ready")
        s_iota = sem("iota_ready")
        s_ends_zero = sem("ends_zeroed")
        s_ends = {T.name: sem(f"{T.name}_ends_loaded") for T in TABLES}
        s_rows = {T.name: sem(f"{T.name}_rows_written") for T in TABLES}
        s_src = sem("src_loaded")
        s_agg = sem("aggregate_zeroed")
        s_w0 = sem("w0_loaded")
        s_wl = sem("wl_loaded")
        s_dve = sem("dve_chain")
        s_steps = sem("steps_counted")
        s_incl = sem("steps_summed")
        s_done = sem("done_marked")
        s_tile = sem("tile_summed")
        s_tile_i = sem("tile_ready")
        s_got = {T.name: sem(f"{T.name}_rows_gathered") for T in TABLES}
        s_rel = sem("rel_ready")
        s_relt = sem("rel_transposed")
        s_tab = sem("table_ready")
        s_nt_out = {T.name: sem(f"{T.name}_nt_written") for T in TABLES}
        s_nt_in = {T.name: sem(f"{T.name}_nt_loaded") for T in TABLES}
        s_pairs = sem("pairs_ready")
        s_pairs_out = sem("pairs_written")
        s_pairs_in = sem("pairs_gathered")
        s_ahead = sem("steps_ahead_counted")
        s_order = sem("order_ready")
        s_again = sem("rows_gathered_in_order")
        s_wprep = sem("weights_mixed")
        s_wmm = sem("weight_products")
        s_identity = sem("identity_ready")

        es_in = sems("es_attr_loaded", 2 * ES_SLOTS)
        es_sel_dve = sem("es_sel_ready_dve")
        es_sel_act = sem("es_sel_ready_act")
        es_dist_ready = sem("es_dist_ready")
        es_summed = sem("es_summed")
        es_added = sem("es_added")
        hist_oh = sem("hist_onehots_ready")
        hist_mm = sem("hist_counted")
        s_degdve = sem("degree_parts_ready")
        s_degpow = sem("degree_std_ready")

        block = ctx.enter_context(nc.Block())

        def column(a):
            return a.rearrange("(p o) -> p o", o=1)

        n_rows = {"es": 0, "at": 0}
        W0_LOADS = 3 + 2 + 3
        WL_LOADS = LAYERS * (3 + 1 + 1 + 1 + 1 + 3 + 7 + 1 + 2)

        def sp_prepare(sp):
            sp.wait_ge(s_ends_zero, 1)
            sp.wait_ge(s_const, 1)
            for T in TABLES:
                e, full, tail = T.edges, (T.chunks - 1) * P, T.tiles - (T.chunks - 1) * P
                tiled = dst[0:(T.tiles - 1) * e].rearrange("(t e) -> t e", e=e)
                parts = []
                for c in range(T.chunks - 1):
                    parts += [(T.first[:, c:c + 1], tiled[c * P:(c + 1) * P, 0:1]),
                              (T.last[:, c:c + 1], tiled[c * P:(c + 1) * P, e - 1:e])]
                c = T.chunks - 1
                parts += [(T.first[0:tail - 1, c:c + 1], tiled[full:, 0:1]),
                          (T.last[0:tail - 1, c:c + 1], tiled[full:, e - 1:e]),
                          (T.first[tail - 1:tail, c:c + 1], column(dst[(T.tiles - 1) * e:(T.tiles - 1) * e + 1])),
                          (T.last[tail - 1:tail, c:c + 1], column(dst[E - 1:E]))]
                for o, i in parts:
                    sp.dma_start(o, i).then_inc(s_ends[T.name], 16)
                last = T.tiles - 1
                r = T.rows_dram
                parts = [(r[0:last, 0:e], dst[0:last * e].rearrange("(t e) -> t e", e=e)),
                         (r[last:last + 1, T.repeated:e], dst[last * e:E].rearrange("(o e) -> o e", o=1)),
                         (r[0:last, T.width - 1:T.width], dst[0:last * e].rearrange("(t e) -> t e", e=e)[:, 0:1]),
                         (r[last:last + 1, T.width - 1:T.width], column(dst[last * e:last * e + 1])),
                         (r[T.tiles:T.rows, T.width - 1:T.width], past_i[0:T.rows - T.tiles, 0:1])]
                for a in range(0, T.repeated, P):
                    w = min(P, T.repeated - a)
                    parts.append((r[last:last + 1, a:a + w], neg1[0:1, 0:w]))
                for a in range(0, e, P):
                    parts.append((r[T.tiles:T.rows, a:a + P], neg1[0:T.rows - T.tiles, :]))
                if T.src:
                    parts += [(r[0:last, e:2 * e], src[0:last * e].rearrange("(t e) -> t e", e=e)),
                              (r[last:last + 1, e:2 * e], src[T.last_start:E].rearrange("(o e) -> o e", o=1)),
                              (r[T.tiles:T.rows, e:2 * e], zero_i[0:T.rows - T.tiles, 0:e])]
                for o, i in parts:
                    sp.dma_start(o, i).then_inc(s_rows[T.name], 16)
                n_rows[T.name] = 16 * len(parts)

        def sp_table(sp, T):
            sp.wait_ge(s_rel, T.no + 1)
            sp.dma_start(T.nt_dram.rearrange("(k p) -> p k", p=P), T.nt_i).then_inc(s_nt_out[T.name], 16)
            n = 16
            if T is ES:
                sp.dma_start(es_start_dram.rearrange("(k p) -> p k", p=P), T.start_i).then_inc(s_nt_out[T.name], 16)
                n = 32
            sp.wait_ge(s_nt_out[T.name], n)
            sp.dma_start((es_nt if T is ES else at_nt)[:, :],
                         T.nt_dram.rearrange("(o s) -> o s", o=1)).then_inc(s_nt_in[T.name], 16)
            if T is ES:
                sp.dma_start(es_start[:, :], es_start_dram.rearrange("(o s) -> o s", o=1)).then_inc(s_nt_in[T.name], 16)

        def act_load_src(act):
            act.wait_ge(s_ends_zero, 1)
            act.dma_start(src_i[:, 0, 0:HIST_COLS], src.rearrange("(p c) -> p c", p=HIST_ROWS)).then_inc(s_src, 16)

        def pool_load_weights(pool):
            for o, i in ((w1_0, A["L0_gnn_W1"].rearrange("(k p) n -> p k n", p=P)),
                         (w2_0, A["L0_gnn_W2"]), (w3_0, A["L0_gnn_W3"]),
                         (cols_0[:, 0:1], column(A["L0_gnn_b1"])), (cols_0[:, 1:2], column(A["L0_gnn_b2"])),
                         (rows_0[:, 0, :], A["L0_gnn_b3"].partition_broadcast(P)),
                         (rows_0[:, 1, :], A["L0_gnn_ln_w"].partition_broadcast(P)),
                         (rows_0[:, 2, :], A["L0_gnn_ln_b"].partition_broadcast(P))):
                pool.dma_start(o, i).then_inc(s_w0, 16)
            for l in range(LAYERS):
                w = {k[len("L1_gnn_"):]: v[l] for k, v in A.items() if k.startswith("L1_gnn_")}
                loads = [(raw_qkv[l][:, i * D:(i + 1) * D], w[k]) for i, k in enumerate(("Wq", "Wk", "Wv"))]
                loads += [(raw_pos[l], w["Wpos"]), (w_o[l][:, :], w["Wo"]), (w_up[l][:, :], w["W1"]),
                          (w_down[l][:, :, :], w["W2"].rearrange("(k p) n -> p k n", p=P))]
                loads += [(bqkv_row[l][:, i * D:(i + 1) * D], w[k].rearrange("(o d) -> o d", o=1))
                          for i, k in enumerate(("bq", "bk", "bv"))]
                cols = [w["ln1_g"], w["ln1_b"], w["bpos"], w["bdeg"], w["Wdeg"].rearrange("o d -> (o d)"), w["ln2_g"], w["ln2_b"]]
                loads += [(cols_l[l][:, i:i + 1], column(c)) for i, c in enumerate(cols)]
                loads += [(cols_l[l][:, 7:7 + FF // P], w["b1"].rearrange("(k p) -> p k", p=P)),
                          (rows_l[l][:, 0, :], w["bo"].partition_broadcast(P)),
                          (rows_l[l][:, 1, :], w["b2"].partition_broadcast(P))]
                for o, i in loads:
                    pool.dma_start(o, i).then_inc(s_wl, 16)

        def pool_prepare(pool):
            pool.memset(neg1, -1)
            pool.memset(zero_i, 0)
            pool.memset(past_i, (NT - 1) * P)
            pool.memset(ones_b, 1.0)
            pool.memset(ones_3[:, :], 1.0)
            pool.memset(tri, 1.0)
            pool.memset(ones_f[:, :], 1.0)
            pool.memset(ident[:, :], 1.0)
            pool.memset(half_neg[:, :], -0.5).then_inc(s_const, 1)
            pool.iota(iota_i, [[1, AT.steps]], base=0, channel_multiplier=0)
            pool.iota(step_id_i, [[P, AT.step_chunks]], base=0, channel_multiplier=1)
            pool.iota(node_id_i, [[P, NT]], base=0, channel_multiplier=1).then_inc(s_iota, 1)
            pool.wait_ge(s_const, 1)
            pool.affine_select(out=tri, in_=tri, pattern=[[1, P]], compare_op=ALU.is_ge, fill=0.0, base=0, channel_multiplier=-1)
            pool.affine_select(out=ident[:, :], in_=ident[:, :], pattern=[[1, P]], compare_op=ALU.is_equal, fill=0.0, base=0,
                               channel_multiplier=-1).then_inc(s_identity, 1)

        def pool_gather_rows(pool):
            for T in TABLES:
                pool.wait_ge(s_rows[T.name], n_rows[T.name])
                pool.wait_ge(s_tile_i, T.no + 1)
                for k in range(T.step_chunks):
                    pool.indirect_dma_start(T.step_rows[:, k, :], None, T.rows_dram,
                                            bass.IndirectOffsetOnAxis(T.tile_i[:, k:k + 1], 0)).then_inc(s_got[T.name], 16)
                if T is ES:
                    pool.memset(agg[:, :, :], 0.0).then_inc(s_agg, 1)

        def pool_gather_in_order(pool):
            pool.wait_ge(s_pairs, 1)
            pool.dma_start(pairs_dram.rearrange("(k p) w -> p k w", p=P), pairs).then_inc(s_pairs_out, 16)
            pool.wait_ge(s_pairs_out, 16)
            pool.wait_ge(s_order, 1)
            for k in range(AT.step_chunks):
                pool.indirect_dma_start(pairs_in_order[:, k, :], None, pairs_dram,
                                        bass.IndirectOffsetOnAxis(order_i[:, k:k + 1], 0)).then_inc(s_pairs_in, 16)
            pool.wait_ge(s_pairs_in, 16 * AT.step_chunks)
            for k in range(AT.step_chunks):
                pool.indirect_dma_start(AT.step_rows[:, k, :], None, AT.rows_dram,
                                        bass.IndirectOffsetOnAxis(pairs_in_order[:, k, 0:1], 0)).then_inc(s_again, 16)

        chain = [0]

        def link(dve, ins):
            chain[0] += 1
            ins.then_inc(s_dve, 1)
            dve.wait_ge(s_dve, chain[0])

        def dve_prepare(dve):
            for T in TABLES:
                dve.memset(T.first, 0)
                dve.memset(T.last, 0)
            dve.memset(src_i, -1).then_inc(s_ends_zero, 1)
            for T in TABLES:
                last = dve.memset(T.ones_steps, 1.0)
            link(dve, last)
            dve.wait_ge(s_iota, 1)
            dve.tensor_copy(iota_s, iota_i)
            dve.tensor_copy(iota_n[:, :], iota_i[:, 0:P])
            for T in TABLES:
                dve.tensor_copy(T.step_id, step_id_i[:, 0:T.step_chunks])
            dve.tensor_scalar(node_mask[:, :], node_id_i, float(N), None, ALU.is_lt)
            for i in range(2):
                dve.tensor_scalar(minus_past[:, i:i + 1], node_id_i[:, 0:1], float(i + 1), -1.0, ALU.is_ge, ALU.mult)
            link(dve, dve.tensor_copy(hist_iota, iota_i[:, 0:P].unsqueeze(2).to_broadcast([P, P, HIST_ROUND])))
            dve_steps(dve, ES)
            dve.wait_ge(s_src, 16)
            dve.tensor_scalar(src_i[:, 1, :], src_i[:, 0, :], SHIFT, None, ALU.arith_shift_right)
            link(dve, dve.tensor_scalar(src_i[:, 0, :], src_i[:, 0, :], P - 1, None, ALU.bitwise_and))
            dve.tensor_copy(src_lo, src_i[:, 0, :])
            link(dve, dve.tensor_copy(src_hi, src_i[:, 1, :]))
            dve_done(dve, ES)
            dve_tiles(dve, ES)
            dve_node_tiles(dve, ES)
            dve_relative(dve, ES)
            dve.wait_ge(s_relt, 1)
            dve.tensor_copy(es_dst.rearrange("p (k s) j -> p k s j", s=P),
                            bank[:, 6:8, :].rearrange("p b (j s) -> p b s j", s=P)).then_inc(s_tab, 1)
            dve_steps(dve, AT)
            dve_done(dve, AT)
            dve_tiles(dve, AT)

        def dve_steps(dve, T):
            dve.wait_ge(s_ends[T.name], n_ends(T))
            dve.tensor_scalar(T.first, T.first, SHIFT, None, ALU.arith_shift_right)
            link(dve, dve.tensor_scalar(T.last, T.last, SHIFT, None, ALU.arith_shift_right))
            dve.scalar_tensor_tensor(out=T.ones_steps[:, :, 1], in0=T.last, scalar=1.0, in1=T.first, op0=ALU.add,
                                     op1=ALU.subtract).then_inc(s_steps, 1)

        def dve_done(dve, T):
            dve.wait_ge(s_incl, T.no + 1)
            link(dve, dve.tensor_copy(T.incl, small(T, 0)))
            for c in range(T.chunks):
                last = dve.tensor_scalar(T.done[:, c, :], iota_s[:, 0:T.steps], T.incl[:, c:c + 1], None, ALU.is_ge)
            last.then_inc(s_done, 1)

        def dve_tiles(dve, T):
            dve.wait_ge(s_tile, T.no + 1)
            sums = small(T, 1)
            dve.tensor_copy(T.off, sums[:, :, 1])
            if T is ES:
                dve.tensor_scalar(T.start_i, sums[:, :, 0], float(T.edges), float(T.last_start), ALU.mult, ALU.min)
            dve.tensor_scalar(T.tile_i, sums[:, :, 0], float(T.rows - 1), None, ALU.min).then_inc(s_tile_i, 1)

        def dve_node_tiles(dve, T):
            dve.wait_ge(s_got[T.name], 16 * T.step_chunks)
            link(dve, dve.tensor_scalar(T.ftile_i, T.step_rows[:, :, T.width - 1], SHIFT, None, ALU.arith_shift_right))
            link(dve, dve.tensor_tensor(T.ftile, T.ftile_i, T.off, ALU.subtract))
            link(dve, dve.tensor_tensor(T.ftile, T.ftile, T.step_id, ALU.add))
            link(dve, dve.tensor_scalar(T.ftile, T.ftile, 0.0, float(NT - 1), ALU.max, ALU.min))

        def dve_relative(dve, T):
            dve.tensor_copy(T.nt_i, T.ftile)
            link(dve, dve.tensor_scalar(T.nt_nodes, T.ftile, float(P), None, ALU.mult))
            for k in range(T.step_chunks):
                rel = T.nt_nodes[:, k:k + 1]
                if T is ES:
                    last = dve.tensor_scalar(T.rel[:, k, :], T.step_rows[:, k, 0:T.edges], rel, None, ALU.subtract)
                else:
                    last = dve.tensor_scalar(T.rel[:, k, :], T.step_rows[:, k, 0:T.edges], -1.0, rel, ALU.mult, ALU.add)
            if T.src:
                last = dve.tensor_copy(src_f, T.step_rows[:, :, T.edges:2 * T.edges])
            last.then_inc(s_rel, 1)

        AHEAD_BANK = 2

        def dve_count_steps(dve):
            dve_node_tiles(dve, AT)
            dve.tensor_copy(pairs[:, :, 0], AT.tile_i)
            dve.tensor_copy(pairs[:, :, 1], AT.ftile).then_inc(s_pairs, 1)
            before = grid[0][:, 0:FULL * AT.step_chunks].rearrange("p (u k) -> p u k", u=FULL)
            link(dve, dve.tensor_scalar(quarter, AT.ftile, 1.0 / UNIT, None, ALU.mult))
            link(dve, dve.tensor_tensor(before, quarter.unsqueeze(1).to_broadcast([P, FULL, AT.step_chunks]),
                                        iota_n[:, 1:UNITS].unsqueeze(2).to_broadcast([P, FULL, AT.step_chunks]), ALU.is_lt))
            dve.tensor_reduce(per_unit[0][:, 0:FULL], before, AX_X, ALU.add).then_inc(s_pairs, 1)

        def pe_count_steps(pe):
            pe.wait_ge(s_pairs, 2)
            pe.matmul(bank[:, AHEAD_BANK, 0:FULL], ones_f[:, :], per_unit[0][:, 0:FULL], start=True, stop=True).then_inc(s_ahead, 1)

        def dve_order_steps(dve):
            first, count, key, rank, start, end, shift = (t[:, 0:FULL] for t in per_unit[1:])
            units = iota_n[:, 0:FULL]

            def rows(a, n=FULL):
                return a.unsqueeze(1).to_broadcast([P, n, FULL])

            def columns(a):
                return a.unsqueeze(2).to_broadcast([P, a.shape[1], FULL])
            less, part = (g[:, 0:FULL * FULL].rearrange("p (u v) -> p u v", u=FULL) for g in grid)
            dve.wait_ge(s_ahead, 1)
            dve.memset(first[:, 0:1], 0.0)
            link(dve, dve.tensor_copy(first[:, 1:FULL], bank[:, AHEAD_BANK, 0:FULL - 1]))
            link(dve, dve.tensor_tensor(count, bank[:, AHEAD_BANK, 0:FULL], first, ALU.subtract))
            link(dve, dve.scalar_tensor_tensor(out=key, in0=count, scalar=float(UNITS), in1=units, op0=ALU.mult, op1=ALU.add))
            link(dve, dve.tensor_tensor(less, rows(key), columns(key), ALU.is_lt))
            dve.tensor_reduce(rank, less, AX_X, ALU.add)
            link(dve, dve.tensor_tensor(part, less, rows(count), ALU.mult))
            link(dve, dve.tensor_reduce(start, part, AX_X, ALU.add))
            dve.tensor_tensor(end, start, count, ALU.add)
            link(dve, dve.tensor_tensor(shift, first, start, ALU.subtract))
            inside, below = (g[:, 0:AT.step_chunks * FULL].rearrange("p (k u) -> p k u", u=FULL) for g in grid)
            n = AT.step_chunks
            dve.tensor_tensor(inside, columns(AT.step_id), rows(start, n), ALU.is_ge)
            link(dve, dve.tensor_tensor(below, columns(AT.step_id), rows(end, n), ALU.is_lt))
            link(dve, dve.tensor_tensor(inside, inside, below, ALU.mult))
            link(dve, dve.tensor_tensor(inside, inside, rows(shift, n), ALU.mult))
            link(dve, dve.tensor_reduce(order_f, inside, AX_X, ALU.add))
            dve.tensor_tensor(order_i, order_f, AT.step_id, ALU.add).then_inc(s_order, 1)
            link(dve, dve.tensor_tensor(less, rows(rank), columns(units), ALU.is_equal))
            link(dve, dve.tensor_tensor(part, less, rows(units), ALU.mult))
            link(dve, dve.tensor_reduce(key, part, AX_X, ALU.add))
            dve.tensor_scalar(unit_base[0:1, 0:FULL], key[0:1, :], float(UNIT), None, ALU.mult).then_inc(s_order, 1)

        def n_ends(T):
            return 16 * (2 * (T.chunks - 1) + 4)

        def small(T, what):
            if what == 0:
                return bank[:, T.no, 0:T.chunks]
            return bank[:, T.no, 16:16 + 2 * T.step_chunks].rearrange("p (k w) -> p k w", w=2)

        QS = 1.0 / float(HD) ** 0.5

        ROW_BANK, W_BANK = 4, 6
        SUM_AT = (384, 448)

        def dve_between(dve, n):
            if n == 0:
                dve.wait_ge(s_wl, 16 * WL_LOADS)
                for l in range(LAYERS):
                    c = cols_l[l]
                    dve.tensor_tensor(raw_pos[l], raw_pos[l], ident[:, :], ALU.add)
                    link(dve, dve.tensor_tensor(c[:, 2:3], c[:, 2:3], c[:, 3:4], ALU.add))
                    for i, k in enumerate((1, 2, 4)):
                        last = dve.tensor_copy(bc_l[l][:, i, :], c[:, k:k + 1].to_broadcast([P, P]))
                    last.then_inc(s_wprep, 1)
                dve.wait_ge(s_again, 16 * AT.step_chunks)
                link(dve, dve.tensor_copy(AT.ftile, pairs_in_order[:, :, 1]))
                dve_relative(dve, AT)
            if n == 1:
                dve.wait_ge(s_relt, 2)
                dve_degree_mean(dve)
                rows = bank[:, ROW_BANK:ROW_BANK + 2, :].rearrange("p b c -> p (b c)")[:, 0:AT.steps]
                dve.tensor_copy(at_negdst[:, :], rows).then_inc(s_tab, 1)
                for l in range(LAYERS):
                    b = bank[:, W_BANK + l, :]
                    dve.wait_ge(s_wmm, 1 + l)
                    dve.tensor_copy(pos_t[l], b[:, 0:P])
                    dve.tensor_scalar(wdeg_bc[l][:, 0:D], b[:, P:P + D], QS, None, ALU.mult)
                    dve.tensor_copy(wdeg_bc[l][:, D:3 * D], b[:, P + D:P + 3 * D]).then_inc(s_wprep, 1)
                dve.wait_ge(s_relt, 3)
                dve_degree_variance(dve)
                dve.tensor_copy(at_src[:, :], rows).then_inc(s_tab, 1)
            if n == 2:
                for l in range(LAYERS):
                    a, c = bank[:, W_BANK + l, 0:3 * D], cols_l[l]
                    dve.wait_ge(s_wmm, 3 + l)
                    dve.tensor_copy(raw_a[l], a)
                    dve.tensor_scalar(w_qkv[l][:, 0:D], a[:, 0:D], c[:, 0:1], QS, ALU.mult, ALU.mult)
                    dve.tensor_scalar(w_qkv[l][:, D:3 * D], a[:, D:3 * D], c[:, 0:1], None, ALU.mult)
                    dve.tensor_tensor(b_up[l][:, :], bank[:, W_BANK + l, 3 * D:3 * D + FF // P], c[:, 7:11], ALU.add).then_inc(s_wprep, 1)
                    dve.tensor_scalar(w_up[l][:, :], w_up[l][:, :], c[:, 5:6], None, ALU.mult)
                for l in range(LAYERS):
                    b = bank[:, W_BANK + l, 0:3 * D]
                    dve.wait_ge(s_wmm, 5 + l)
                    dve.tensor_scalar(bias_rest[l][:, 0:D], b[0:3, 0:D], QS, None, ALU.mult)
                    link(dve, dve.tensor_copy(bias_rest[l][:, D:3 * D], b[0:3, D:3 * D]))
                for i in range(2):
                    for l in range(LAYERS):
                        last = dve.tensor_copy(bias_part[l], bias_rest[l])
                        if i == l == 0:
                            last.then_inc(s_wprep, 1)
                    link(dve, last)
                    for l in range(LAYERS):
                        last = dve.scalar_tensor_tensor(out=bias_rest[l], in0=bias_part[l], scalar=minus_past[0:3, i:i + 1], in1=bias_rest[l],
                                                        op0=ALU.mult, op1=ALU.add)
                    link(dve, last)
                for l in range(LAYERS):
                    dve.tensor_copy(bias_rows[l][:, :], bias_rest[l])
                dve_degree(dve)

        def pe_prepare(pe):
            pe.wait_ge(s_identity, 1)
            for T in TABLES:
                pe.wait_ge(s_steps, T.no + 1)
                last = pe.matmul(small(T, 0), tri, T.ones_steps[:, :, 1], start=True, stop=T.chunks == 1, skip_group_check=True)
                for c in range(T.chunks - 1):
                    last = pe.matmul(small(T, 0)[:, c + 1:], ones_b, T.ones_steps[:, c:c + 1, 1].to_broadcast([P, T.chunks - 1 - c]),
                                     start=False, stop=c == T.chunks - 2, skip_group_check=True)
                last.then_inc(s_incl, 1)
                pe.wait_ge(s_done, T.no + 1)
                for k in range(T.step_chunks):
                    for c in range(T.chunks):
                        last = pe.matmul(small(T, 1)[:, k, :], T.done[:, c, k * P:(k + 1) * P], T.ones_steps[:, c, :],
                                         start=c == 0, stop=c == T.chunks - 1)
                last.then_inc(s_tile, 1)
                if T is ES:
                    pe.wait_ge(s_rel, 1)
                    for k in range(ES.step_chunks):
                        for j in range(ES_SUB):
                            last = pe.transpose(bank[:, 6 + k, j * P:(j + 1) * P],
                                                ES.rel[:, k, :].rearrange("s (p j) -> s p j", j=ES_SUB)[:, :, j], ident[:, :])
                    last.then_inc(s_relt, 1)

        def pe_between(pe, n):
            def table_rows(rows):
                for k in range(AT.step_chunks):
                    last = pe.transpose(bank[:, ROW_BANK + k // 4, k % 4 * P:(k % 4 + 1) * P], rows[:, k, :], ident[:, :])
                last.then_inc(s_relt, 1)

            def degree_sum(i):
                pe.matmul(bank[:, ROW_BANK + 1, SUM_AT[i]:SUM_AT[i] + NT], ones_f[:, :], deg_tmp[:, :], start=True, stop=True)

            if n == 0:
                for l in range(LAYERS):
                    b = bank[:, W_BANK + l, :]
                    pe.wait_ge(s_wprep, 1 + l)
                    pe.transpose(b[:, 0:P], raw_pos[l], ident[:, :])
                    pe.matmul(b[:, P:P + 3 * D], bc_l[l][:, 2, :], raw_qkv[l], start=True, stop=True).then_inc(s_wmm, 1)
                pe.wait_ge(s_degdve, 1)
                degree_sum(0)
                pe.wait_ge(s_rel, 2)
                table_rows(AT.rel)
            if n == 1:
                pe.wait_ge(s_degdve, 2)
                pe.wait_ge(s_tab, 2)
                degree_sum(1)
                table_rows(src_f)
                for l in range(LAYERS):
                    b = bank[:, W_BANK + l, :]
                    pe.wait_ge(s_wprep, 3 + l)
                    pe.matmul(b[:, 0:3 * D], pos_t[l], raw_qkv[l], start=True, stop=True)
                    for k in range(FF // P):
                        last = pe.matmul(b[:, 3 * D + k:3 * D + k + 1], w_up[l][:, k * P:(k + 1) * P], cols_l[l][:, 6:7], start=True, stop=True)
                    last.then_inc(s_wmm, 1)
                pe.wait_ge(s_tab, 3)
            if n == 2:
                for l in range(LAYERS):
                    b = bank[:, W_BANK + l, 0:3 * D]
                    pe.wait_ge(s_wprep, 5 + l)
                    pe.matmul(b, bc_l[l][:, 1, :], raw_qkv[l], start=True, stop=False)
                    pe.matmul(b, ones_f[0:1, :], bqkv_row[l], start=False, stop=False)
                    pe.matmul(b, bc_l[l][:, 0, :], raw_a[l], start=False, stop=True).then_inc(s_wmm, 1)
                pe.wait_ge(s_wprep, 5 + LAYERS)

        def sp_edge_sums(sp):
            sp.wait_ge(s_nt_in["es"], 32)

            def body(i, first):
                _, starts = nc.values_load_multi_w_load_instructions(
                    es_start[0:1, bass.ds(i * 2 * ES_SLOTS, 2 * ES_SLOTS)], engines=(ENGINE.SP,), min_val=0, max_val=E - ES_EDGES,
                    skip_runtime_bounds_check_because=CLAMPED)
                for n in range(2 * ES_SLOTS):
                    if not first:
                        sp.wait_ge(es_summed, (i - 1) * 2 * ES_SLOTS + n + 1)
                    sp.dma_start(es_attr[:, n // ES_SLOTS, n % ES_SLOTS, :, :],
                                 edge_attr[bass.ds(starts[n], ES_EDGES), :].rearrange("(p j) d -> p j d", j=ES_SUB)
                                 ).then_inc(es_in[n], 16)
            body(0, True)
            with sp.Fori(1, ES_BODIES) as i:
                body(i, False)

        STOPS = tuple(ES_BODIES * n // 8 for n in (2, 3, 4))

        def run_rounds(eng, body, between=None):
            body(0, True, False)
            stops = (1,) + (STOPS if between else ()) + (ES_BODIES - 1,)
            for n, (lo, hi) in enumerate(zip(stops, stops[1:])):
                if n:
                    between(n - 1)
                with eng.Fori(lo, hi) as i:
                    body(i, False, False)
            body(ES_BODIES - 1, False, True)

        def act_edge_sums(act):
            act.wait_ge(s_tab, 1)

            def build(m, h, first):
                before = m * ACT_SLOTS
                for n in range(ACT_SLOTS):
                    if not first:
                        act.wait_ge(es_sel_act, before + n + 1 - ACT_SLOTS)
                    for j in range(ES_SUB):
                        last = act.activation(es_dist[:, n, j, :], iota_n[:, :], ACT.Abs, scale=-1.0,
                                              bias=es_dst[:, bass.ds(m * ES_SLOTS + DVE_SLOTS + n, 1), j])
                    last.then_inc(es_dist_ready, 1)
                for n in range(ACT_SLOTS):
                    s = DVE_SLOTS + n
                    act.wait_ge(es_dist_ready, before + n + 1)
                    if not (isinstance(m, int) and m < 2):
                        act.wait_ge(es_summed, (m - 2) * ES_SLOTS + s + 1)
                    act.activation(es_sel[:, h, s, :, :], es_dist[:, n, :, :], ACT.Relu, scale=-1.0, bias=1.0).then_inc(es_sel_act, 1)

            def body(i, first, last):
                for h in range(2):
                    build(i * 2 + h, h, first and h == 0)
            run_rounds(act, body)

        def pe_edge_sums(pe):
            def body(i, first, last_body):
                for h in range(2):
                    m = i * 2 + h
                    for s in range(ES_SLOTS):
                        pe.wait_ge(es_in[h * ES_SLOTS + s], 16 * (i + 1))
                        if s < DVE_SLOTS:
                            pe.wait_ge(es_sel_dve, m * DVE_SLOTS + s + 1)
                        else:
                            pe.wait_ge(es_sel_act, m * ACT_SLOTS + s - DVE_SLOTS + 1)
                        if not (first and h == 0):
                            pe.wait_ge(es_added, (m - 1) * ES_SLOTS + s + 1)
                        for j in range(ES_SUB):
                            last = pe.matmul(bank[:, 4 + s, 0:D], es_sel[:, h, s, j, :], es_attr[:, h, s, j, :],
                                             start=j == 0, stop=j == ES_SUB - 1)
                        last.then_inc(es_summed, 1)
                    pe.wait_ge(hist_oh, m + 1)
                    for c in range(HIST_ROUND):
                        last = pe.matmul(bank[:, 0, 0:NT], oh_lo[h][:, :, c], oh_hi[h][:, :, c], start=first and h == 0 and c == 0,
                                         stop=last_body and h == 1 and c == HIST_ROUND - 1, skip_group_check=True)
                    last.then_inc(hist_mm, 1)

            def between(n):
                if n == 1:
                    pe_count_steps(pe)
            run_rounds(pe, body, between)

        def dve_edge_sums(dve):
            dve.wait_ge(s_nt_in["es"], 32)
            dve.wait_ge(s_tab, 1)
            dve.wait_ge(s_agg, 1)

            def one_hots(m, h, buf, parts, codes):
                return dve.tensor_tensor(buf[h], hist_iota[0:HIST_ROWS, 0:parts, :],
                                         codes[:, bass.ds(m * HIST_ROUND, HIST_ROUND)].unsqueeze(1)
                                         .to_broadcast([HIST_ROWS, parts, HIST_ROUND]), ALU.is_equal)

            def select(m, h, s):
                if not (isinstance(m, int) and m < 2):
                    dve.wait_ge(es_summed, (m - 2) * ES_SLOTS + s + 1)
                dve.tensor_tensor(es_sel[:, h, s, :, :], iota_n[:, :].unsqueeze(1).to_broadcast([P, ES_SUB, P]),
                                  es_dst[:, bass.ds(m * ES_SLOTS + s, 1), :].rearrange("p s j -> p (s j)").unsqueeze(2)
                                  .to_broadcast([P, ES_SUB, P]), ALU.is_equal).then_inc(es_sel_dve, 1)

            def body(i, first, last):
                _, tiles = nc.values_load_multi_w_load_instructions(
                    es_nt[0:1, bass.ds(i * 2 * ES_SLOTS, 2 * ES_SLOTS)], engines=(ENGINE.DVE,), min_val=0, max_val=NT - 1,
                    skip_runtime_bounds_check_because=CLAMPED)

                def add(m, h, s):
                    dve.wait_ge(es_summed, m * ES_SLOTS + s + 1)
                    if not (first and h == 0 and s == 0):
                        dve.wait_ge(es_added, m * ES_SLOTS + s)
                    a = agg[:, bass.ds(tiles[h * ES_SLOTS + s], 1), 0:D].rearrange("p t d -> p (t d)")
                    dve.tensor_tensor(a, bank[:, 4 + s, 0:D], a, ALU.add).then_inc(es_added, 1)

                for h in range(2):
                    m, ahead = i * 2 + h, not (last and h == 1)
                    if ahead:
                        if not (first and h == 0):
                            dve.wait_ge(hist_mm, m)
                        one_hots(m + 1, 1 - h, oh_lo, P, src_lo)
                    add(m, h, 0)
                    if ahead:
                        one_hots(m + 1, 1 - h, oh_hi, NT, src_hi).then_inc(hist_oh, 1)
                    add(m, h, 1)
                    for s in range(2):
                        if ahead and s < DVE_SLOTS:
                            select(m + 1, 1 - h, s)
                        add(m, h, 2 + s)
            one_hots(0, 0, oh_lo, P, src_lo)
            one_hots(0, 0, oh_hi, NT, src_hi).then_inc(hist_oh, 1)
            for s in range(DVE_SLOTS):
                select(0, 0, s)

            def between(n):
                if n == 0:
                    dve_count_steps(dve)
                if n == 2:
                    dve_order_steps(dve)
            run_rounds(dve, body, between)
            dve.wait_ge(hist_mm, ES_ROUNDS)
            link(dve, dve.tensor_scalar(deg[:, :], bank[:, 0, 0:NT], 1.0, None, ALU.add))
            dve.tensor_tensor(deg_tmp[:, :], deg[:, :], node_mask[:, :], ALU.mult).then_inc(s_degdve, 1)

        def dve_degree_mean(dve):
            link(dve, dve.tensor_reduce(stat[:, 0:1], bank[:, ROW_BANK + 1, SUM_AT[0]:SUM_AT[0] + NT], AX_X, ALU.add))
            link(dve, dve.tensor_scalar(stat[:, 1:2], stat[:, 0:1], 1.0 / N, None, ALU.mult))
            link(dve, dve.tensor_scalar(deg[:, :], deg[:, :], stat[:, 1:2], None, ALU.subtract))
            link(dve, dve.tensor_tensor(deg[:, :], deg[:, :], node_mask[:, :], ALU.mult))
            dve.tensor_tensor(deg_tmp[:, :], deg[:, :], deg[:, :], ALU.mult).then_inc(s_degdve, 1)

        def dve_degree_variance(dve):
            link(dve, dve.tensor_reduce(stat[:, 2:3], bank[:, ROW_BANK + 1, SUM_AT[1]:SUM_AT[1] + NT], AX_X, ALU.add))
            dve.tensor_scalar(stat[:, 3:4], stat[:, 2:3], 1.0 / (N - 1), None, ALU.mult).then_inc(s_degdve, 1)

        def dve_degree(dve):
            dve.wait_ge(s_degpow, 2)
            link(dve, dve.tensor_scalar(stat[:, 5:6], stat[:, 5:6], 1e-6, None, ALU.add))
            link(dve, dve.reciprocal(stat[:, 6:7], stat[:, 5:6]))
            dve.tensor_scalar(deg[:, :], deg[:, :], stat[:, 6:7], None, ALU.mult).then_inc(s_wprep, 1)

        def pool_degree(pool):
            pool.memset(stat[:, 4:5], 0.5).then_inc(s_degpow, 1)
            pool.wait_ge(s_degdve, 3)
            pool.wait_ge(s_degpow, 1)
            pool.tensor_tensor(stat[:, 5:6], stat[:, 3:4], stat[:, 4:5], ALU.pow).then_inc(s_degpow, 1)

        def norm_steps(k):
            return (f"bn{k}", f"sums{k}", f"halves{k}", f"var{k}")

        def rstd_steps(k):
            return (f"rstd{k}", f"shift{k}")

        def each(name, n):
            return tuple(f"{name}{k}" for k in range(n))

        SELF = ("prod", "logit", "number", "clip", "att", "self")

        def steps_of(who, t):
            return {
                "pe": ("aggt", "zt", "h1", "h2", "o", "xt") + each("qkv", t),
                "act": ("z0", "aggt_sb", "zt_sb", "h1_sb", "h2_sb", "z1", "z2", "z3", "xt_sb", "exp"),
                "dve": norm_steps(0) + ("o",) + norm_steps(1) + norm_steps(2) + norm_steps(3) + each("qkv", t) + SELF,
                "pool": rstd_steps(0) + ("xs",) + rstd_steps(1) + ("zw", "x1") + rstd_steps(2) + rstd_steps(3),
            }[who]

        TRANSFERS = {"loaded": 2, "saved": 1, "kept": 1, "out": 2}
        step_sem = {(who, b): sem(f"{who}_unit{b}") for who in ("pe", "act", "dve", "pool") for b in range(BUFS)}
        move_sem = {(name, b): sem(f"rows_{name}{b}") for name in TRANSFERS for b in range(BUFS)}

        def unit_tiles(n):
            return min(UNIT, NT - n * UNIT)

        class Unit:

            def __init__(self, n, i=0):
                self.b, self.t = n % BUFS, unit_tiles(n) if isinstance(i, int) else UNIT
                self.before = n // BUFS + i
                self.base = (n + i * BUFS) * UNIT
                self.again = n >= BUFS
                self.cols = self.t * P

            def nodes(self, buf, lo=0, hi=D):
                return buf[:, bass.ds(self.base, self.t), lo:hi]

            def rows(self, d):
                if d.shape[0] == N and isinstance(self.base, int) and self.base == NT - 1:
                    return d[(NT - 1) * P:N, :].rearrange("(t p) c -> p t c", t=1), LAST_ROWS
                return d[bass.ds(self.base * P, self.t * P), :].rearrange("(t p) c -> p t c", p=P), P

        def unit_sem(who, u):
            return step_sem[who, u.b]

        def done(who, step, u, back=0):
            t = UNIT if back else u.t
            return step_sem[who, u.b], len(steps_of(who, UNIT)) * (u.before - back) + steps_of(who, t).index(step) + 1

        def moved(name, u, back=0):
            return move_sem[name, u.b], 16 * TRANSFERS[name] * (u.before - back + 1)

        def run_units(eng, step, between=None):
            wide = 4 + (eng is nc.sync)

            def at(n, i=0):
                return [Unit(n - k, i) if not isinstance(i, int) or 0 <= n - k < UNITS else None for k in range(wide)]
            rounds = (UNITS - 1 - BUFS) // BUFS
            for n in range(BUFS):
                step(*at(n))
                if between is not None:
                    between(eng, n)
            with eng.Fori(0, rounds) as i:
                for n in range(BUFS, 2 * BUFS):
                    step(*at(n, i))
            for n in range(BUFS * (1 + rounds), UNITS + wide - 1):
                step(*at(n))

        def dense_done(eng):
            for b in range(BUFS):
                units = range(b, UNITS, BUFS)
                for who in ("pe", "act", "dve", "pool"):
                    eng.wait_ge(step_sem[who, b], sum(len(steps_of(who, unit_tiles(n))) for n in units))
                for name, n in TRANSFERS.items():
                    eng.wait_ge(move_sem[name, b], 16 * n * len(units))

        def sp_between(sp, n):
            if n == 3:
                sp_table(sp, AT)

        def sp_dense(sp):
            def load(u):
                b, t = u.b, u.t
                if u.again:
                    sp.wait_ge(*done("pool", "x1", u, 1))
                rows, p = u.rows(x)
                sp.dma_start(xb[b][0:p, 0:t, :], rows).then_inc(move_sem["loaded", b], 16)
                if u.again:
                    sp.wait_ge(*done("pe", "aggt", u, 1))
                sp.dma_start(agg_s[b][:, 0:t, :], u.nodes(agg)).then_inc(move_sem["loaded", b], 16)

            def project(u):
                sp.wait_ge(*done("dve", f"qkv{u.t - 1}", u))
                sp.sem_inc(Z.turn, 1)
                sp.dma_start(u.nodes(q_all), qkv[u.b][:, 0:u.t, 0:D]).then_inc(move_sem["out", u.b], 16)
                sp.dma_start(u.rows(kv_dram[0])[0], qkv[u.b][:, 0:u.t, D:3 * D]).then_inc(move_sem["out", u.b], 16)

            def step(a, _, __, d, e):
                if a:
                    load(a)
                if d:
                    sp.wait_ge(*done("pool", "x1", d))
                    sp.dma_start(d.rows(x1_dram)[0], xo[d.b][:, 0:d.t, :]).then_inc(move_sem["saved", d.b], 16)
                    sp.wait_ge(*done("act", "z2", d))
                    sp.dma_start(d.nodes(xcur), xob[d.b][:, 0:d.t, :]).then_inc(move_sem["kept", d.b], 16)
                if e:
                    project(e)
            return step

        def pool_between(pool, n):
            if n == 2:
                pool_degree(pool)

        def pool_dense(pool):
            def rstd(u, k):
                neg_mean, _, _, var_eps, factor, shift = stat_rows(u)
                pool.wait_ge(*done("dve", f"var{k}", u))
                pool.tensor_tensor(factor, var_eps, half_neg[:, 0:u.t], ALU.pow).then_inc(unit_sem("pool", u), 1)
                pool.wait_ge(*done("pool", f"rstd{k}", u))
                pool.tensor_tensor(shift, factor, neg_mean, ALU.mult).then_inc(unit_sem("pool", u), 1)

            def add_row(u, o, a, row):
                pool.tensor_tensor(o[u.b][:, 0:u.t, :], a[u.b][:, 0:u.t, :], row.to_broadcast([P, u.t, D]), ALU.add
                                   ).then_inc(unit_sem("pool", u), 1)

            def mlp_step(a, c, d, e):
                if d:
                    pool.wait_ge(*done("pool", "zw", d))
                    pool.tensor_tensor(xo[d.b][:, 0:d.t, :], z[d.b][:, 0:d.t, :], xb[d.b][:, 0:d.t, :], ALU.add
                                       ).then_inc(unit_sem("pool", d), 1)
                if a:
                    rstd(a, 0)
                if d:
                    rstd(d, 2)
                if c:
                    pool.wait_ge(*done("act", "z0", c))
                    add_row(c, xb, xb, rows_0[:, 2:3, :])
                    rstd(c, 1)
                if d:
                    rstd(d, 3)
                if c:
                    pool.wait_ge(*done("act", "z1", c))
                    pool.tensor_tensor(z[c.b][:, 0:c.t, :], z[c.b][:, 0:c.t, :], rows_0[:, 1:2, :].to_broadcast([P, c.t, D]), ALU.mult
                                       ).then_inc(unit_sem("pool", c), 1)

            return mlp_step

        def pe_dense(pe):
            def transposes(u, rows, side):
                for t in range(u.t):
                    last = pe.transpose(bank[:, 2 * u.b + side, t * P:(t + 1) * P], rows[u.b][:, t, :], ident[:, :])
                last.then_inc(unit_sem("pe", u), 1)

            def product(u, side, w, act_rows, start=True, stop=True):
                return pe.matmul(bank[:, 2 * u.b + side, 0:u.cols], w, act_rows[u.b][:, 0:u.cols], start=start, stop=stop)

            def node_product(u, side, act_rows, w):
                for t in range(u.t):
                    last = pe.matmul(bank[:, 2 * u.b + side, t * P:(t + 1) * P], act_rows[u.b][:, t * P:(t + 1) * P], w,
                                     start=True, stop=True)
                last.then_inc(unit_sem("pe", u), 1)

            def project(u, tiles):
                for t in tiles:
                    if t >= u.t:
                        continue
                    if t >= 2:
                        pe.wait_ge(*done("dve", f"qkv{t - 2}", u))
                    o = bank[:, 2 * u.b + t % 2, 0:3 * D]
                    pe.matmul(o, t_sb[u.b][:, t * P:(t + 1) * P], w_qkv[0][:, :], start=True, stop=False)
                    pe.matmul(o, ones_3[:, :], bias_rows[0][:, :], start=False, stop=True).then_inc(unit_sem("pe", u), 1)

            def free(u):
                if u.again:
                    pe.wait_ge(*done("dve", "self", u, 1))

            def mlp_step(a, c, d, e):
                if c:
                    pe.wait_ge(*done("act", "zt_sb", c))
                    product(c, 0, w1_0[:, 0, :], t_sb, stop=False)
                    product(c, 0, w1_0[:, 1, :], agg_t, start=False).then_inc(unit_sem("pe", c), 1)
                    pe.wait_ge(*done("act", "h1_sb", c))
                    product(c, 1, w2_0[:, :], h1_t).then_inc(unit_sem("pe", c), 1)
                if a:
                    free(a)
                    pe.wait_ge(*moved("loaded", a))
                    transposes(a, agg_s, 1)
                if e and isinstance(e.base, int) and e.base == 0:
                    pe.wait_ge(s_wprep, 6 + LAYERS)
                if e:
                    pe.wait_ge(*done("act", "z3", e))
                    transposes(e, z, 1)
                if c:
                    pe.wait_ge(*done("act", "h2_sb", c))
                    node_product(c, 0, h2_t, w3_0[:, :])
                if e:
                    pe.wait_ge(*done("act", "xt_sb", e))
                    project(e, (0, 1))
                if a:
                    pe.wait_ge(*done("act", "z0", a))
                    transposes(a, z, 0)
                if e:
                    project(e, (2, 3))

            return mlp_step

        def act_dense(act):
            def move(u, side, dest, func=ACT.Copy, **kw):
                act.activation(dest[:, 0:u.cols], bank[:, 2 * u.b + side, 0:u.cols], func, **kw).then_inc(unit_sem("act", u), 1)

            def normalise(u, k, rows, dest, func=ACT.Identity):
                _, _, _, _, factor, shift = stat_rows(u)
                act.wait_ge(*done("pool", f"shift{k}", u))
                for t in range(u.t):
                    last = act.activation(dest[u.b][:, t, :], rows[u.b][:, t, :], func, bias=shift[:, t:t + 1], scale=factor[:, t:t + 1])
                last.then_inc(unit_sem("act", u), 1)

            def exp(u):
                act.wait_ge(*done("dve", "att", u))
                act.activation(u.nodes(agg, D, MW), att_s[u.b][:, 2, 0:u.t * HEADS].rearrange("p (t h) -> p t h", h=HEADS),
                               ACT.Exp).then_inc(unit_sem("act", u), 1)

            def free(u):
                if u.again:
                    for name in TRANSFERS:
                        if name != "loaded":
                            act.wait_ge(*moved(name, u, 1))

            def mlp_step(a, c, d, e):
                if c:
                    act.wait_ge(*done("pe", "h2", c))
                    move(c, 1, h2_t[c.b], ACT.Relu, bias=cols_0[:, 1:2])
                if e:
                    act.wait_ge(*done("pe", "xt", e))
                    move(e, 1, t_sb[e.b])
                if a:
                    normalise(a, 0, xb, z, ACT.Relu)
                    free(a)
                    act.wait_ge(*done("pe", "aggt", a))
                    move(a, 1, agg_t[a.b])
                if d:
                    normalise(d, 2, xo, xob, ACT.Relu)
                if a:
                    act.wait_ge(*done("pe", "zt", a))
                    move(a, 0, t_sb[a.b])
                if c:
                    normalise(c, 1, xob, z)
                if d:
                    normalise(d, 3, xob, z)
                if a:
                    act.wait_ge(*done("pe", "h1", a))
                    move(a, 0, h1_t[a.b], ACT.Relu, bias=cols_0[:, 0:1])
                if e:
                    exp(e)

            return mlp_step

        def dve_dense(dve):
            def count(u, ins):
                ins.then_inc(unit_sem("dve", u), 1)

            def stats(u, k, rows):
                neg_mean, gap, spread2, var_eps, _, _ = stat_rows(u)
                halves = bn[u.b][:, 0:u.t, :]
                for t in range(u.t):
                    last = dve.bn_stats(bn[u.b][:, t, :], rows[u.b][:, t, :])
                count(u, last)
                dve.wait_ge(*done("dve", f"bn{k}", u))
                dve.tensor_tensor(neg_mean, halves[:, :, 1], halves[:, :, 4], ALU.add)
                dve.tensor_tensor(gap, halves[:, :, 1], halves[:, :, 4], ALU.subtract)
                count(u, dve.tensor_tensor(spread2, halves[:, :, 2], halves[:, :, 5], ALU.add))
                dve.wait_ge(*done("dve", f"sums{k}", u))
                dve.tensor_scalar(neg_mean, neg_mean, -0.5, None, ALU.mult)
                dve.tensor_tensor(gap, gap, gap, ALU.mult)
                count(u, dve.tensor_scalar(spread2, spread2, 1.0 / D, EPS, ALU.mult, ALU.add))
                dve.wait_ge(*done("dve", f"halves{k}", u))
                count(u, dve.scalar_tensor_tensor(out=var_eps, in0=gap, scalar=0.25, in1=spread2, op0=ALU.mult, op1=ALU.add))

            def from_bank(u):
                return bank[:, 2 * u.b, 0:u.cols].rearrange("p (t d) -> p t d", d=D)

            def project(u, tiles):
                for t in tiles:
                    if t >= u.t:
                        continue
                    dve.wait_ge(*done("pe", f"qkv{t}", u))
                    count(u, dve.scalar_tensor_tensor(out=qkv[u.b][:, t, :], in0=wdeg_bc[0][:, :], scalar=deg[:, bass.ds(u.base + t, 1)],
                                                      in1=bank[:, 2 * u.b + t % 2, 0:3 * D], op0=ALU.mult, op1=ALU.add))

            def loop_logits(u):
                rows, n = qkv[u.b][:, 0:u.t, :], u.t * HEADS
                raw, number, logit = (att_s[u.b][:, i, 0:n] for i in range(3))
                dve.wait_ge(*done("dve", f"qkv{u.t - 1}", u))
                count(u, dve.tensor_tensor(z[u.b][:, 0:u.t, :], rows[:, :, 0:D], rows[:, :, D:2 * D], ALU.mult))
                dve.wait_ge(*done("dve", "prod", u))
                count(u, dve.tensor_reduce(raw, z[u.b][:, 0:u.t, :].rearrange("p t (h c) -> p (t h) c", h=HEADS), AX_X, ALU.add))
                dve.wait_ge(*done("dve", "logit", u))
                count(u, dve.tensor_tensor(number, raw, raw, ALU.is_equal))
                count(u, dve.tensor_scalar(logit, raw, -CLIP, CLIP, ALU.max, ALU.min))
                dve.wait_ge(*done("dve", "clip", u))
                count(u, dve.tensor_tensor(logit, logit, number, ALU.mult))

            def loop_messages(u):
                rows = qkv[u.b][:, 0:u.t, :]
                dve.wait_ge(*done("act", "exp", u))
                count(u, dve.tensor_tensor(u.nodes(agg).rearrange("p t (h c) -> p t h c", h=HEADS),
                                           rows[:, :, 2 * D:3 * D].rearrange("p t (h c) -> p t h c", h=HEADS),
                                           u.nodes(agg, D, MW).unsqueeze(3).to_broadcast([P, u.t, HEADS, HD]), ALU.mult))

            def mlp_step(a, c, d, e):
                if a:
                    dve.wait_ge(*moved("loaded", a))
                    stats(a, 0, xb)
                if d:
                    dve.wait_ge(*done("pool", "x1", d))
                    stats(d, 2, xo)
                if c:
                    dve.wait_ge(*done("pe", "o", c))
                    count(c, dve.tensor_tensor(xob[c.b][:, 0:c.t, :], from_bank(c), rows_0[:, 0:1, :].to_broadcast([P, c.t, D]), ALU.add))
                    dve.wait_ge(*done("dve", "o", c))
                    stats(c, 1, xob)
                if e:
                    project(e, (0, 1))
                if d:
                    dve.wait_ge(*done("act", "z2", d))
                    stats(d, 3, xob)
                if e:
                    project(e, (2, 3))
                    loop_logits(e)
                    loop_messages(e)

            return mlp_step

        def update_steps(who, t, part):
            return {
                "pe": (("aggt", "o", "zt") + each("up", UPS) + ("down",), ("xt",) + each("qkv", t)),
                "act": (("aggt_sb", "x", "z0", "zt_sb") + each("up_sb", UPS) + ("y",), ("z1", "xt_sb", "exp")),
                "dve": (("guard", "inverse", "an") + norm_steps(0), norm_steps(1) + each("qkv", t) + SELF[:-1] + ("weights", "self")),
                "pool": (rstd_steps(0), rstd_steps(1)),
            }[who][part]

        SLOT = {"x1": 8, "sums": UPDATE_SLOT,
                "aggt": 5, "aggt_sb": 6, "o": 6, "x": 7, "stats0": 8, "rstd0": 13, "z0": 12,
                "zt": 12, "zt_sb": 13, "up_a": 13, "up_sb_a": 14, "up_b": 14, "up_sb_b": 14,
                "down0": 15, "down1": 15, "down2": 16, "down3": 16, "y": 16, "keep": 20,
                "stats1": 17, "rstd1": 20, "z1": 19, "xt": 24, "xt_sb": 24,
                "qkv_a": 24, "qkv_add_a": 25, "qkv_b": 25, "qkv_add_b": 27,
                "logits": 29, "exp": 29, "messages": 30, "send": 31}

        UPDATE_TRANSFERS = {"x1": (0, 1), "kept": (1, 1), "out": (2, 0)}
        UPDATE_UNITS, UPDATE_TILES, UPDATE_BANKS = (FULL - 1, 1, 1), (UNIT, UNIT, 1), ((6, 7), (0, 1), (2, 3))
        WHO, SETS, PARTS = ("pe", "act", "dve", "pool"), range(3), range(2)
        update_sem = {(who, part, b): sem(f"{who}_{('update', 'project')[part]}{b}") for who in WHO for part in PARTS for b in SETS}
        update_move = {(name, b): sem(f"update_{name}{b}") for name in UPDATE_TRANSFERS for b in SETS}

        class Updated:

            def __init__(self, l, j, base, b=0):
                self.l, self.j, self.base, self.b = l, j, base, b
                self.t = UPDATE_TILES[b]
                self.cols = self.t * P
                self.again = not (isinstance(j, int) and j == 0)
                self.more = l + 1 < LAYERS

            def __getitem__(self, name):
                return upd[self.b][name]

            def bank(self, side):
                return bank[:, UPDATE_BANKS[self.b][side], 0:self.cols]

            def nodes(self, buf, lo=0, hi=D):
                return buf[:, bass.ds(self.base, self.t), lo:hi]

            def degree(self):
                return deg[:, bass.ds(self.base, self.t)]

            def rows(self, d):
                if self.t == 1:
                    return d[(NT - 1) * P:min(d.shape[0], NPAD), :].rearrange("(t p) c -> p t c", t=1)
                return d[0:FULL * UNIT * P, :].rearrange("(t p) c -> p t c", p=P)[:, bass.ds(self.base, UNIT), :]

            def atts(self, i):
                return att_s[self.b][:, i, 0:self.t * HEADS]

            def stats(self, k):
                b = BUFS - 1 if k == 1 and self.b == 0 else self.b
                return [norm_stat[b][:, i, 0:self.t] for i in range(6)], bn[b][:, 0:self.t, :]

            def sem(self, who, part=0):
                return update_sem[who, part, self.b]

            def done(self, who, step):
                part = int(step not in update_steps(who, self.t, 0))
                steps = update_steps(who, self.t, part)
                return self.sem(who, part), len(steps) * self.j + steps.index(step) + 1 + update_count(who, part, self.b, self.l)

            def moved(self, name, back=0):
                return (update_move[name, self.b],
                        16 * UPDATE_TRANSFERS[name][self.l] * (self.j - back + 1) + update_moves(name, self.b, self.l))

        def update_count(who, part, b, layers):
            return len(update_steps(who, UPDATE_TILES[b], part)) * UPDATE_UNITS[b] * (min(layers, LAYERS - 1) if part else layers)

        def update_moves(name, b, layers):
            return 16 * sum(UPDATE_TRANSFERS[name][:layers]) * UPDATE_UNITS[b]

        def u_before(u):
            return Updated(u.l, u.j - 1, None, u.b)

        class Updates:

            def __init__(self, eng, l, stages):
                self.eng, self.l, self.stages = eng, l, stages
                self.engine = {nc.vector: ENGINE.DVE, nc.sync: ENGINE.SP, nc.tensor: ENGINE.PE}.get(eng)

            def load(self, j, n):
                if self.engine is None:
                    return [None] * n
                _, bases = nc.values_load_multi_w_load_instructions(
                    unit_base[0:1, bass.ds(j, n)], engines=(self.engine,), min_val=0,
                    max_val=NT - 1 - UNIT, skip_runtime_bounds_check_because=CLAMPED)
                return list(bases)

            def __call__(self, i, r):
                counted = not isinstance(i, int)
                begins, ends = counted or i >= LAG, counted or i > LAG
                if r == 0 and ends:
                    self.bases = self.load(i - LAG - 1, 2)
                elif r == 0 and begins:
                    self.bases = [None] + self.load(i - LAG, 1)
                if ends:
                    self.stages(QUADS + r, Updated(self.l, i - LAG - 1, self.bases[0]))
                if begins:
                    self.stages(r, Updated(self.l, i - LAG, self.bases[1]))

            def rest(self):
                bases = self.load(FULL - 2, 2)
                before = Updated(self.l, FULL - 2, bases[0])
                rest = Updated(self.l, 0, bases[1], 1), Updated(self.l, 0, NT - 1, 2)
                self.eng.wait_ge(Z.added, (self.l + 1) * AT_STEPS)
                for r in range(-UPDATE_SLOT, 2 * QUADS):
                    if 0 <= r < QUADS:
                        self.stages(QUADS + r, before)
                    if r + UPDATE_SLOT < 2 * QUADS:
                        for u in rest:
                            self.stages(r + UPDATE_SLOT, u)
        assert AT_BODIES - LAG == FULL - 1

        def update_done(eng, l):
            for b in SETS:
                for who in WHO:
                    for part in PARTS:
                        if part == 0 or l + 1 < LAYERS:
                            eng.wait_ge(update_sem[who, part, b], update_count(who, part, b, l + 1))
                for name in UPDATE_TRANSFERS:
                    if UPDATE_TRANSFERS[name][l]:
                        eng.wait_ge(update_move[name, b], update_moves(name, b, l + 1))

        def sp_update(sp, l):
            def stages(r, u):
                if r == SLOT["x1"] and not u.more:
                    if u.again:
                        sp.wait_ge(*u_before(u).done("pe", "down"))
                        sp.sem_inc(Z.turn, 1)
                    sp.dma_start(u["x1"], u.rows(x1_dram)).then_inc(update_move["x1", u.b], 16)
                if r == SLOT["keep"]:
                    sp.wait_ge(*u.done("act", "y"))
                    sp.sem_inc(Z.turn, 1)
                    o = u.nodes(xcur) if u.more else u.rows(out)
                    sp.dma_start(o, u["y"][0:o.shape[0], :, :]).then_inc(update_move["kept", u.b], 16)
                if r == SLOT["send"] and u.more:
                    sp.wait_ge(*u.done("dve", f"qkv{u.t - 1}"))
                    sp.sem_inc(Z.turn, 1)
                    sp.dma_start(u.rows(kv_dram[l + 1]), u["qkv"][:, :, D:3 * D]).then_inc(update_move["out", u.b], 16)
                    sp.dma_start(u.nodes(q_all), u["qkv"][:, :, 0:D]).then_inc(update_move["out", u.b], 16)
            return stages

        def pool_update(pool, l):
            def rstd(u, k):
                neg_mean, _, _, var_eps, factor, shift = u.stats(k)[0]
                pool.wait_ge(*u.done("dve", f"var{k}"))
                pool.tensor_tensor(factor, var_eps, half_neg[:, 0:u.t], ALU.pow).then_inc(u.sem("pool", k), 1)
                pool.wait_ge(*u.done("pool", f"rstd{k}"))
                pool.tensor_tensor(shift, factor, neg_mean, ALU.mult).then_inc(u.sem("pool", k), 1)

            def stages(r, u):
                if r == SLOT["rstd0"]:
                    rstd(u, 0)
                if r == SLOT["rstd1"] and u.more:
                    rstd(u, 1)
            return stages

        def pe_update(pe, l):
            def transposes(u, rows, part):
                for t in range(u.t):
                    last = pe.transpose(u.bank(0)[:, t * P:(t + 1) * P], rows[:, t, :], ident[:, :])
                last.then_inc(u.sem("pe", part), 1)

            def node_product(u, tiles, weights, acts, row, *plus):
                last = None
                for t in tiles:
                    o = u.bank(1)[:, t * P:(t + 1) * P]
                    for k, (w, act) in enumerate(zip(weights, acts)):
                        pe.matmul(o, act[:, t * P:(t + 1) * P], w, start=k == 0, stop=False)
                    last = pe.matmul(o, ones_f[0:1, :], row, start=False, stop=False)
                    for n, a in enumerate(plus):
                        last = pe.matmul(o, ident[:, :], a[:, t, :], start=False, stop=n == len(plus) - 1)
                return last

            def up(u, chunks):
                for k in chunks:
                    if k >= 2:
                        pe.wait_ge(*u.done("act", f"up_sb{k - 2}"))
                    pe.matmul(u.bank((k + 1) % 2), w_up[l][:, k * P:(k + 1) * P], u["t"], start=True, stop=True).then_inc(u.sem("pe"), 1)

            def down(u, tiles):
                return node_product(u, tiles, [w_down[l][:, k, :] for k in range(UPS)],
                                    [u["hid"][:, k * u.cols:(k + 1) * u.cols] for k in range(UPS)], rows_l[l][0:1, 1, :],
                                    *([u["x"]] if u.more else [u["x"], u["x1"]]))

            def project(u, tiles):
                for t in tiles:
                    if t >= u.t:
                        continue
                    if t >= 2:
                        pe.wait_ge(*u.done("dve", f"qkv{t - 2}"))
                    o = bank[:, UPDATE_BANKS[u.b][(t + 1) % 2], 0:3 * D]
                    pe.matmul(o, u["tn"][:, t * P:(t + 1) * P], w_qkv[l + 1][:, :], start=True, stop=False)
                    pe.matmul(o, ones_3[:, :], bias_rows[l + 1][:, :], start=False, stop=True).then_inc(u.sem("pe", 1), 1)

            def stages(r, u):
                if r == SLOT["aggt"]:
                    pe.wait_ge(*u.done("dve", "an"))
                    transposes(u, u["z"], 0)
                if r == SLOT["o"]:
                    pe.wait_ge(*u.done("act", "aggt_sb"))
                    node_product(u, range(u.t), [w_o[l][:, :]], [u["t"]], rows_l[l][0:1, 0, :], u.nodes(xcur)).then_inc(u.sem("pe"), 1)
                if r == SLOT["zt"]:
                    pe.wait_ge(*u.done("act", "z0"))
                    if u.again and u.more:
                        pe.wait_ge(*u_before(u).done("dve", f"qkv{u.t - 1}"))
                    transposes(u, u["z"], 0)
                if r == SLOT["up_a"]:
                    pe.wait_ge(*u.done("act", "zt_sb"))
                    up(u, (0, 1))
                if r == SLOT["up_b"]:
                    up(u, (2, 3))
                if r == SLOT["down0"]:
                    pe.wait_ge(*u.done("act", f"up_sb{UPS - 1}"))
                    if not u.more:
                        pe.wait_ge(*u.moved("x1"))
                for t in range(u.t):
                    if r == SLOT[f"down{t}"]:
                        last = down(u, (t,))
                        if t == u.t - 1:
                            last.then_inc(u.sem("pe"), 1)
                if u.more:
                    if r == SLOT["xt"]:
                        pe.wait_ge(*u.done("act", "z1"))
                        transposes(u, u["zn"], 1)
                    if r == SLOT["qkv_a"]:
                        pe.wait_ge(*u.done("act", "xt_sb"))
                        project(u, (0, 1))
                    if r == SLOT["qkv_b"]:
                        project(u, (2, 3))
            return stages

        def act_update(act, l):
            def move(u, side, dest, func=ACT.Copy, part=0, **kw):
                act.activation(dest, u.bank(side), func, **kw).then_inc(u.sem("act", part), 1)

            def normalise(u, k, rows, dest):
                _, _, _, _, factor, shift = u.stats(k)[0]
                act.wait_ge(*u.done("pool", f"shift{k}"))
                for t in range(u.t):
                    last = act.activation(dest[:, t, :], rows[:, t, :], ACT.Identity, bias=shift[:, t:t + 1], scale=factor[:, t:t + 1])
                last.then_inc(u.sem("act", k), 1)

            def gelu(u, chunks):
                for k in chunks:
                    act.wait_ge(*u.done("pe", f"up{k}"))
                    move(u, (k + 1) % 2, u["hid"][:, k * u.cols:(k + 1) * u.cols], ACT.Gelu, bias=b_up[l][:, k:k + 1])

            def stages(r, u):
                if r == SLOT["aggt_sb"]:
                    act.wait_ge(*u.done("pe", "aggt"))
                    move(u, 0, u["t"])
                if r == SLOT["x"]:
                    act.wait_ge(*u.done("pe", "o"))
                    move(u, 1, u["x"].rearrange("p t d -> p (t d)"))
                if r == SLOT["z0"]:
                    normalise(u, 0, u["x"], u["z"])
                if r == SLOT["zt_sb"]:
                    act.wait_ge(*u.done("pe", "zt"))
                    move(u, 0, u["t"])
                if r == SLOT["up_sb_a"]:
                    gelu(u, (0, 1))
                if r == SLOT["up_sb_b"]:
                    gelu(u, (2, 3))
                if r == SLOT["y"]:
                    act.wait_ge(*u.done("pe", "down"))
                    if u.again:
                        act.wait_ge(*u.moved("kept", 1))
                        act.sem_inc(Z.turn, 1)
                    move(u, 1, u["y"].rearrange("p t d -> p (t d)"))
                if u.more:
                    if r == SLOT["z1"]:
                        normalise(u, 1, u["y"], u["zn"])
                    if r == SLOT["xt_sb"]:
                        act.wait_ge(*u.done("pe", "xt"))
                        move(u, 0, u["tn"], part=1)
                    if r == SLOT["exp"]:
                        act.wait_ge(*u.done("dve", "att"))
                        act.activation(u.atts(5), u.atts(2), ACT.Exp).then_inc(u.sem("act", 1), 1)
            return stages

        def dve_update(dve, l):
            def count(u, ins, part=1):
                ins.then_inc(u.sem("dve", part), 1)

            def heads(a):
                return a.rearrange("p t (h c) -> p t h c", h=HEADS)

            def per_head(a, u):
                return a.rearrange("p (t h) -> p t h", h=HEADS).unsqueeze(3).to_broadcast([P, u.t, HEADS, HD])

            def stats(u, k, rows):
                (neg_mean, gap, spread2, var_eps, _, _), halves = u.stats(k)
                for t in range(u.t):
                    last = dve.bn_stats(halves[:, t, :], rows[:, t, :])
                count(u, last, k)
                dve.wait_ge(*u.done("dve", f"bn{k}"))
                dve.tensor_tensor(neg_mean, halves[:, :, 1], halves[:, :, 4], ALU.add)
                dve.tensor_tensor(gap, halves[:, :, 1], halves[:, :, 4], ALU.subtract)
                count(u, dve.tensor_tensor(spread2, halves[:, :, 2], halves[:, :, 5], ALU.add), k)
                dve.wait_ge(*u.done("dve", f"sums{k}"))
                dve.tensor_scalar(neg_mean, neg_mean, -0.5, None, ALU.mult)
                dve.tensor_tensor(gap, gap, gap, ALU.mult)
                count(u, dve.tensor_scalar(spread2, spread2, 1.0 / D, EPS, ALU.mult, ALU.add), k)
                dve.wait_ge(*u.done("dve", f"halves{k}"))
                count(u, dve.scalar_tensor_tensor(out=var_eps, in0=gap, scalar=0.25, in1=spread2, op0=ALU.mult, op1=ALU.add), k)

            def project(u, tiles):
                for t in tiles:
                    if t >= u.t:
                        continue
                    dve.wait_ge(*u.done("pe", f"qkv{t}"))
                    count(u, dve.scalar_tensor_tensor(out=u["qkv"][:, t, :], in0=wdeg_bc[l + 1][:, :], scalar=u.degree()[:, t:t + 1],
                                                      in1=bank[:, UPDATE_BANKS[u.b][(t + 1) % 2], 0:3 * D], op0=ALU.mult, op1=ALU.add))

            def loop_logits(u):
                rows = u["qkv"]
                raw, number, logit = (u.atts(i) for i in range(3))
                dve.wait_ge(*u.done("dve", f"qkv{u.t - 1}"))
                count(u, dve.tensor_tensor(u["zn"], rows[:, :, 0:D], rows[:, :, D:2 * D], ALU.mult))
                dve.wait_ge(*u.done("dve", "prod"))
                count(u, dve.tensor_reduce(raw, u["zn"].rearrange("p t (h c) -> p (t h) c", h=HEADS), AX_X, ALU.add))
                dve.wait_ge(*u.done("dve", "logit"))
                count(u, dve.tensor_tensor(number, raw, raw, ALU.is_equal))
                count(u, dve.tensor_scalar(logit, raw, -CLIP, CLIP, ALU.max, ALU.min))
                dve.wait_ge(*u.done("dve", "clip"))
                count(u, dve.tensor_tensor(logit, logit, number, ALU.mult))

            def loop_messages(u):
                dve.wait_ge(*u.done("act", "exp"))
                count(u, dve.tensor_copy(u.nodes(agg, D, MW), u.atts(5).rearrange("p (t h) -> p t h", h=HEADS)))
                count(u, dve.tensor_tensor(heads(u.nodes(agg)), heads(u["qkv"][:, :, 2 * D:3 * D]), per_head(u.atts(5), u), ALU.mult))

            def stages(r, u):
                if u.more:
                    if r == SLOT["qkv_add_a"]:
                        if u.again:
                            dve.wait_ge(*u.moved("out", 1))
                            dve.sem_inc(Z.turn, 1)
                        project(u, (0, 1))
                    if r == SLOT["qkv_add_b"]:
                        project(u, (2, 3))
                    if r == SLOT["logits"]:
                        loop_logits(u)
                    if r == SLOT["messages"]:
                        loop_messages(u)
                if r == SLOT["sums"]:
                    count(u, dve.tensor_scalar(u.atts(3).rearrange("p (t h) -> p t h", h=HEADS), u.nodes(agg, D, MW), SUM_GUARD, None, ALU.add), 0)
                    dve.wait_ge(*u.done("dve", "guard"))
                    count(u, dve.reciprocal(u.atts(4), u.atts(3)), 0)
                    if u.again:
                        dve.wait_ge(*u_before(u).done("pe", "up0"))
                        dve.sem_inc(Z.turn, 1)
                    dve.wait_ge(*u.done("dve", "inverse"))
                    count(u, dve.tensor_tensor(heads(u["z"]), heads(u.nodes(agg)), per_head(u.atts(4), u), ALU.mult), 0)
                if r == SLOT["stats0"]:
                    dve.wait_ge(*u.done("act", "x"))
                    stats(u, 0, u["x"])
                if r == SLOT["stats1"] and u.more:
                    dve.wait_ge(*u.done("act", "y"))
                    stats(u, 1, u["y"])
            return stages

        class Attention:

            def __init__(self):
                self.kv_in = sems("kv_loaded", KV_QUADS)
                self.qw_in = sems("q_loaded", 2)
                self.idx = sem("idx_staged")
                self.turn = sem("gather_turn")
                self.sel = sem("sel_ready")
                self.dist = sem("dist_ready")
                self.selt = sem("selt_ready")
                self.selt_sb = sem("selt_copied")
                self.qe = sem("q_spread")
                self.prod = sem("prod_ready")
                self.att = sem("att_chain")
                self.logit = sem("logits_ready")
                self.ex = sem("exp_ready")
                self.msg = sem("msg_ready")
                self.sum = sem("summed")
                self.added = sem("added")

        Z = Attention()
        ATT_BANK = ((0, 1), (2, 3), 4)

        def sums_of(j):
            return bank[:, ATT_BANK[2] + j // 2, j % 2 * 256:j % 2 * 256 + MW]

        def run_bodies(eng, body):
            for i in range(LAG + 1):
                body(i, i == 0, False)
            with eng.Fori(LAG + 1, AT_BODIES - 1) as i:
                body(i, False, False)
            body(AT_BODIES - 1, False, True)

        def pool_attention(pool, l):
            k0 = l * AT_QUADS
            update = Updates(pool, l, pool_update(pool, l))

            def body(i, first, last):
                for r in range(QUADS):
                    slot = r % (KV_QUADS)
                    k = i * QUADS + r
                    if not (first and r < KV_QUADS):
                        pool.wait_ge(Z.msg, k0 + k - KV_QUADS + 1)
                    half = r * QUAD // KV_SLOTS
                    if slot == 0:
                        pool.wait_ge(Z.idx, (k0 // QUADS + i) * HALVES + half + 1)
                    pool.sem_inc(Z.turn, 1)
                    for j in range(QUAD):
                        n = slot * QUAD + j
                        pool.indirect_dma_start(kv[:, n, :], None, kv_dram[l], bass.IndirectOffsetOnAxis(idx_stage[:, half % 2, n:n + 1], 0)
                                                ).then_inc(Z.kv_in[slot], 16)
                    update(i, r)
            run_bodies(pool, body)
            update.rest()

        def sp_attention(sp, l):
            k0 = l * AT_QUADS
            update = Updates(sp, l, sp_update(sp, l))
            def body(i, first, last):
                for r in range(QUADS):
                    k = i * QUADS + r
                    _, tiles = nc.values_load_multi_w_load_instructions(
                        at_nt[0:1, bass.ds(i * BODY + r * QUAD, QUAD)], engines=(ENGINE.SP,), min_val=0, max_val=NT - 1,
                        skip_runtime_bounds_check_because=CLAMPED)
                    if not (first and r < 2):
                        sp.wait_ge(Z.qe, k0 + k - 1)
                    for j in range(QUAD):
                        sp.dma_start(q_win[:, r % 2, j, :], q_all[:, bass.ds(tiles[j], 1), :].rearrange("p t d -> p (t d)")
                                     ).then_inc(Z.qw_in[r % 2], 16)
                    update(i, r)
            run_bodies(sp, body)
            update.rest()

        def act_attention(act, l):
            k0 = l * AT_QUADS
            update = Updates(act, l, act_update(act, l))
            def select(k, r, step, first):
                if not first:
                    act.wait_ge(Z.sel, (k0 + k))
                for j in range(QUAD):
                    m = act.activation(dist[:, j, :], iota_n[:, :], ACT.Abs, bias=at_negdst[:, bass.ds(step + j, 1)])
                m.then_inc(Z.dist, 1)
                act.wait_ge(Z.dist, k0 + k + 1)
                if not (isinstance(k, int) and k < SEL_SLOTS):
                    act.wait_ge(Z.sum, (k0 + k - SEL_SLOTS + 1) * QUAD)
                act.activation(sel[:, r % SEL_SLOTS, :, :], dist, ACT.Relu, scale=-1.0, bias=1.0).then_inc(Z.sel, 1)

            def copy_t(k, r):
                act.wait_ge(Z.selt, k0 + k + 1)
                if not (isinstance(k, int) and k < 2):
                    act.wait_ge(Z.qe, k0 + k - 1)
                act.activation(sel_t[:, r % 2, :, :], bank[:, ATT_BANK[0][r % 2], :].rearrange("p (j e) -> p j e", j=QUAD),
                               ACT.Copy).then_inc(Z.selt_sb, 1)

            def body(i, first, last):
                for r in range(QUADS):
                    k = i * QUADS + r
                    if not (last and r + 2 >= QUADS):
                        copy_t(k + 2, r + 2)
                    if not (last and r + 3 >= QUADS):
                        select(k + 3, r + 3, (i * QUADS + r + 3) * QUAD, False)
                    act.wait_ge(Z.logit, k0 + k + 1)
                    act.activation(msg[:, r % 2, :, D:MW], att[:, r % 2, 2, :].rearrange("p (j h) -> p j h", j=QUAD),
                                   ACT.Exp).then_inc(Z.ex, 1)
                    update(i, r)
            select(0, 0, 0, True)
            copy_t(0, 0)
            select(1, 1, QUAD, False)
            copy_t(1, 1)
            select(2, 2, 2 * QUAD, False)
            run_bodies(act, body)
            update.rest()

        def pe_attention(pe, l):
            k0 = l * AT_QUADS
            update = Updates(pe, l, pe_update(pe, l))
            def transposes(k, r):
                pe.wait_ge(Z.sel, k0 + k + 1)
                if not (isinstance(k, int) and k < 2):
                    pe.wait_ge(Z.selt_sb, k0 + k - 1)
                for j in range(QUAD):
                    m = pe.transpose(bank[:, ATT_BANK[0][r % 2], j * P:(j + 1) * P], sel[:, r % SEL_SLOTS, j, :], ident[:, :])
                m.then_inc(Z.selt, 1)

            def spread(k, r, i):
                pe.wait_ge(Z.selt_sb, k0 + k + 1)
                pe.wait_ge(Z.qw_in[r % 2], 16 * QUAD * (k0 // 2 + i * (QUADS // 2) + r // 2 + 1))
                if not (isinstance(k, int) and k < 2):
                    pe.wait_ge(Z.prod, k0 + k - 1)
                for j in range(QUAD):
                    m = pe.matmul(bank[:, ATT_BANK[1][r % 2], j * D:(j + 1) * D], sel_t[:, r % 2, j, :], q_win[:, r % 2, j, :],
                                  start=True, stop=True)
                m.then_inc(Z.qe, 1)

            def sums(k, r):
                pe.wait_ge(Z.msg, k0 + k + 1)
                for j in range(QUAD):
                    if j % 2 == 0 and not (isinstance(k, int) and k < 1):
                        pe.wait_ge(Z.added, (k0 + k - 1) * QUAD + j + 2)
                    pe.matmul(sums_of(j), sel[:, r % SEL_SLOTS, j, :], msg[:, r % 2, j, :],
                              start=True, stop=True).then_inc(Z.sum, 1)

            def body(i, first, last):
                for r in range(QUADS):
                    k = i * QUADS + r
                    if not (last and r + 2 >= QUADS):
                        spread(k + 2, r + 2, i)
                    if not (first and r == 0):
                        sums(k - 1, (r - 1) % QUADS)
                    if not (last and r + 3 >= QUADS):
                        transposes(k + 3, r + 3)
                    update(i, r)
            transposes(0, 0)
            spread(0, 0, 0)
            transposes(1, 1)
            spread(1, 1, 0)
            transposes(2, 2)
            run_bodies(pe, body)
            sums(AT_QUADS - 1, QUADS - 1)
            update.rest()

        def dve_attention(dve, l):
            k0 = l * AT_QUADS
            update = Updates(dve, l, dve_update(dve, l))
            def load_tiles(step, n):
                _, tiles = nc.values_load_multi_w_load_instructions(
                    at_nt[0:1, bass.ds(step, n)], engines=(ENGINE.DVE,), min_val=0, max_val=NT - 1,
                    skip_runtime_bounds_check_because=CLAMPED)
                return tiles

            def add(k, j, tile):
                dve.wait_ge(Z.sum, (k0 + k) * QUAD + j // 2 * 2 + 2)
                if not (isinstance(k, int) and k * QUAD + j == 0):
                    dve.wait_ge(Z.added, (k0 + k) * QUAD + j)
                a = agg[:, bass.ds(tile, 1), :].rearrange("p t c -> p (t c)")
                dve.tensor_tensor(a, sums_of(j), a, ALU.add).then_inc(Z.added, 1)

            def weigh(k, r):
                dve.wait_ge(Z.ex, k0 + k + 1)
                if not (isinstance(k, int) and k < 2):
                    dve.wait_ge(Z.sum, (k0 + k - 1) * QUAD)
                s = r * QUAD % KV_SLOTS
                dve.tensor_tensor(msg[:, r % 2, :, 0:D].rearrange("p j (h c) -> p j h c", h=HEADS),
                                  kv[:, s:s + QUAD, D:2 * D].rearrange("p j (h c) -> p j h c", h=HEADS),
                                  msg[:, r % 2, :, D:MW].unsqueeze(3).to_broadcast([P, QUAD, HEADS, HD]), ALU.mult).then_inc(Z.msg, 1)

            def stage_indices(i, half):
                dve.tensor_copy(idx_stage[:, half % 2, :], at_src[:, bass.ds(i * BODY + half * KV_SLOTS, KV_SLOTS)]).then_inc(Z.idx, 1)

            def stage_first():
                for half in range(2):
                    stage_indices(0, half)

            def body(i, first, last):
                for r in range(QUADS):
                    k = i * QUADS + r
                    a = att[:, r % 2, :, :]
                    s = r * QUAD % KV_SLOTS
                    dve.wait_ge(Z.qe, k0 + k + 1)
                    dve.wait_ge(Z.kv_in[s // QUAD], 16 * QUAD * (k0 // KV_QUADS + i * HALVES + r // KV_QUADS + 1))
                    dve.tensor_tensor(prod[:, r % 2, :, :], bank[:, ATT_BANK[1][r % 2], :].rearrange("p (j d) -> p j d", j=QUAD),
                                      kv[:, s:s + QUAD, 0:D], ALU.mult).then_inc(Z.prod, 1)
                    if (r + 1) % KV_QUADS == 0 and not (last and r // KV_QUADS + 2 >= HALVES):
                        stage_indices(i, r // KV_QUADS + 2)
                    behind = 0 if first and r < GROUP else 2
                    if r % GROUP == 0:
                        tiles = load_tiles((k - behind) * QUAD, (GROUP - 2 + behind) * QUAD)

                    def join(j):
                        if not (first and r < 2):
                            add(k - 2, j, tiles[(r % GROUP - 2 + behind) * QUAD + j])
                    join(0)
                    dve.wait_ge(Z.prod, k0 + k + 1)
                    dve.tensor_reduce(a[:, 0, :], prod[:, r % 2, :, :].rearrange("p j (h c) -> p (j h) c", h=HEADS), AX_X,
                                      ALU.add).then_inc(Z.att, 1)
                    join(1)
                    if not (first and r == 0):
                        weigh(k - 1, (r - 1) % QUADS)
                    dve.wait_ge(Z.att, 3 * (k0 + k) + 1)
                    dve.tensor_tensor(a[:, 1, :], a[:, 0, :], a[:, 0, :], ALU.is_equal).then_inc(Z.att, 1)
                    join(2)
                    dve.tensor_scalar(a[:, 2, :], a[:, 0, :], -CLIP, CLIP, ALU.max, ALU.min).then_inc(Z.att, 1)
                    join(3)
                    dve.wait_ge(Z.att, 3 * (k0 + k) + 3)
                    dve.tensor_tensor(a[:, 2, :], a[:, 2, :], a[:, 1, :], ALU.mult).then_inc(Z.logit, 1)
                    update(i, r)
            if l == 0:
                stage_first()
            run_bodies(dve, body)
            weigh(AT_QUADS - 1, QUADS - 1)
            tiles = load_tiles(AT_STEPS - 2 * QUAD, 2 * QUAD)
            for n, tile in enumerate(tiles):
                add(AT_QUADS - 2 + n // QUAD, n % QUAD, tile)
            if l + 1 < LAYERS:
                stage_first()
            update.rest()

        @block.vector
        def _(dve):
            dve_prepare(dve)
            dve_edge_sums(dve)
            dve.wait_ge(s_w0, 16 * W0_LOADS)
            run_units(dve, dve_dense(dve), dve_between)
            dve.wait_ge(s_nt_in["at"], 16)
            dve.wait_ge(s_order, 2)
            dense_done(dve)
            for l in range(LAYERS):
                dve_attention(dve, l)
                update_done(dve, l)

        @block.sync
        def _(sp):
            sp_prepare(sp)
            sp_table(sp, ES)
            sp_edge_sums(sp)
            sp.wait_ge(es_added, ES_STEPS)
            sp.wait_ge(hist_mm, ES_ROUNDS)
            run_units(sp, sp_dense(sp), sp_between)
            sp.wait_ge(s_nt_in["at"], 16)
            sp.wait_ge(s_order, 2)
            dense_done(sp)
            for l in range(LAYERS):
                sp_attention(sp, l)
                update_done(sp, l)

        @block.scalar
        def _(act):
            act_load_src(act)
            act_edge_sums(act)
            act.wait_ge(s_w0, 16 * W0_LOADS)
            act.wait_ge(es_added, ES_STEPS)
            act.wait_ge(hist_mm, ES_ROUNDS)
            run_units(act, act_dense(act))
            dense_done(act)
            for l in range(LAYERS):
                act_attention(act, l)
                update_done(act, l)

        @block.gpsimd
        def _(pool):
            pool_prepare(pool)
            pool_gather_rows(pool)
            pool_load_weights(pool)
            pool_gather_in_order(pool)
            pool.wait_ge(es_added, ES_STEPS)
            pool.wait_ge(hist_mm, ES_ROUNDS)
            run_units(pool, pool_dense(pool), pool_between)
            dense_done(pool)
            for l in range(LAYERS):
                pool_attention(pool, l)
                if l + 1 < LAYERS:
                    for b in SETS:
                        pool.wait_ge(update_move["out", b], update_moves("out", b, l + 1))

        @block.tensor
        def _(pe):
            pe_prepare(pe)
            pe_edge_sums(pe)
            pe.wait_ge(s_w0, 16 * W0_LOADS)
            run_units(pe, pe_dense(pe), pe_between)
            pe.wait_ge(s_order, 2)
            dense_done(pe)
            for l in range(LAYERS):
                pe_attention(pe, l)
                update_done(pe, l)


_INS = ["x", "src", "dst", "edge_attr_128"] + [f"L0_gnn_{k}" for k in ("W1", "b1", "W2", "b2", "W3", "b3", "ln_w", "ln_b")] + [
    f"L1_gnn_{k}" for k in ("Wq", "bq", "Wk", "bk", "Wv", "bv", "Wo", "bo", "Wpos", "bpos", "Wdeg", "bdeg", "ln1_g", "ln1_b",
                            "ln2_g", "ln2_b", "W1", "b1", "W2", "b2")]


def kernel(**inputs):
    import numpy as _np
    import concourse.bacc as _bacc
    from concourse.bass_utils import run_bass_kernel_spmd as _run

    nc = _bacc.Bacc("TRN2", target_bir_lowering=False, num_devices=1)
    arrays, args = {}, {}
    for name in _INS:
        a = _np.ascontiguousarray(inputs[name])
        arrays[f"in_{name}_dram"] = a
        args[name] = nc.dram_tensor(f"in_{name}_dram", a.shape, mybir.dt.from_np(a.dtype), kind="ExternalInput").ap()
    out = nc.dram_tensor("out_0_dram", (N, D), F32, kind="ExternalOutput").ap()
    gnn_kernel(nc, args, out)
    r = _run(nc, [arrays], core_ids=[0])
    return r.results[0]["out_0_dram"]
```
